# Optimizing a Trainium2 kernel written in Bass

```python
import numpy as np
import jax
import jax.numpy as jnp

def _softmax(x, axis=-1):
    return jax.nn.softmax(x, axis=axis)

def _gelu(x):
    return jax.nn.gelu(x, approximate=True)

def _silu(x):
    return jax.nn.silu(x)

def _sigmoid(x):
    return jax.nn.sigmoid(x)

def _layernorm(x, axis=-1, eps=1e-05):
    m = jnp.mean(x, axis=axis, keepdims=True)
    v = jnp.var(x, axis=axis, keepdims=True)
    return (x - m) / jnp.sqrt(v + eps)

def _scatter_add(tgt, idx, src, axis=0):
    return tgt.at[idx].add(src)

def _segment_sum(src, seg, n):
    return jax.ops.segment_sum(src, seg, n)
kernel_name = 'mk_seq_postln_d1_jaxref_r8_ee95e3'

def setup_inputs(seed: int=0):
    np.random.seed(seed)
    _w = jnp.asarray

    def _L0_attn_setup():
        import jax, jax.numpy as jnp
        import numpy as np
        N_HEAD = 16
        WINDOW = 40
        CHUNK = 50
        MAX_SPAN = 50

        def _layer_norm(x, g, b, eps=1e-05):
            m = x.mean(-1, keepdims=True)
            v = ((x - m) ** 2).mean(-1, keepdims=True)
            return (x - m) / jnp.sqrt(v + eps) * g + b

        def _mha(q, k, v, w_in, b_in, w_out, b_out, n_head):
            D = q.shape[-1]
            dh = D // n_head
            wq, wk, wv = (w_in[:D], w_in[D:2 * D], w_in[2 * D:])
            bq, bk, bv = (b_in[:D], b_in[D:2 * D], b_in[2 * D:])
            qp = (q @ wq.T + bq) * dh ** (-0.5)
            kp = k @ wk.T + bk
            vp = v @ wv.T + bv
            B, Lq, _ = q.shape
            Lk = k.shape[1]
            qh = qp.reshape(B, Lq, n_head, dh)
            kh = kp.reshape(B, Lk, n_head, dh)
            vh = vp.reshape(B, Lk, n_head, dh)
            s = jnp.einsum('bqhd,bkhd->bhqk', qh, kh)
            a = jax.nn.softmax(s, axis=-1)
            o = jnp.einsum('bhqk,bkhd->bqhd', a, vh).reshape(B, Lq, D)
            return o @ w_out.T + b_out
        key = jax.random.key(seed)
        ks = jax.random.split(key, 5)
        B, S, D = (8, 128, 128)
        sc = 0.02
        return {'x': jax.random.normal(ks[0], (B, S, D), jnp.float32), 'ln_l_g': jnp.ones((D,), jnp.float32), 'ln_l_b': jnp.zeros((D,), jnp.float32), 'ln_g_g': jnp.ones((D,), jnp.float32), 'ln_g_b': jnp.zeros((D,), jnp.float32), 'wl_in': jax.random.normal(ks[1], (3 * D, D), jnp.float32) * sc, 'bl_in': jnp.zeros((3 * D,), jnp.float32), 'wl_out': jax.random.normal(ks[2], (D, D), jnp.float32) * sc, 'bl_out': jnp.zeros((D,), jnp.float32), 'wg_in': jax.random.normal(ks[3], (3 * D, D), jnp.float32) * sc, 'bg_in': jnp.zeros((3 * D,), jnp.float32), 'wg_out': jax.random.normal(ks[4], (D, D), jnp.float32) * sc, 'bg_out': jnp.zeros((D,), jnp.float32)}
    _L0_attn_in = _L0_attn_setup()

    def _L0_ffn_setup():
        import jax, jax.numpy as jnp
        import numpy as np

        def _moe_forward(x, Wg, W1, b1, W2, b2):
            B, S, H = x.shape
            E = Wg.shape[1]
            tokens = x.reshape(-1, H)
            T = tokens.shape[0]
            C = -(-T // E)
            logits = tokens @ Wg
            gates = jax.nn.softmax(logits, axis=-1)
            idx = jnp.argmax(gates, axis=1)
            mask1 = jax.nn.one_hot(idx, E, dtype=gates.dtype)
            locations1 = jnp.cumsum(mask1, axis=0) - 1.0
            mask1 = mask1 * (locations1 < C).astype(gates.dtype)
            loc_s = jnp.sum(locations1 * mask1, axis=1).astype(jnp.int32)
            gates1 = jnp.sum(gates * mask1, axis=1)
            loc_oh = jax.nn.one_hot(loc_s, C, dtype=gates.dtype)
            dispatch = mask1[:, :, None] * loc_oh[:, None, :]
            combine = gates1[:, None, None] * dispatch
            expert_in = jnp.einsum('tec,th->ech', dispatch, tokens)
            hidden = jax.nn.relu(jnp.einsum('ech,ehf->ecf', expert_in, W1) + b1[:, None, :])
            expert_out = jnp.einsum('ecf,efh->ech', hidden, W2) + b2[:, None, :]
            out = jnp.einsum('tec,ech->th', combine, expert_out)
            return out.reshape(B, S, H)
        key = jax.random.key(seed)
        ks = jax.random.split(key, 6)
        B, S, H, F, E = (4, 256, 128, 512, 8)
        x = jax.random.normal(ks[0], (B, S, H), dtype=jnp.float32)
        Wg = jax.random.normal(ks[1], (H, E), dtype=jnp.float32) * (1.0 / np.sqrt(H))
        W1 = jax.random.normal(ks[2], (E, H, F), dtype=jnp.float32) * (1.0 / np.sqrt(H))
        b1 = jnp.zeros((E, F), dtype=jnp.float32)
        W2 = jax.random.normal(ks[3], (E, F, H), dtype=jnp.float32) * (1.0 / np.sqrt(F))
        b2 = jnp.zeros((E, H), dtype=jnp.float32)
        return {'x': x, 'Wg': Wg, 'W1': W1, 'b1': b1, 'W2': W2, 'b2': b2}
    _L0_ffn_in = _L0_ffn_setup()
    _d = {'L0_attn_x': _L0_attn_in['x'], 'L0_attn_ln_l_g': _L0_attn_in['ln_l_g'], 'L0_attn_ln_l_b': _L0_attn_in['ln_l_b'], 'L0_attn_ln_g_g': _L0_attn_in['ln_g_g'], 'L0_attn_ln_g_b': _L0_attn_in['ln_g_b'], 'L0_attn_wl_in': _L0_attn_in['wl_in'], 'L0_attn_bl_in': _L0_attn_in['bl_in'], 'L0_attn_wl_out': _L0_attn_in['wl_out'], 'L0_attn_bl_out': _L0_attn_in['bl_out'], 'L0_attn_wg_in': _L0_attn_in['wg_in'], 'L0_attn_bg_in': _L0_attn_in['bg_in'], 'L0_attn_wg_out': _L0_attn_in['wg_out'], 'L0_attn_bg_out': _L0_attn_in['bg_out'], 'L0_ffn_Wg': _L0_ffn_in['Wg'], 'L0_ffn_W1': _L0_ffn_in['W1'], 'L0_ffn_b1': _L0_ffn_in['b1'], 'L0_ffn_W2': _L0_ffn_in['W2'], 'L0_ffn_b2': _L0_ffn_in['b2']}
    _x0 = _d['L0_attn_x']
    _d['L0_attn_x'] = jax.random.normal(jax.random.fold_in(jax.random.key(seed), 1), (32, 256, 128), dtype=_x0.dtype)
    del _x0
    return _d

def reference(L0_attn_x, L0_attn_ln_l_g, L0_attn_ln_l_b, L0_attn_ln_g_g, L0_attn_ln_g_b, L0_attn_wl_in, L0_attn_bl_in, L0_attn_wl_out, L0_attn_bl_out, L0_attn_wg_in, L0_attn_bg_in, L0_attn_wg_out, L0_attn_bg_out, L0_ffn_Wg, L0_ffn_W1, L0_ffn_b1, L0_ffn_W2, L0_ffn_b2):

    def _L0_attn_ref(x, ln_l_g, ln_l_b, ln_g_g, ln_g_b, wl_in, bl_in, wl_out, bl_out, wg_in, bg_in, wg_out, bg_out):
        import jax, jax.numpy as jnp
        import numpy as np
        N_HEAD = 16
        WINDOW = 40
        CHUNK = 50
        MAX_SPAN = 50

        def _layer_norm(x, g, b, eps=1e-05):
            m = x.mean(-1, keepdims=True)
            v = ((x - m) ** 2).mean(-1, keepdims=True)
            return (x - m) / jnp.sqrt(v + eps) * g + b

        def _mha(q, k, v, w_in, b_in, w_out, b_out, n_head):
            D = q.shape[-1]
            dh = D // n_head
            wq, wk, wv = (w_in[:D], w_in[D:2 * D], w_in[2 * D:])
            bq, bk, bv = (b_in[:D], b_in[D:2 * D], b_in[2 * D:])
            qp = (q @ wq.T + bq) * dh ** (-0.5)
            kp = k @ wk.T + bk
            vp = v @ wv.T + bv
            B, Lq, _ = q.shape
            Lk = k.shape[1]
            qh = qp.reshape(B, Lq, n_head, dh)
            kh = kp.reshape(B, Lk, n_head, dh)
            vh = vp.reshape(B, Lk, n_head, dh)
            s = jnp.einsum('bqhd,bkhd->bhqk', qh, kh)
            a = jax.nn.softmax(s, axis=-1)
            o = jnp.einsum('bhqk,bkhd->bqhd', a, vh).reshape(B, Lq, D)
            return o @ w_out.T + b_out
        B, S, D = x.shape
        xl = _layer_norm(x, ln_l_g, ln_l_b)
        xg = _layer_norm(x, ln_g_g, ln_g_b)
        span = min(int(MAX_SPAN * 1.0), B)
        local = jnp.zeros_like(xl)
        for i in range(0, B, WINDOW):
            end = min(i + WINDOW, B)
            start = max(0, i - WINDOW)
            q = xl[:span, i:end]
            kv = xl[:span, start:end]
            o = _mha(q, kv, kv, wl_in, bl_in, wl_out, bl_out, N_HEAD)
            local = local.at[:span, i:end].set(o[:, :end - i])
        glb = jnp.zeros_like(xg)
        for i in range(0, B, CHUNK):
            qc = xg[i:i + CHUNK]
            glb = glb.at[i:i + CHUNK].set(_mha(qc, qc, qc, wg_in, bg_in, wg_out, bg_out, N_HEAD))
        return local + glb

    def _L0_ffn_ref(x, Wg, W1, b1, W2, b2):
        import jax, jax.numpy as jnp
        import numpy as np

        def _moe_forward(x, Wg, W1, b1, W2, b2):
            B, S, H = x.shape
            E = Wg.shape[1]
            tokens = x.reshape(-1, H)
            T = tokens.shape[0]
            C = -(-T // E)
            logits = tokens @ Wg
            gates = jax.nn.softmax(logits, axis=-1)
            idx = jnp.argmax(gates, axis=1)
            mask1 = jax.nn.one_hot(idx, E, dtype=gates.dtype)
            locations1 = jnp.cumsum(mask1, axis=0) - 1.0
            mask1 = mask1 * (locations1 < C).astype(gates.dtype)
            loc_s = jnp.sum(locations1 * mask1, axis=1).astype(jnp.int32)
            gates1 = jnp.sum(gates * mask1, axis=1)
            loc_oh = jax.nn.one_hot(loc_s, C, dtype=gates.dtype)
            dispatch = mask1[:, :, None] * loc_oh[:, None, :]
            combine = gates1[:, None, None] * dispatch
            expert_in = jnp.einsum('tec,th->ech', dispatch, tokens)
            hidden = jax.nn.relu(jnp.einsum('ech,ehf->ecf', expert_in, W1) + b1[:, None, :])
            expert_out = jnp.einsum('ecf,efh->ech', hidden, W2) + b2[:, None, :]
            out = jnp.einsum('tec,ech->th', combine, expert_out)
            return out.reshape(B, S, H)
        return _moe_forward(x, Wg, W1, b1, W2, b2)
    x = L0_attn_x
    x = _layernorm(x + _L0_attn_ref(x, L0_attn_ln_l_g, L0_attn_ln_l_b, L0_attn_ln_g_g, L0_attn_ln_g_b, L0_attn_wl_in, L0_attn_bl_in, L0_attn_wl_out, L0_attn_bl_out, L0_attn_wg_in, L0_attn_bg_in, L0_attn_wg_out, L0_attn_bg_out), axis=-1)
    x = _layernorm(x + _L0_ffn_ref(x, L0_ffn_Wg, L0_ffn_W1, L0_ffn_b1, L0_ffn_W2, L0_ffn_b2), axis=-1)
    return x

_drawn_inputs = setup_inputs


def setup_inputs(seed=0):
    import zlib

    import numpy as np

    out = dict(_drawn_inputs(seed))
    spreads = {'L0_attn_ln_l_g': (1.0, 0.6),
     'L0_attn_ln_l_b': (0.0, 0.8),
     'L0_attn_ln_g_g': (1.0, 0.6),
     'L0_attn_ln_g_b': (0.0, 0.371),
     'L0_attn_bl_in': (0.0, 0.506),
     'L0_attn_bl_out': (0.0, 0.1),
     'L0_attn_bg_in': (0.0, 0.1),
     'L0_attn_bg_out': (0.0, 0.1),
     'L0_ffn_b1': (0.0, 0.324),
     'L0_ffn_b2': (0.0, 0.1)}
    factors = {'L0_attn_wl_in': 7.126, 'L0_attn_wl_out': 2.938, 'L0_attn_wg_in': 3.602}
    for name, (base, spread) in spreads.items():
        noise = np.random.default_rng([zlib.crc32(name.encode()), seed]).standard_normal(out[name].shape)
        drawn = base * np.exp(spread * noise) if base else spread * noise
        out[name] = jnp.asarray(drawn.astype(out[name].dtype))
    for name, factor in factors.items():
        out[name] = (out[name] * factor).astype(out[name].dtype)
    return out
```

```python
from contextlib import ExitStack

import concourse.bass as bass
from concourse import mybir

F32 = mybir.dt.float32
BF16 = mybir.dt.bfloat16
U32 = mybir.dt.uint32
ALU = mybir.AluOpType
ACT = mybir.ActivationFunctionType
AX = mybir.AxisListType.X

P = 128
B, S, D = 32, 256, 128
T = B * S
NH, DH = 16, 8
SCALE = DH ** -0.5
LW = 32
EPS = 1e-5
PAIR = 2 * S
NPAIR = T // PAIR
LPAIR = B * LW // PAIR
TERMS = 6
STACK = TERMS * DH
MASKROW = STACK
NBLK = S // LW
MAXROW = 96
KMAX = MAXROW
KEXP = MAXROW + 3
E, F = 8, 512
FT = F // P
CAP = T // E
ROW = D + 2
NOWHERE = float(2 * T)
CH = 512
NCH = T // CH
CT = CH // P


def wait(eng, sem, value):
    if isinstance(value, int) and value <= 0:
        return
    eng.wait_ge(sem, value)


def hold(eng, sem, value):
    if isinstance(value, int) and value <= 0:
        return
    eng.wait_ge(sem, value)
    if not isinstance(value, int):
        eng.nop(nofuse=True)


class Chain:

    def __init__(self, sem, steps):
        self.sem, self.steps, self.base, self.k = sem, steps, 0, 0

    def start(self, n):
        self.base, self.k = n * self.steps, 0

    def link(self, eng, ins):
        ins.then_inc(self.sem, 1)
        self.k += 1
        hold(eng, self.sem, self.base + self.k)

    def end(self):
        assert self.k == self.steps, (self.k, self.steps)


def stepped(eng, steps, body):
    body(0, True, steps == 1)
    if steps > 2:
        with eng.Fori(1, steps - 1) as i:
            body(i, False, False)
    if steps > 1:
        body(steps - 1, False, True)


def rows(ap, start, count):
    return ap[bass.ds(start, count)]


def build(nc, x, wqkv, bqk, bv_row, ln_cols, wo, bo_row, wg, w1, b1, w2, b2,
          eye_in, tri_in, blockq_in, blockk_in, tokid_in, slot_in, prio_in, out):
    ctx = ExitStack()
    with ctx:
        def sb(name, shape, dt=F32):
            return ctx.enter_context(nc.sbuf_tensor(name, shape, dt))

        ident = sb("ident", [P, P])
        ident_bf = sb("ident_bf", [P, P], BF16)
        tri = sb("tri", [P, P])
        ones = sb("ones", [P, P])
        wqkv_sb = sb("wqkv_sb", [P, 2, 3 * D])
        bqk_sb = sb("bqk_sb", [P, 2, 2])
        bv_sb = sb("bv_sb", [P, 2, D])
        ln_sb = sb("ln_sb", [P, 4])
        wo_sb = sb("wo_sb", [P, 2, D])
        bo_sb = sb("bo_sb", [P, 2, D])
        wg_sb = sb("wg_sb", [P, E])
        powm = sb("powm", [P, 8])
        tokid = sb("tokid", [P, 2])
        slot0 = sb("slot0", [P, 2, E])
        prio = sb("prio", [P, 2, E])
        base = sb("base", [P, 2, E])

        q_stack = nc.dram_tensor("q_stack", [NPAIR + LPAIR, P, TERMS, PAIR], BF16, kind="Internal").ap()
        k_stack = nc.dram_tensor("k_stack", [NPAIR + LPAIR, P, TERMS, PAIR], BF16, kind="Internal").ap()
        v_rows = nc.dram_tensor("v_rows", [(NPAIR + LPAIR) * 2, S, D], F32, kind="Internal").ap()
        x_local = nc.dram_tensor("x_local", [B, LW, D], F32, kind="Internal").ap()
        routed = nc.dram_tensor("routed", [T, ROW], F32, kind="Internal").ap()

        c = dict(ident=ident, ident_bf=ident_bf, tri=tri, ones=ones, wqkv=wqkv_sb, bqk=bqk_sb, bv=bv_sb,
                 ln=ln_sb, wo=wo_sb, bo=bo_sb, wg=wg_sb, powm=powm, tokid=tokid, slot0=slot0, prio=prio,
                 base=base)
        front(nc, c, x, q_stack, k_stack, v_rows, routed,
              dict(ident=eye_in, tri=tri_in, wqkv=wqkv, bqk=bqk, bv=bv_row, ln=ln_cols, wo=wo, bo=bo_row,
                   wg=wg, tokid=tokid_in, slot0=slot_in, prio=prio_in))
        with ExitStack() as stacks:
            qs = stacks.enter_context(nc.sbuf_tensor("qs", [P, 2, NH, S], BF16))
            ks = stacks.enter_context(nc.sbuf_tensor("ks", [P, 2, NH, S], BF16))
            vp = stacks.enter_context(nc.sbuf_tensor("vp", [P, 2, 2, NH, 32], F32))
            prepare_stacks(nc, qs, ks, vp, blockq_in, blockk_in)
            attend(nc, c, "local", qs, ks, vp, x, q_stack, k_stack, v_rows, x_local, routed, out)
            clear_mask_rows(nc, qs, ks)
            attend(nc, c, "global", qs, ks, vp, x, q_stack, k_stack, v_rows, x_local, routed, out)
        experts(nc, c, w1, b1, w2, b2, routed, out)


def front(nc, c, x, q_stack, k_stack, v_rows, routed, given):
    x_t = x.rearrange("b (h p) d -> (b h) p d", p=P)
    v_t = v_rows.rearrange("u (h p) d -> (u h) p d", p=P)
    ctx = ExitStack()
    with ctx:
        def sb(name, shape, dt=F32):
            return ctx.enter_context(nc.sbuf_tensor(name, shape, dt))

        def sem(name):
            return ctx.enter_context(nc.semaphore(name))

        xt = sb("xt", [P, 2, 4, D])
        stats = sb("stats", [P, 2, 4, 6])
        mv = sb("mv", [P, 2, 4, 2])
        veps = sb("veps", [P, 2, 4])
        rstd = sb("rstd", [P, 2, 4])
        xh = sb("xh", [P, 2, 4, D])
        xg = sb("xg", [P, 2, PAIR])
        xl = sb("xl", [P, B * LW])
        full = sb("full", [P, 2, 2, PAIR])
        rest = sb("rest", [P, 2, 2, PAIR])
        part = sb("part", [P, 2, 2, 3, PAIR], BF16)
        v_sb = sb("v_sb", [P, 2, 4, D])
        empty = sb("empty", [P, ROW])
        ps_x = ctx.enter_context(nc.psum_tensor("ps_x", [P, 2, PAIR], F32))
        ps_q = ctx.enter_context(nc.psum_tensor("ps_q", [P, 2, PAIR], F32))
        ps_k = ctx.enter_context(nc.psum_tensor("ps_k", [P, 2, PAIR], F32))
        ps_v = ctx.enter_context(nc.psum_tensor("ps_v", [P, 2, PAIR], F32))

        const_loaded = sem("const_loaded")
        empty_made = sem("empty_made")
        routed_cleared = sem("routed_cleared")
        x_loaded = [sem("x_loaded0"), sem("x_loaded1")]
        stats_done = sem("stats_done")
        stats_ready = sem("stats_ready")
        norm_chain = Chain(sem("front_norm_chain"), 2)
        pow_set = sem("pow_set")
        xh_ready = sem("xh_ready")
        xT_ready = sem("xT_ready")
        xg_ready = sem("xg_ready")
        xl_ready = sem("xl_ready")
        qk_projected = sem("qk_projected")
        v_projected = sem("v_projected")
        full_ready = sem("full_ready")
        v_ready = sem("v_ready")
        part1_ready = sem("part1_ready")
        rest_ready = sem("rest_ready")
        part2_ready = sem("part2_ready")
        part3_ready = sem("part3_ready")
        stack_stored = [sem("stack_stored0"), sem("stack_stored1")]
        v_stored = [sem("v_stored0"), sem("v_stored1")]
        block = ctx.enter_context(nc.Block())
        NCONST = len(given)

        def kind(p):
            return 1 if isinstance(p, int) and p >= NPAIR else 0

        def steps(eng, early, late):
            early(0, 0, 0)

            def body(i, first, last):
                for h in range(2):
                    p = 2 * i + h
                    if not (last and h == 1):
                        early(p + 1, i + (h + 1) // 2, (h + 1) % 2)
                    late(p, i, h)
            stepped(eng, NPAIR // 2, body)
            for p in range(NPAIR, NPAIR + LPAIR):
                late(p, p // 2, p % 2)

        @block.sync
        def _(sp):
            for name, src in given.items():
                sp.dma_start(c[name][:], src).then_inc(const_loaded, 16)
            sp.wait_ge(empty_made, 2)
            sp.dma_start(routed.rearrange("(t p) r -> p t r", p=P),
                         empty[:].unsqueeze(1).to_broadcast([P, T // P, ROW])).then_inc(routed_cleared, 16)

            def early(p, i, h):
                wait(sp, xh_ready, p - 1)
                sp.dma_start(xt[:, h], rows(x_t, 4 * p, 4).rearrange("t p d -> p t d")).then_inc(x_loaded[h], 16)

            def late(p, i, h):
                sp.wait_ge(part3_ready, p + 1)
                for s, stack in enumerate((q_stack, k_stack)):
                    dst = rows(stack, p, 1).rearrange("o r t n -> (o r) t n")
                    for t0, n in ((0, 3), (3, 2), (5, 1)):
                        if s == 0:
                            k = {0: 0, 3: 1, 5: 2}[t0]
                            src = part[:, h, 0, k:k + 1, :].to_broadcast([P, n, PAIR])
                        else:
                            src = part[:, h, 1, 0:n, :]
                        sp.dma_start(dst[:, t0:t0 + n, :], src).then_inc(stack_stored[h], 16)
                sp.wait_ge(v_ready, p + 1)
                sp.dma_start(rows(v_t, 4 * p, 4).rearrange("t p d -> p t d"), v_sb[:, h]).then_inc(v_stored[h], 16)
            steps(sp, early, late)
            total = NPAIR + LPAIR
            for h in range(2):
                sp.wait_ge(stack_stored[h], 16 * 6 * (total // 2))
                sp.wait_ge(v_stored[h], 16 * (total // 2))
            sp.wait_ge(routed_cleared, 16)

        @block.vector
        def _(dve):
            nc.vector.memset(c["powm"][:], -0.5).then_inc(pow_set, 1)
            nc.vector.memset(c["ones"][:], 1.0)
            nc.vector.memset(c["base"][:], 0.0)
            nc.vector.memset(empty[:, 0:D + 1], 0.0).then_inc(empty_made, 1)
            nc.vector.memset(empty[:, D + 1:ROW], NOWHERE).then_inc(empty_made, 1)
            dve.wait_ge(const_loaded, 16 * NCONST)
            nc.vector.tensor_copy(c["ident_bf"][:], c["ident"][:])

            def early(p, i, h):
                dve.wait_ge(x_loaded[h], 16 * (i + 1))
                for t in range(4):
                    last = nc.vector.bn_stats(stats[:, h, t], xt[:, h, t])
                last.then_inc(stats_done, 1)
                hold(dve, stats_done, p + 1)
                for t in range(4):
                    last = nc.vector.bn_aggr(mv[:, h, t], stats[:, h, t])
                last.then_inc(stats_ready, 1)

            def late(p, i, h):
                k = kind(p)
                if k == 0:
                    dve.wait_ge(xg_ready, p + 1)
                    src = ps_x[:, h].rearrange("f (b s) -> f b s", b=2)[:, :, 0:LW]
                    dst = xl[:, bass.ds(2 * LW * p, 2 * LW)].rearrange("f (b s) -> f b s", b=2)
                    nc.vector.tensor_scalar(dst, src, c["ln"][:, 2:3], c["ln"][:, 3:4], ALU.mult,
                                            ALU.add).then_inc(xl_ready, 1)
                dve.wait_ge(qk_projected, p + 1)
                nc.vector.tensor_scalar(full[:, h, 0], ps_q[:, h], c["bqk"][:, k, 0:1], SCALE, ALU.add, ALU.mult)
                nc.vector.tensor_scalar(full[:, h, 1], ps_k[:, h], c["bqk"][:, k, 1:2], None,
                                        ALU.add).then_inc(full_ready, 1)
                dve.wait_ge(v_projected, p + 1)
                wait(dve, v_stored[h], 16 * i)
                nc.vector.tensor_tensor(v_sb[:, h], ps_v[:, h].rearrange("p (t d) -> p t d", t=4),
                                        c["bv"][:, k].unsqueeze(1).to_broadcast([P, 4, D]),
                                        ALU.add).then_inc(v_ready, 1)
                dve.wait_ge(part1_ready, p + 1)
                nc.vector.tensor_tensor(rest[:, h], full[:, h], part[:, h, :, 0], ALU.subtract).then_inc(rest_ready, 1)
            steps(dve, early, late)

        @block.gpsimd
        def _(pool):
            hold(pool, pow_set, 1)

            def early(p, i, h):
                hold(pool, stats_ready, p + 1)
                norm_chain.start(p)
                norm_chain.link(pool, nc.gpsimd.tensor_scalar(veps[:, h], mv[:, h, :, 1], EPS, None, ALU.add))
                norm_chain.link(pool, nc.gpsimd.tensor_tensor(rstd[:, h], veps[:, h], c["powm"][:, 0:4], ALU.pow))
                norm_chain.end()
                hold(pool, xT_ready, p - 1)
                for t in range(4):
                    last = nc.gpsimd.tensor_scalar(xh[:, h, t], xt[:, h, t], mv[:, h, t, 0:1], rstd[:, h, t:t + 1],
                                                   ALU.subtract, ALU.mult)
                last.then_inc(xh_ready, 1)

            def late(p, i, h):
                hold(pool, part2_ready, p + 1)
                nc.gpsimd.tensor_tensor(part[:, h, :, 2], rest[:, h], part[:, h, :, 1],
                                        ALU.subtract).then_inc(part3_ready, 1)
            steps(pool, early, late)

        @block.scalar
        def _(act):
            act.wait_ge(const_loaded, 16 * NCONST)

            def early(p, i, h):
                pass

            def late(p, i, h):
                if kind(p) == 0:
                    act.wait_ge(xT_ready, p + 1)
                    wait(act, v_projected, p - 1)
                    nc.scalar.activation(xg[:, h], ps_x[:, h], ACT.Identity, scale=c["ln"][:, 0:1],
                                         bias=c["ln"][:, 1:2]).then_inc(xg_ready, 1)
                act.wait_ge(full_ready, p + 1)
                wait(act, stack_stored[h], 16 * 6 * i)
                nc.scalar.copy(part[:, h, :, 0], full[:, h]).then_inc(part1_ready, 1)
                act.wait_ge(rest_ready, p + 1)
                nc.scalar.copy(part[:, h, :, 1], rest[:, h]).then_inc(part2_ready, 1)
            steps(act, early, late)

        @block.tensor
        def _(pe):
            pe.wait_ge(const_loaded, 16 * NCONST)

            def early(p, i, h):
                pe.wait_ge(xh_ready, p + 1)
                wait(pe, xl_ready, p - 1)
                for t in range(4):
                    last = nc.tensor.transpose(ps_x[:, h, t * P:(t + 1) * P], xh[:, h, t], c["ident"][:])
                last.then_inc(xT_ready, 1)

            def late(p, i, h):
                k = kind(p)
                w = c["wqkv"][:, k]
                if k == 0:
                    pe.wait_ge(xg_ready, p + 1)
                    src = xg[:, h]
                else:
                    pe.wait_ge(xl_ready, NPAIR)
                    src = xl[:, (p - NPAIR) * PAIR:(p - NPAIR + 1) * PAIR]
                wait(pe, full_ready, p - 1)
                nc.tensor.matmul(ps_q[:, h], w[:, 0:D], src, start=True, stop=True)
                nc.tensor.matmul(ps_k[:, h], w[:, D:2 * D], src, start=True, stop=True).then_inc(qk_projected, 1)
                wait(pe, v_ready, p - 1)
                for t in range(4):
                    last = nc.tensor.matmul(ps_v[:, h, t * D:(t + 1) * D], src[:, t * P:(t + 1) * P],
                                            w[:, 2 * D:3 * D], start=True, stop=True)
                last.then_inc(v_projected, 1)
            steps(pe, early, late)


def prepare_stacks(nc, qs, ks, vp, blockq_in, blockk_in):
    with ExitStack() as ctx:
        bq32 = ctx.enter_context(nc.sbuf_tensor("bq32", [NBLK, S], F32))
        bk32 = ctx.enter_context(nc.sbuf_tensor("bk32", [NBLK, S], F32))
        bqb = ctx.enter_context(nc.sbuf_tensor("bqb", [NBLK, S], BF16))
        bkb = ctx.enter_context(nc.sbuf_tensor("bkb", [NBLK, S], BF16))
        loaded = ctx.enter_context(nc.semaphore("mask_loaded"))
        cast = ctx.enter_context(nc.semaphore("mask_cast"))
        cleared = ctx.enter_context(nc.semaphore("stacks_cleared"))
        v_cleared = ctx.enter_context(nc.semaphore("v_cleared"))
        placed = ctx.enter_context(nc.semaphore("mask_placed"))
        block = ctx.enter_context(nc.Block())

        @block.sync
        def _(sp):
            sp.dma_start(bq32[:], blockq_in).then_inc(loaded, 16)
            sp.dma_start(bk32[:], blockk_in).then_inc(loaded, 16)
            sp.wait_ge(cleared, 3)
            sp.wait_ge(cast, 2)
            for h in range(2):
                for dst, src in ((qs, bqb), (ks, bkb)):
                    sp.dma_start(dst[MASKROW:MASKROW + NBLK, h],
                                 src[:].unsqueeze(1).to_broadcast([NBLK, NH, S])).then_inc(placed, 16)
            sp.wait_ge(placed, 64)

        @block.vector
        def _(dve):
            nc.vector.memset(qs[:], 0.0).then_inc(cleared, 1)
            dve.wait_ge(loaded, 32)
            nc.vector.tensor_copy(bqb[:], bq32[:]).then_inc(cast, 1)
            nc.vector.tensor_copy(bkb[:], bk32[:]).then_inc(cast, 1)

        @block.gpsimd
        def _(pool):
            nc.gpsimd.memset(ks[:], 0.0).then_inc(cleared, 1)
            nc.gpsimd.memset(vp[:], 0.0).then_inc(v_cleared, 1)
            hold(pool, cleared, 1)
            hold(pool, v_cleared, 1)
            for g in range(2):
                dst = vp[:].rearrange("p c k (u g j) w -> p (c k u) g j w", g=2, j=4)
                nc.gpsimd.memset(dst[:, :, g, :, 16 * g + DH:16 * g + DH + 1], 1.0).then_inc(v_cleared, 1)
            hold(pool, cleared, 2)
            pool.wait_ge(v_cleared, 3)
            nc.gpsimd.memset(ks[MAXROW:KEXP], -1.0).then_inc(cleared, 1)


def clear_mask_rows(nc, qs, ks):
    with nc.Block() as block:
        @block.vector
        def _(dve):
            nc.vector.memset(qs[32:64], 0.0)

        @block.gpsimd
        def _(pool):
            nc.gpsimd.memset(ks[32:64], 0.0)


def attend(nc, c, kind, qs, ks, vp, x, q_stack, k_stack, v_rows, x_local, routed, out):
    local = kind == "local"
    K = 1 if local else 0
    U = B * LW // S if local else B
    UNIT0 = T // S if local else 0
    PAIR0 = NPAIR if local else 0
    x_rows = x
    ctx = ExitStack()
    with ctx:
        def sb(name, shape, dt=F32):
            return ctx.enter_context(nc.sbuf_tensor(f"{kind}_{name}", shape, dt))

        def sem(name):
            return ctx.enter_context(nc.semaphore(f"{kind}_{name}"))

        prob = sb("prob", [P, 4, 2 * 2 * S])
        vc = sb("vc", [P, 2, 2, D])
        mx = sb("mx", [P, 2, 2, NH])
        mrest = sb("mrest", [P, 2, 2, 8])
        mpart = sb("mpart", [P, 2, 2, 3, 8], BF16)
        mT = sb("mT", [24, 2, S], BF16)
        oT = sb("oT", [P, 2 * S])
        rden = sb("rden", [P, 4, 8])
        oN = sb("oN", [P, 2, D])
        oNT = sb("oNT", [P, S])
        xr = sb("xr", [P, 2, 2, D])
        y = sb("y", [P, 2, 2, D])
        ps_b = ctx.enter_context(nc.psum_tensor(f"{kind}_ps_b", [P, 4, 2 * S], F32))
        ps_a = ctx.enter_context(nc.psum_tensor(f"{kind}_ps_a", [P, 2, 2 * S], F32))
        ps_o = ctx.enter_context(nc.psum_tensor(f"{kind}_ps_o", [P, 2 * S], F32))
        ps_m = ctx.enter_context(nc.psum_tensor(f"{kind}_ps_m", [P, 2 * S], F32))
        ps_m_bf = ps_m[:].bitcast(BF16)
        if not local:
            stats = sb("stats", [P, 2, 6])
            mv = sb("mv", [P, 2, 2])
            veps = sb("veps", [P, 2])
            rstd = sb("rstd", [P, 2])
            row = sb("row", [P, 2, 2, ROW])
            x1T = sb("x1T", [P, S])
            stats2 = sb("stats2", [P, 2, 6])
            mv2 = sb("mv2", [P, 2, 2])
            veps2 = sb("veps2", [P, 2])
            rstd2 = sb("rstd2", [P, 2])
            o1 = sb("o1", [P, 2, D])
            lmax = sb("lmax", [P, 2])
            shifted = sb("shifted", [P, 2, E])
            gexp = sb("gexp", [P, 2, E])
            gsum = sb("gsum", [P, 2])
            pri = sb("pri", [P, 2, E])
            pmax = sb("pmax", [P, 2])
            mask = sb("mask", [P, 2, E])
            count = sb("count", [P, 2, 2, E])
            loc = sb("loc", [P, 2, E])
            locslot = sb("locslot", [P, 2, 2, E])
            picked = sb("picked", [P, 2, 2])
            over = sb("over", [P, 2])
            slot = sb("slot", [P, 2], U32)

        stack_loaded = [[sem(f"stack_loaded{h}{f}") for f in range(2)] for h in range(2)]
        v_loaded = [sem("v_loaded0"), sem("v_loaded1")]
        xr_loaded = [sem("xr_loaded0"), sem("xr_loaded1")]
        max_scores = sem("max_scores")
        max_done = sem("max_done")
        max_split = sem("max_split")
        max_transposed = sem("max_transposed")
        mT_ready = sem("mT_ready")
        max_rows = [sem("max_rows0"), sem("max_rows1")]
        v_spread = sem("v_spread")
        scores = sem("scores")
        exp_done = sem("exp_done")
        pv_done = sem("pv_done")
        oT_ready = sem("oT_ready")
        o_turned = sem("o_turned")
        o_normed = sem("o_normed")
        oN_turned = sem("oN_turned")
        oNT_ready = sem("oNT_ready")
        projected = sem("projected")
        xr_ready = sem("xr_ready")
        y_ready = sem("y_ready")
        split_chain = Chain(sem("split_chain"), 6)
        norm_chain = Chain(sem("norm_chain"), 1)
        if local:
            y_stored = [sem("y_stored0"), sem("y_stored1")]
        else:
            stat_chain = Chain(sem("stat_chain"), 2)
            stats_ready = sem("stats_ready")
            ln_chain = Chain(sem("ln_chain"), 2)
            x1_ready = sem("x1_ready")
            row_ready = sem("row_ready")
            stat2_chain = Chain(sem("stat2_chain"), 1)
            stats2_ready = sem("stats2_ready")
            ln2_chain = Chain(sem("ln2_chain"), 2)
            o1_ready = sem("o1_ready")
            o1_stored = sem("o1_stored")
            x1_turned = sem("x1_turned")
            x1T_ready = sem("x1T_ready")
            logits_ready = sem("logits_ready")
            logits_read = sem("logits_read")
            gexp_ready = sem("gexp_ready")
            mask_ready = sem("mask_ready")
            gate_ready = sem("gate_ready")
            counted = sem("counted")
            counts_copied = sem("counts_copied")
            mask_chain = Chain(sem("mask_chain"), 3)
            gate_chain = Chain(sem("gate_chain"), 1)
            slot_chain = Chain(sem("slot_chain"), 4)
            picks_ready = sem("picks_ready")
            pick_chain = Chain(sem("pick_chain"), 2)
            slot_ready = sem("slot_ready")
            scattered = [sem("scattered0"), sem("scattered1")]
            tok_chain = Chain(sem("tok_chain"), 1)
        block = ctx.enter_context(nc.Block())

        def nxt(i, h):
            return i + (h + 1) // 2, (h + 1) % 2

        def units(eng, before, unit, after):
            before()

            def body(i, first, last):
                for h in range(2):
                    unit(2 * i + h, i, h, not (last and h == 1), not (first and h == 0), not first)
            stepped(eng, U // 2, body)
            after()

        @block.sync
        def _(sp):
            def load_stack(m, im, hm, half):
                wait(sp, scores, 8 * (m - 2) + 4 * half + 4)
                for dst, stack in ((qs, q_stack), (ks, k_stack)):
                    src = rows(stack, PAIR0 + im, 1)[0, 64 * half:64 * half + 64, :,
                                                        hm * S:(hm + 1) * S].rearrange("(g d) t n -> (d t) g n", d=DH)
                    sp.dma_start(dst[0:STACK, hm, 8 * half:8 * half + 8, :], src).then_inc(stack_loaded[hm][half], 16)

            def load_v(m, hm):
                wait(sp, v_spread, m - 1)
                sp.dma_start(vc[:, hm], rows(v_rows, UNIT0 + m, 1).rearrange("o (k p) d -> p (o k) d", p=P)).then_inc(v_loaded[hm], 16)

            def load_xr(m, hm):
                wait(sp, y_ready, m - 1)
                if local:
                    for t in range(2):
                        sp.dma_start(xr[:, hm, t], rows(x, 8 * m + 4 * t, 4)[:, 0:LW, :]).then_inc(xr_loaded[hm], 16)
                else:
                    sp.dma_start(xr[0:LW, hm, 0], rows(x_local, m, 1).rearrange("o s d -> (o s) d")).then_inc(xr_loaded[hm], 16)
                    sp.dma_start(xr[LW:P, hm, 0], rows(x, m, 1)[0, LW:P, :]).then_inc(xr_loaded[hm], 16)
                    sp.dma_start(xr[:, hm, 1], rows(x, m, 1)[0, P:S, :]).then_inc(xr_loaded[hm], 16)

            def place_max(m, hm, half):
                sp.wait_ge(mT_ready, 2 * m + half + 1)
                sp.dma_start(qs[MAXROW:KEXP, hm, 8 * half:8 * half + 8, :], mT[:, half, :]).then_inc(max_rows[half], 16)

            def store_y(m, hm):
                sp.wait_ge(y_ready, m + 1)
                for t in range(2):
                    sp.dma_start(rows(x_local, 8 * m + 4 * t, 4), y[:, hm, t]).then_inc(y_stored[hm], 16)

            def store_o1(m):
                sp.wait_ge(o1_ready, m + 1)
                sp.dma_start(rows(out, m, 1).rearrange("o (t p) d -> p (o t) d", p=P), o1[:]).then_inc(o1_stored, 16)

            def before():
                load_stack(0, 0, 0, 0)
                load_stack(0, 0, 0, 1)
                load_v(0, 0)
                load_stack(1, 0, 1, 0)
                place_max(0, 0, 0)

            def unit(n, i, h, more, prev, prev2):
                i1, h1 = nxt(i, h)
                if more:
                    load_stack(n + 1, i1, h1, 1)
                    load_v(n + 1, h1)
                load_xr(n, h)
                place_max(n, h, 1)
                if more and not (isinstance(i, int) and n + 2 >= U):
                    load_stack(n + 2, i + 1, h, 0)
                if more:
                    place_max(n + 1, h1, 0)
                if prev and local:
                    store_y(n - 1, 1 - h)
                if prev2 and not local:
                    store_o1(n - 2)

            def after():
                if local:
                    store_y(U - 1, 1)
                    for h in range(2):
                        sp.wait_ge(y_stored[h], 32 * (U // 2))
                else:
                    store_o1(U - 2)
                    store_o1(U - 1)
                    sp.wait_ge(o1_stored, 16 * U)
            units(sp, before, unit, after)

        @block.tensor
        def _(pe):
            def max_pass(m, im, hm, hp):
                if hp % 4 == 0:
                    pe.wait_ge(stack_loaded[hm][hp // 4], 32 * (im + 1))
                for qt in range(2):
                    wait(pe, max_done, 16 * m + 2 * hp + qt - 1)
                    for e in range(2):
                        last = nc.tensor.matmul(ps_a[:, qt, e * S:(e + 1) * S],
                                                qs[0:KMAX, hm, 2 * hp + e, qt * P:(qt + 1) * P],
                                                ks[0:KMAX, hm, 2 * hp + e, :], start=True, stop=True)
                    last.then_inc(max_scores, 1)

            def exp_pass(n, h, hp):
                if hp % 4 == 0:
                    pe.wait_ge(max_rows[hp // 4], 16 * (n + 1))
                wait(pe, exp_done, 8 * n + hp - 1)
                for e in range(2):
                    for kt in range(2):
                        last = nc.tensor.matmul(ps_b[:, 2 * (hp % 2) + e, kt * S:(kt + 1) * S],
                                                ks[0:KEXP, h, 2 * hp + e, kt * P:(kt + 1) * P],
                                                qs[0:KEXP, h, 2 * hp + e, :], start=True, stop=True)
                last.then_inc(scores, 1)

            def p_v(n, h, q):
                if q == 0:
                    wait(pe, oT_ready, n)
                    pe.wait_ge(v_spread, n + 1)
                pe.wait_ge(exp_done, 8 * n + 2 * q + 2)
                for kt in range(2):
                    for j in range(4):
                        at = (j % 2) * 2 * S + kt * S
                        last = nc.tensor.matmul(ps_o[32 * j:32 * j + 32, (q // 2) * S:(q // 2 + 1) * S],
                                                vp[:, h, kt, 4 * q + j, :],
                                                prob[:, (2 * q + j // 2) % 4, at:at + S],
                                                start=(q % 2 == 0 and kt == 0), stop=(q % 2 == 1 and kt == 1))
                last.then_inc(pv_done, 1)

            def turn_max(m, half):
                pe.wait_ge(max_split, 2 * m + half + 1)
                for qt in range(2):
                    last = nc.tensor.transpose(ps_m_bf[0:24, qt * P:(qt + 1) * P],
                                               mpart[:, half, qt].rearrange("p a h -> p (a h)"), c["ident_bf"][:])
                last.then_inc(max_transposed, 1)

            def before():
                for hp in range(8):
                    max_pass(0, 0, 0, hp)
                    if hp == 5:
                        turn_max(0, 0)

            def output_stage(m, hm, hp, n=None):
                if hp == 2:
                    pe.wait_ge(oT_ready, m + 1)
                    for qt in range(2):
                        for u in range(2):
                            last = nc.tensor.transpose(ps_m[:, (2 * qt + u) * P:(2 * qt + u + 1) * P],
                                                       oT[:, u * S + qt * P:u * S + (qt + 1) * P], c["ident"][:])
                    last.then_inc(o_turned, 1)
                if hp == 3:
                    pe.wait_ge(o_normed, m + 1)
                    for qt in range(2):
                        last = nc.tensor.transpose(ps_m[:, qt * P:(qt + 1) * P], oN[:, qt], c["ident"][:])
                    last.then_inc(oN_turned, 1)
                if hp == 4:
                    pe.wait_ge(oNT_ready, m + 1)
                    for qt in range(2):
                        last = nc.tensor.matmul(ps_m[:, qt * D:(qt + 1) * D], oNT[:, qt * P:(qt + 1) * P],
                                                c["wo"][:, K], start=True, stop=True)
                    last.then_inc(projected, 1)
                if local:
                    return
                if hp == 6:
                    pe.wait_ge(x1_ready, m + 1)
                    for qt in range(2):
                        last = nc.tensor.transpose(ps_m[:, qt * P:(qt + 1) * P], row[:, hm, qt, 0:D], c["ident"][:])
                    last.then_inc(x1_turned, 1)
                if hp == 7:
                    pe.wait_ge(x1T_ready, m + 1)
                    for qt in range(2):
                        last = nc.tensor.matmul(ps_m[:, qt * E:(qt + 1) * E], x1T[:, qt * P:(qt + 1) * P],
                                                c["wg"][:], start=True, stop=True)
                    last.then_inc(logits_ready, 1)

            def count_stage(m):
                pe.wait_ge(mask_ready, m + 1)
                nc.tensor.matmul(ps_m[:, 0:2 * E], c["tri"][:], mask[:].rearrange("p t e -> p (t e)"), start=True, stop=True)
                nc.tensor.matmul(ps_m[:, 2 * E:4 * E], c["ones"][:], mask[:].rearrange("p t e -> p (t e)"),
                                 start=True, stop=True).then_inc(counted, 1)

            def unit(n, i, h, more, prev, prev2):
                i1, h1 = nxt(i, h)
                for hp in range(8):
                    exp_pass(n, h, hp)
                    if hp == 1 and prev:
                        p_v(n - 1, 1 - h, 3)
                    if hp in (3, 5, 7):
                        p_v(n, h, (hp - 3) // 2)
                    if more:
                        max_pass(n + 1, i1, h1, hp)
                    if hp == 0:
                        if not local and prev2:
                            pe.wait_ge(logits_read, n - 1)
                        pe.wait_ge(mT_ready, 2 * n + 1)
                        turn_max(n, 1)
                    if hp == 1 and prev2 and not local:
                        pe.wait_ge(mT_ready, 2 * n + 2)
                        count_stage(n - 2)
                    if hp == 2 and prev:
                        pe.wait_ge(mT_ready, 2 * n + 2)
                        if not local and prev2:
                            pe.wait_ge(counts_copied, n - 1)
                    if hp == 5 and more:
                        if prev:
                            pe.wait_ge(y_ready, n)
                        turn_max(n + 1, 0)
                    if hp == 6 and prev and not local and more:
                        pe.wait_ge(mT_ready, 2 * n + 3)
                    if hp == 6 and prev and not local and not more:
                        pe.wait_ge(y_ready, n)
                    if prev:
                        output_stage(n - 1, 1 - h, hp)

            def after():
                if not local:
                    pe.wait_ge(logits_read, U - 1)
                    count_stage(U - 2)
                p_v(U - 1, 1, 3)
                if not local:
                    pe.wait_ge(counts_copied, U - 1)
                else:
                    pe.wait_ge(y_ready, U - 1)
                for hp in range(8):
                    if hp == 6:
                        pe.wait_ge(y_ready, U)
                    output_stage(U - 1, 1, hp)
                if not local:
                    pe.wait_ge(logits_read, U)
                    count_stage(U - 1)
            units(pe, before, unit, after)

        @block.scalar
        def _(act):
            def exponential(n, hp):
                act.wait_ge(scores, 8 * n + hp + 1)
                wait(act, pv_done, 4 * n + hp // 2 - 1)
                nc.scalar.activation(prob[:, hp % 4, :], ps_b[:, 2 * (hp % 2):2 * (hp % 2) + 2, :].rearrange("p a n -> p (a n)"),
                                     ACT.Exp).then_inc(exp_done, 1)

            def copy_max(m, half):
                act.wait_ge(max_transposed, 2 * m + half + 1)
                wait(act, max_rows[half], 16 * m)
                nc.scalar.copy(mT[:, half, :], ps_m_bf[0:24, 0:S]).then_inc(mT_ready, 1)

            def copy_o(m):
                act.wait_ge(pv_done, 4 * m + 4)
                wait(act, o_turned, m)
                nc.scalar.copy(oT[:], ps_o[:]).then_inc(oT_ready, 1)

            def copy_oNT(m):
                act.wait_ge(oN_turned, m + 1)
                wait(act, projected, m)
                nc.scalar.copy(oNT[:], ps_m[:, 0:S]).then_inc(oNT_ready, 1)

            def copy_x1T(m):
                act.wait_ge(x1_turned, m + 1)
                wait(act, logits_ready, m)
                nc.scalar.copy(x1T[:], ps_m[:, 0:S]).then_inc(x1T_ready, 1)

            def gate_exp(m):
                act.wait_ge(logits_read, m + 1)
                wait(act, gate_ready, m)
                nc.scalar.activation(gexp[:], shifted[:], ACT.Exp).then_inc(gexp_ready, 1)

            def copy_counts(m):
                act.wait_ge(counted, m + 1)
                wait(act, picks_ready, m)
                nc.scalar.copy(count[:].rearrange("p a t e -> p (a t e)"), ps_m[:, 0:4 * E]).then_inc(counts_copied, 1)

            def before():
                copy_max(0, 0)

            def unit(n, i, h, more, prev, prev2):
                for hp in range(8):
                    exponential(n, hp)
                    if hp == 0:
                        if prev2 and not local:
                            gate_exp(n - 2)
                        copy_max(n, 1)
                    if hp == 1 and prev:
                        copy_o(n - 1)
                        if prev2 and not local:
                            copy_counts(n - 2)
                    if hp == 3 and prev:
                        copy_oNT(n - 1)
                    if hp == 5 and more:
                        copy_max(n + 1, 0)
                    if hp == 6 and prev and not local:
                        copy_x1T(n - 1)

            def after():
                if not local:
                    gate_exp(U - 2)
                    copy_counts(U - 2)
                copy_o(U - 1)
                copy_oNT(U - 1)
                if not local:
                    copy_x1T(U - 1)
                    gate_exp(U - 1)
                    copy_counts(U - 1)
            units(act, before, unit, after)

        @block.vector
        def _(dve):
            def take_max(m, hm, hp):
                for qt in range(2):
                    dve.wait_ge(max_scores, 16 * m + 2 * hp + qt + 1)
                    if qt == 0 and hp % 4 == 0:
                        wait(dve, max_split, 2 * m - 3 + hp // 4)
                    nc.vector.reduce_max(mx[:, hm, qt, 2 * hp:2 * hp + 2],
                                         ps_a[:, qt].rearrange("p (e k) -> p e k", e=2), axis=AX).then_inc(max_done, 1)

            def norm_o(m):
                dve.wait_ge(o_turned, m + 1)
                v = ps_m[:].rearrange("p (a g w) -> p a g w", a=4, w=16)
                norm_chain.start(m)
                norm_chain.link(dve, nc.vector.reciprocal(rden[:], v[:, :, :, DH]))
                norm_chain.end()
                wait(dve, oN_turned, m)
                nc.vector.tensor_tensor(oN[:].rearrange("p t (g d) -> p (t g) d", d=DH).rearrange("p (a g) d -> p a g d", a=4),
                                        v[:, :, :, 0:DH],
                                        rden[:].unsqueeze(3).to_broadcast([P, 4, 8, DH]), ALU.mult).then_inc(o_normed, 1)

            def add_residual(m, im, hm):
                dve.wait_ge(projected, m + 1)
                dve.wait_ge(xr_ready, m + 1)
                if local:
                    wait(dve, y_stored[hm], 32 * im)
                nc.vector.tensor_tensor(y[:, hm], ps_m[:, 0:2 * D].rearrange("p (t d) -> p t d", t=2), xr[:, hm],
                                        ALU.add).then_inc(y_ready, 1)
                if local:
                    return
                stat_chain.start(m)
                dve.wait_ge(y_ready, m + 1)
                for t in range(2):
                    last = nc.vector.bn_stats(stats[:, t], y[:, hm, t])
                stat_chain.link(dve, last)
                hold(dve, x1_ready, m)
                for t in range(2):
                    last = nc.vector.bn_aggr(mv[:, t], stats[:, t])
                stat_chain.link(dve, last)
                stat_chain.end()
                nc.vector.tensor_copy(veps[:], mv[:, :, 1]).then_inc(stats_ready, 1)

            def second_stats(m, hm):
                dve.wait_ge(x1_ready, m + 1)
                stat2_chain.start(m)
                for t in range(2):
                    last = nc.vector.bn_stats(stats2[:, t], row[:, hm, t, 0:D])
                stat2_chain.link(dve, last)
                stat2_chain.end()
                hold(dve, o1_ready, m)
                for t in range(2):
                    last = nc.vector.bn_aggr(mv2[:, t], stats2[:, t])
                last.then_inc(stats2_ready, 1)

            def route(m, hm):
                dve.wait_ge(logits_ready, m + 1)
                lg = ps_m[:, 0:2 * E].rearrange("p (t e) -> p t e", t=2)
                mask_chain.start(m)
                mask_chain.link(dve, nc.vector.reduce_max(lmax[:], lg, axis=AX))
                wait(dve, gexp_ready, m)
                nc.vector.tensor_tensor(shifted[:], lg, lmax[:].unsqueeze(2).to_broadcast([P, 2, E]),
                                        ALU.subtract).then_inc(logits_read, 1)
                dve.wait_ge(logits_read, m + 1)
                mask_chain.link(dve, nc.vector.scalar_tensor_tensor(out=pri[:], in0=shifted[:], scalar=0.0,
                                                                    in1=c["prio"][:], op0=ALU.is_ge, op1=ALU.mult))
                mask_chain.link(dve, nc.vector.reduce_max(pmax[:], pri[:], axis=AX))
                mask_chain.end()
                wait(dve, picks_ready, m)
                nc.vector.tensor_tensor(mask[:], pri[:], pmax[:].unsqueeze(2).to_broadcast([P, 2, E]),
                                        ALU.is_equal).then_inc(mask_ready, 1)
                dve.wait_ge(gexp_ready, m + 1)
                gate_chain.start(m)
                gate_chain.link(dve, nc.vector.reduce_sum(gsum[:], gexp[:], axis=AX))
                gate_chain.end()
                nc.vector.reciprocal(row[:, hm, :, D], gsum[:]).then_inc(gate_ready, 1)

            def pick(m):
                dve.wait_ge(picks_ready, m + 1)
                pick_chain.start(m)
                pick_chain.link(dve, nc.vector.reduce_sum(picked[:], locslot[:], axis=AX))
                pick_chain.link(dve, nc.vector.tensor_scalar(over[:], picked[:, 0], CAP + 0.5, NOWHERE, ALU.is_gt, ALU.mult))
                pick_chain.end()
                wait_scatter(dve, m)
                nc.vector.tensor_tensor(slot[:], picked[:, 1], over[:], ALU.add).then_inc(slot_ready, 1)

            def wait_scatter(eng, m):
                if isinstance(m, int):
                    if m > 0:
                        eng.wait_ge(scattered[(m - 1) % 2], 32 * ((m - 1) // 2 + 1))
                else:
                    eng.wait_ge(scattered[scatter_parity[0]], scatter_value[0])

            scatter_parity, scatter_value = [0], [0]

            def before():
                for hp in range(8):
                    take_max(0, 0, hp)

            def unit(n, i, h, more, prev, prev2):
                i1, h1 = nxt(i, h)
                scatter_parity[0] = 1 - h
                scatter_value[0] = 32 * i - 32 + 32 * h
                for hp in range(8):
                    if hp == 0 and prev2 and not local:
                        route(n - 2, h)
                    if hp == 2 and prev2 and not local:
                        pick(n - 2)
                    if hp == 3 and prev:
                        norm_o(n - 1)
                    if hp == 5 and prev:
                        add_residual(n - 1, i if h else i - 1, 1 - h)
                    if hp == 7 and prev and not local:
                        second_stats(n - 1, 1 - h)
                    if more:
                        take_max(n + 1, h1, hp)

            def after():
                if not local:
                    route(U - 2, 0)
                    pick(U - 2)
                norm_o(U - 1)
                add_residual(U - 1, U // 2 - 1, 1)
                if not local:
                    second_stats(U - 1, 1)
                    route(U - 1, 1)
                    pick(U - 1)
            units(dve, before, unit, after)

        @block.gpsimd
        def _(pool):
            def split_max(m, hm, half):
                hold(pool, max_done, 16 * m + 8 * half + 8)
                hold(pool, max_transposed, 2 * m + half - 1)
                src = mx[:, hm, :, 8 * half:8 * half + 8]
                r, part = mrest[:, half], mpart[:, half]
                split_chain.base, split_chain.k = 3 * (2 * m + half), 0
                split_chain.link(pool, nc.gpsimd.tensor_copy(part[:, :, 0], src))
                split_chain.link(pool, nc.gpsimd.tensor_tensor(r, src, part[:, :, 0], ALU.subtract))
                split_chain.link(pool, nc.gpsimd.tensor_copy(part[:, :, 1], r))
                nc.gpsimd.tensor_tensor(part[:, :, 2], r, part[:, :, 1], ALU.subtract).then_inc(max_split, 1)

            def spread_v(m, im, hm):
                hold(pool, v_loaded[hm], 16 * (im + 1))
                hold(pool, pv_done, 4 * (m - 1))
                for g in range(2):
                    dst = vp[:, hm].rearrange("p k (u g j) w -> p k u g j w", g=2, j=4)[:, :, :, g, :, 16 * g:16 * g + DH]
                    src = vc[:, hm].rearrange("p k (u g j d) -> p k u g j d", g=2, j=4, d=DH)[:, :, :, g]
                    for kt in range(2):
                        last = nc.gpsimd.tensor_copy(dst[:, kt], src[:, kt])
                last.then_inc(v_spread, 1)

            def bias_residual(m, im, hm):
                hold(pool, xr_loaded[hm], (32 if local else 48) * (im + 1))
                nc.gpsimd.tensor_tensor(xr[:, hm], xr[:, hm], c["bo"][:, K].unsqueeze(1).to_broadcast([P, 2, D]),
                                        ALU.add).then_inc(xr_ready, 1)

            def norm_rows(m, im, hm):
                hold(pool, stats_ready, m + 1)
                ln_chain.start(m)
                ln_chain.link(pool, nc.gpsimd.tensor_scalar(rstd[:], veps[:], EPS, None, ALU.add))
                ln_chain.link(pool, nc.gpsimd.tensor_tensor(rstd[:], rstd[:], c["powm"][:, 0:2], ALU.pow))
                ln_chain.end()
                hold(pool, scattered[hm], 32 * im)
                for t in range(2):
                    last = nc.gpsimd.tensor_scalar(row[:, hm, t, 0:D], y[:, hm, t], mv[:, t, 0:1], rstd[:, t:t + 1],
                                                   ALU.subtract, ALU.mult)
                last.then_inc(x1_ready, 1)
                tok_chain.start(m)
                tok_chain.link(pool, nc.gpsimd.tensor_copy(row[:, hm, :, D + 1], c["tokid"][:]))
                tok_chain.end()
                nc.gpsimd.tensor_scalar(c["tokid"][:], c["tokid"][:], float(S), None, ALU.add).then_inc(row_ready, 1)
                hold(pool, row_ready, m + 1)

            def norm_again(m, hm):
                hold(pool, stats2_ready, m + 1)
                ln2_chain.start(m)
                ln2_chain.link(pool, nc.gpsimd.tensor_scalar(veps2[:], mv2[:, :, 1], EPS, None, ALU.add))
                ln2_chain.link(pool, nc.gpsimd.tensor_tensor(rstd2[:], veps2[:], c["powm"][:, 0:2], ALU.pow))
                ln2_chain.end()
                hold(pool, o1_stored, 16 * m)
                for t in range(2):
                    last = nc.gpsimd.tensor_scalar(o1[:, t], row[:, hm, t, 0:D], mv2[:, t, 0:1], rstd2[:, t:t + 1],
                                                   ALU.subtract, ALU.mult)
                last.then_inc(o1_ready, 1)

            def queue_places(m):
                hold(pool, counts_copied, m + 1)
                hold(pool, mask_ready, m + 1)
                b = c["base"]
                slot_chain.start(m)
                slot_chain.link(pool, nc.gpsimd.tensor_tensor(b[:, 1], b[:, 0], count[:, 1, 0], ALU.add))
                slot_chain.link(pool, nc.gpsimd.tensor_tensor(loc[:], count[:, 0], b[:], ALU.add))
                nc.gpsimd.tensor_tensor(b[:, 0], b[:, 1], count[:, 1, 1], ALU.add)
                nc.gpsimd.tensor_tensor(locslot[:, 0], loc[:], mask[:], ALU.mult)
                slot_chain.link(pool, nc.gpsimd.tensor_tensor(loc[:], loc[:], c["slot0"][:], ALU.add))
                slot_chain.link(pool, nc.gpsimd.tensor_tensor(locslot[:, 1], loc[:], mask[:], ALU.mult))
                slot_chain.end()
                last = nc.gpsimd.tensor_copy(over_dummy[:], b[:, 0, 0:1])
                last.then_inc(picks_ready, 1)

            def scatter(m, hm):
                hold(pool, slot_ready, m + 1)
                hold(pool, gate_ready, m + 1)
                for t in range(2):
                    pool.indirect_dma_start(out=routed, out_offset=bass.IndirectOffsetOnAxis(ap=slot[:, t:t + 1], axis=0),
                                            in_=row[:, hm, t, :], in_offset=None, bounds_check=T - 1,
                                            oob_is_err=False).then_inc(scattered[hm], 16)

            over_dummy = mrest[:, 0, 0, 0:1]

            def before():
                split_max(0, 0, 0)
                spread_v(0, 0, 0)

            def unit(n, i, h, more, prev, prev2):
                i1, h1 = nxt(i, h)
                split_max(n, h, 1)
                if prev2 and not local:
                    queue_places(n - 2)
                if more:
                    spread_v(n + 1, i1, h1)
                bias_residual(n, i, h)
                if prev2 and not local:
                    scatter(n - 2, h)
                if more:
                    split_max(n + 1, h1, 0)
                if prev and not local:
                    norm_rows(n - 1, i if h else i - 1, 1 - h)
                    norm_again(n - 1, 1 - h)

            def after():
                if not local:
                    queue_places(U - 2)
                    scatter(U - 2, 0)
                    norm_rows(U - 1, U // 2 - 1, 1)
                    norm_again(U - 1, 1)
                    queue_places(U - 1)
                    scatter(U - 1, 1)
                    for h in range(2):
                        hold(pool, scattered[h], 32 * (U // 2))
            units(pool, before, unit, after)


def experts(nc, c, w1, b1, w2, b2, routed, out):
    routed_t = routed.rearrange("(n p) r -> n p r", p=P)
    out_rows = out.rearrange("b s d -> (b s) d")
    ctx = ExitStack()
    with ctx:
        def sb(name, shape, dt=F32):
            return ctx.enter_context(nc.sbuf_tensor(name, shape, dt))

        def sem(name):
            return ctx.enter_context(nc.semaphore(name))

        w1_sb = sb("w1_sb", [P, 2, F])
        w2_sb = sb("w2_sb", [P, 2, FT, D])
        b1_sb = sb("b1_sb", [P, 2, FT])
        b2_sb = sb("b2_sb", [P, 2, D])
        rows_sb = sb("rows_sb", [P, 4, CT, ROW])
        xT = sb("xT", [P, 2, CH])
        hT = sb("hT", [P, 2, FT, CH])
        t1 = sb("t1", [P, 2, CT, D])
        z = sb("z", [P, 2, CT, D])
        stats = sb("e_stats", [P, CT, 6])
        mv = sb("e_mv", [P, CT, 2])
        veps = sb("e_veps", [P, CT])
        rstd = sb("e_rstd", [P, CT])
        res = sb("res", [P, 2, CT, D])
        dest = sb("dest", [P, 2, CT], U32)
        ps_x = ctx.enter_context(nc.psum_tensor("e_ps_x", [P, CH], F32))
        ps_h = ctx.enter_context(nc.psum_tensor("e_ps_h", [P, FT, CH], F32))
        ps_y = ctx.enter_context(nc.psum_tensor("e_ps_y", [P, 2, CH], F32))

        w_loaded = [sem("w_loaded0"), sem("w_loaded1")]
        rows_loaded = [sem(f"rows_loaded{h}") for h in range(4)]
        rows_turned = sem("rows_turned")
        xT_ready = sem("e_xT_ready")
        hidden = sem("hidden")
        hT_ready = sem("hT_ready")
        y_ready = sem("e_y_ready")
        y_read = sem("e_y_read")
        post_chain = Chain(sem("post_chain"), 2)
        z_stats = sem("z_stats")
        ln_chain = Chain(sem("e_ln_chain"), 2)
        res_ready = sem("res_ready")
        scattered = [sem("e_scattered0"), sem("e_scattered1")]
        block = ctx.enter_context(nc.Block())

        def steps(eng, before, step, after):
            before()

            def body(i, first, last):
                for h in range(4):
                    step(4 * i + h, i, h, last)
            stepped(eng, NCH // 4, body)
            after()

        @block.sync
        def _(sp):
            def load_w(e, ie, he):
                wait(sp, y_read, 2 * e - 2)
                sp.dma_start(w1_sb[:, he], rows(w1, e, 1).rearrange("o k f -> (o k) f")).then_inc(w_loaded[he], 16)
                sp.dma_start(w2_sb[:, he], rows(w2, e, 1).rearrange("o (g p) d -> p (o g) d", p=P)).then_inc(w_loaded[he], 16)
                sp.dma_start(b1_sb[:, he], rows(b1, e, 1).rearrange("o p g -> (o p) g")).then_inc(w_loaded[he], 16)
                sp.dma_start(b2_sb[:, he], rows(b2, e, 1).to_broadcast([P, D])).then_inc(w_loaded[he], 16)

            def load_rows(k, h):
                wait(sp, z_stats, k - 3)
                sp.dma_start(rows_sb[:, h], rows(routed_t, CT * k, CT).rearrange("t p r -> p t r")).then_inc(rows_loaded[h], 16)

            def before():
                load_rows(0, 0)
                load_w(0, 0, 0)
                load_rows(1, 1)
                load_rows(2, 2)

            def step(k, i, h, last):
                if h % 2 == 0 and not (last and h == 2):
                    load_w(2 * i + h // 2 + 1, i + (h // 2 + 1) // 2, (h // 2 + 1) % 2)
                if not (last and h > 0):
                    load_rows(k + 3, (h + 3) % 4)

            def after():
                pass
            steps(sp, before, step, after)

        @block.tensor
        def _(pe):
            def turn(k, ih, h):
                pe.wait_ge(rows_loaded[h], 16 * (ih + 1))
                wait(pe, xT_ready, k)
                for t in range(CT):
                    last = nc.tensor.transpose(ps_x[:, t * P:(t + 1) * P], rows_sb[:, h, t, 0:D], c["ident"][:])
                last.then_inc(rows_turned, 1)

            def up(k, ie, he):
                pe.wait_ge(xT_ready, k + 1)
                pe.wait_ge(w_loaded[he], 64 * (ie + 1))
                for f in range(FT):
                    wait(pe, hT_ready, FT * (k - 1) + f + 1)
                    nc.tensor.matmul(ps_h[:, f], w1_sb[:, he, f * P:(f + 1) * P], xT[:, h_of(k)],
                                     start=True, stop=True).then_inc(hidden, 1)

            def down(k, he, hk):
                pe.wait_ge(hT_ready, FT * (k + 1))
                wait(pe, y_read, k - 1)
                for t in range(CT):
                    for f in range(FT):
                        last = nc.tensor.matmul(ps_y[:, hk, t * D:(t + 1) * D], hT[:, hk, f, t * P:(t + 1) * P],
                                                w2_sb[:, he, f], start=(f == 0), stop=(f == FT - 1))
                last.then_inc(y_ready, 1)

            parity = [0]

            def h_of(k):
                return parity[0]

            def before():
                turn(0, 0, 0)
                turn(1, 0, 1)
                parity[0] = 0
                up(0, 0, 0)

            def step(k, i, h, last):
                if not (last and h == 3):
                    parity[0] = (h + 1) % 2
                    up(k + 1, i + (h + 1) // 4, ((h + 1) // 2) % 2)
                if not (last and h >= 2):
                    turn(k + 2, i + (h + 2) // 4, (h + 2) % 4)
                down(k, (h // 2) % 2, h % 2)

            def after():
                pass
            steps(pe, before, step, after)

        @block.scalar
        def _(act):
            def copy_x(k, hk):
                act.wait_ge(rows_turned, k + 1)
                wait(act, hidden, FT * (k - 1))
                nc.scalar.copy(xT[:, hk], ps_x[:]).then_inc(xT_ready, 1)

            def relu(k, he, hk):
                wait(act, y_ready, k - 1)
                for f in range(FT):
                    act.wait_ge(hidden, FT * k + f + 1)
                    nc.scalar.activation(hT[:, hk, f], ps_h[:, f], ACT.Relu, bias=b1_sb[:, he, f:f + 1]).then_inc(hT_ready, 1)

            def before():
                copy_x(0, 0)
                copy_x(1, 1)
                relu(0, 0, 0)

            def step(k, i, h, last):
                if not (last and h == 3):
                    relu(k + 1, ((h + 1) // 2) % 2, (h + 1) % 2)
                if not (last and h >= 2):
                    copy_x(k + 2, h % 2)

            def after():
                pass
            steps(act, before, step, after)

        @block.vector
        def _(dve):
            def before():
                pass

            def step(k, i, h, last):
                he, hk = (h // 2) % 2, h % 2
                post_chain.start(k)
                dve.wait_ge(y_ready, k + 1)
                nc.vector.tensor_tensor(t1[:, hk], ps_y[:, hk].rearrange("p (t d) -> p t d", t=CT),
                                        b2_sb[:, he].unsqueeze(1).to_broadcast([P, CT, D]), ALU.add).then_inc(y_read, 1)
                dve.wait_ge(y_read, k + 1)
                wait(dve, res_ready, k - 1)
                for t in range(CT):
                    ins = nc.vector.scalar_tensor_tensor(out=z[:, hk, t], in0=t1[:, hk, t],
                                                         scalar=rows_sb[:, h, t, D:D + 1],
                                                         in1=rows_sb[:, h, t, 0:D], op0=ALU.mult, op1=ALU.add)
                post_chain.link(dve, ins)
                for t in range(CT):
                    ins = nc.vector.bn_stats(stats[:, t], z[:, hk, t])
                post_chain.link(dve, ins)
                post_chain.end()
                wait(dve, scattered[hk], 16 * CT * (2 * i + h // 2))
                nc.vector.tensor_copy(dest[:, hk], rows_sb[:, h, :, D + 1])
                hold(dve, res_ready, k)
                for t in range(CT):
                    ins = nc.vector.bn_aggr(mv[:, t], stats[:, t])
                ins.then_inc(z_stats, 1)

            def after():
                pass
            steps(dve, before, step, after)

        @block.gpsimd
        def _(pool):
            def before():
                pass

            def step(k, i, h, last):
                hk = h % 2
                hold(pool, z_stats, k + 1)
                ln_chain.start(k)
                ln_chain.link(pool, nc.gpsimd.tensor_scalar(veps[:], mv[:, :, 1], EPS, None, ALU.add))
                ln_chain.link(pool, nc.gpsimd.tensor_tensor(rstd[:], veps[:], c["powm"][:, 0:CT], ALU.pow))
                ln_chain.end()
                hold(pool, scattered[hk], 16 * CT * (2 * i + h // 2))
                for t in range(CT):
                    ins = nc.gpsimd.tensor_scalar(res[:, hk, t], z[:, hk, t], mv[:, t, 0:1], rstd[:, t:t + 1],
                                                  ALU.subtract, ALU.mult)
                ins.then_inc(res_ready, 1)
                hold(pool, res_ready, k + 1)
                for t in range(CT):
                    pool.indirect_dma_start(out=out_rows, out_offset=bass.IndirectOffsetOnAxis(ap=dest[:, hk, t:t + 1], axis=0),
                                            in_=res[:, hk, t], in_offset=None, bounds_check=T - 1,
                                            oob_is_err=False).then_inc(scattered[hk], 16)

            def after():
                for h in range(2):
                    hold(pool, scattered[h], 16 * CT * NCH // 2)
            steps(pool, before, step, after)


def kernel(**inputs):
    import numpy as np
    import concourse.bacc as bacc
    from concourse.bass_utils import run_bass_kernel_spmd

    a = {k.removeprefix("L0_attn_").removeprefix("L0_ffn_"): np.asarray(v) for k, v in inputs.items()}
    f32 = np.float32

    def both(g, l, axis=1):
        return np.ascontiguousarray(np.stack([g, l], axis=axis))

    def head_order(w):
        return w.reshape(2, 2, 4, DH, D).transpose(0, 2, 1, 3, 4).reshape(D, D)

    def spread(v):
        return np.ascontiguousarray(np.broadcast_to(v, (P,) + v.shape))

    blk = np.arange(S) // LW
    same = blk[None, :] == np.arange(NBLK)[:, None]
    arrays = {
        "x": a["x"],
        "wqkv": both(a["wg_in"].T, a["wl_in"].T),
        "bqk": both(a["bg_in"][:2 * D].reshape(2, D).T, a["bl_in"][:2 * D].reshape(2, D).T),
        "bv_row": spread(np.stack([a["bg_in"][2 * D:], a["bl_in"][2 * D:]])),
        "ln_cols": np.stack([a["ln_g_g"], a["ln_g_b"], a["ln_l_g"], a["ln_l_b"]], axis=1),
        "wo": both(head_order(a["wg_out"].T), head_order(a["wl_out"].T)),
        "bo_row": spread(np.stack([a["bg_out"], a["bl_out"]])),
        "wg": a["Wg"],
        "w1": a["W1"],
        "b1": a["b1"].reshape(E, FT, P).transpose(0, 2, 1),
        "w2": a["W2"],
        "b2": a["b2"],
        "eye_in": np.eye(P, dtype=f32),
        "tri_in": np.triu(np.ones((P, P), f32)),
        "blockq_in": same.astype(f32),
        "blockk_in": np.where(same, f32(0), f32(-2.0 ** 100)),
        "tokid_in": (np.arange(P)[:, None] + P * np.arange(2)[None, :]).astype(f32),
        "slot_in": spread(np.broadcast_to(CAP * np.arange(E) - 1, (2, E)).astype(f32)),
        "prio_in": spread(np.broadcast_to(E - np.arange(E), (2, E)).astype(f32)),
    }
    arrays = {k: np.ascontiguousarray(v) for k, v in arrays.items()}
    nc = bacc.Bacc("TRN2", target_bir_lowering=False, num_devices=1)
    aps = {k: nc.dram_tensor(k, v.shape, mybir.dt.from_np(v.dtype), kind="ExternalInput").ap() for k, v in arrays.items()}
    out = nc.dram_tensor("out", (B, S, D), F32, kind="ExternalOutput").ap()
    build(nc, out=out, **aps)
    result = run_bass_kernel_spmd(nc, [arrays], core_ids=[0])
    return result.results[0]["out"]
```

```python
from contextlib import ExitStack

import concourse.bass as bass
from concourse import mybir

F32 = mybir.dt.float32
BF16 = mybir.dt.bfloat16
U32 = mybir.dt.uint32
ALU = mybir.AluOpType
ACT = mybir.ActivationFunctionType
AX = mybir.AxisListType.X

P = 128
B, S, D = 32, 256, 128
T = B * S
NH, DH = 16, 8
SCALE = DH ** -0.5
LW = 32
EPS = 1e-5
PAIR = 2 * S
NPAIR = T // PAIR
LPAIR = B * LW // PAIR
TERMS = 6
STACK = TERMS * DH
MASKROW = STACK
NBLK = S // LW
MAXROW = 96
KMAX = MAXROW
KEXP = MAXROW + 3
E, F = 8, 512
FT = F // P
CAP = T // E
ROW = D + 2
NOWHERE = float(2 * T)
CH = 512
NCH = T // CH
CT = CH // P


def wait(eng, sem, value):
    if isinstance(value, int) and value <= 0:
        return
    eng.wait_ge(sem, value)


def hold(eng, sem, value):
    if isinstance(value, int) and value <= 0:
        return
    eng.wait_ge(sem, value)
    if not isinstance(value, int):
        eng.nop(nofuse=True)


class Chain:

    def __init__(self, sem, steps):
        self.sem, self.steps, self.base, self.k = sem, steps, 0, 0

    def start(self, n):
        self.base, self.k = n * self.steps, 0

    def link(self, eng, ins):
        ins.then_inc(self.sem, 1)
        self.k += 1
        hold(eng, self.sem, self.base + self.k)

    def end(self):
        assert self.k == self.steps, (self.k, self.steps)


def stepped(eng, steps, body):
    body(0, True, steps == 1)
    if steps > 2:
        with eng.Fori(1, steps - 1) as i:
            body(i, False, False)
    if steps > 1:
        body(steps - 1, False, True)


class Step:

    def __init__(self, i, j, unroll):
        self.i, self.j, self.unroll = i, j, unroll
        self.n = unroll * i + j

    def mod(self, k):
        return self.j % k

    def plus(self, k):
        return Step(self.i, self.j + k, self.unroll)

    def div(self, k):
        return (self.unroll // k) * self.i + self.j // k if not isinstance(self.i, int) else self.n // k


def pipelined(eng, stages, unroll, loop_from, loop_to, ahead):
    def step(i, j):
        for offset, count, stage in stages:
            u = Step(i, j + offset, unroll)
            if not isinstance(i, int) or 0 <= u.n < count:
                stage(u)
    for s in range(-ahead, loop_from):
        step(0, s)
    with eng.Fori(loop_from // unroll, loop_to // unroll) as i:
        for j in range(unroll):
            step(i, j)
    for s in range(loop_to, max(count - offset for offset, count, _ in stages)):
        step(0, s)


def rows(ap, start, count):
    return ap[bass.ds(start, count)]


def build(nc, x, wqkv, bqk, bv_row, ln_cols, wo, bo_row, wg, w1, b1, w2, b2,
          eye_in, tri_in, blockq_in, blockk_in, tokid_in, slot_in, prio_in, out):
    ctx = ExitStack()
    with ctx:
        def sb(name, shape, dt=F32):
            return ctx.enter_context(nc.sbuf_tensor(name, shape, dt))

        ident = sb("ident", [P, P])
        ident_bf = sb("ident_bf", [P, P], BF16)
        tri = sb("tri", [P, P])
        ones = sb("ones", [P, P])
        wqkv_sb = sb("wqkv_sb", [P, 2, 3 * D])
        bqk_sb = sb("bqk_sb", [P, 2, 2])
        bv_sb = sb("bv_sb", [P, 2, D])
        ln_sb = sb("ln_sb", [P, 4])
        wo_sb = sb("wo_sb", [P, 2, D])
        bo_sb = sb("bo_sb", [P, 2, D])
        wg_sb = sb("wg_sb", [P, E])
        powm = sb("powm", [P, 8])
        tokid = sb("tokid", [P, 2])
        slot0 = sb("slot0", [P, 2, E])
        prio = sb("prio", [P, 2, E])
        base = sb("base", [P, 2, E])
        empty = sb("empty", [P, ROW])

        q_stack = nc.dram_tensor("q_stack", [NPAIR + LPAIR, P, TERMS, PAIR], BF16, kind="Internal").ap()
        k_stack = nc.dram_tensor("k_stack", [NPAIR + LPAIR, P, TERMS, PAIR], BF16, kind="Internal").ap()
        v_rows = nc.dram_tensor("v_rows", [(NPAIR + LPAIR) * 2, S, D], F32, kind="Internal").ap()
        x_local = nc.dram_tensor("x_local", [B, LW, D], F32, kind="Internal").ap()
        routed = nc.dram_tensor("routed", [T, ROW], F32, kind="Internal").ap()

        c = dict(ident=ident, ident_bf=ident_bf, tri=tri, ones=ones, wqkv=wqkv_sb, bqk=bqk_sb, bv=bv_sb,
                 ln=ln_sb, wo=wo_sb, bo=bo_sb, wg=wg_sb, powm=powm, tokid=tokid, slot0=slot0, prio=prio,
                 base=base, empty=empty)
        with ExitStack() as stacks:
            qs = stacks.enter_context(nc.sbuf_tensor("qs", [P, 2, NH, S], BF16))
            ks = stacks.enter_context(nc.sbuf_tensor("ks", [P, 2, NH, S], BF16))
            vp = stacks.enter_context(nc.sbuf_tensor("vp", [P, 2, 2, NH, 32], F32))
            front(nc, c, qs, ks, vp, x, q_stack, k_stack, v_rows,
                  dict(ident=eye_in, tri=tri_in, wqkv=wqkv, bqk=bqk, bv=bv_row, ln=ln_cols, wo=wo, bo=bo_row,
                       wg=wg, tokid=tokid_in, slot0=slot_in, prio=prio_in), blockq_in, blockk_in)
            attend(nc, c, qs, ks, vp, x, q_stack, k_stack, v_rows, x_local, routed, out)
        experts(nc, c, w1, b1, w2, b2, routed, out)


def front(nc, c, qs, ks, vp, x, q_stack, k_stack, v_rows, given, blockq_in, blockk_in):
    x_t = x.rearrange("b (h p) d -> (b h) p d", p=P)
    v_t = v_rows.rearrange("u (h p) d -> (u h) p d", p=P)
    ctx = ExitStack()
    with ctx:
        def sb(name, shape, dt=F32):
            return ctx.enter_context(nc.sbuf_tensor(name, shape, dt))

        def sem(name):
            return ctx.enter_context(nc.semaphore(name))

        xt = sb("xt", [P, 4, 4, D])
        stats = sb("stats", [P, 4, 6])
        mv = sb("mv", [P, 4, 4, 2])
        veps = sb("veps", [P, 2, 4])
        rstd = sb("rstd", [P, 2, 4])
        xh = sb("xh", [P, 2, 4, D])
        xg = sb("xg", [P, 2, PAIR])
        xl = sb("xl", [P, B * LW])
        full = sb("full", [P, 2, 2, PAIR])
        rest = sb("rest", [P, 2, 2, PAIR])
        part = sb("part", [P, 4, 2, 3, PAIR], BF16)
        v_sb = sb("v_sb", [P, 4, 4, D])
        block_q = sb("block_q", [NBLK, S])
        block_k = sb("block_k", [NBLK, S])
        block_qb = sb("block_qb", [NBLK, S], BF16)
        block_kb = sb("block_kb", [NBLK, S], BF16)
        ps_x = ctx.enter_context(nc.psum_tensor("ps_x", [P, 2, PAIR], F32))
        ps_q = ctx.enter_context(nc.psum_tensor("ps_q", [P, 2, PAIR], F32))
        ps_k = ctx.enter_context(nc.psum_tensor("ps_k", [P, 2, PAIR], F32))
        ps_v = ctx.enter_context(nc.psum_tensor("ps_v", [P, 2, PAIR], F32))

        const_loaded = sem("const_loaded")
        stacks_cleared = sem("stacks_cleared")
        v_cleared = sem("v_cleared")
        mask_loaded = sem("mask_loaded")
        mask_cast = sem("mask_cast")
        mask_placed = sem("mask_placed")
        x_loaded = [sem(f"x_loaded{b}") for b in range(4)]
        stats_done = sem("stats_done")
        stats_ready = sem("stats_ready")
        norm_chain = Chain(sem("front_norm_chain"), 1)
        pow_set = sem("pow_set")
        rstd_ready = sem("rstd_ready")
        xh_ready = sem("xh_ready")
        xT_ready = sem("xT_ready")
        xg_ready = sem("xg_ready")
        xl_ready = sem("xl_ready")
        qk_projected = sem("qk_projected")
        v_projected = sem("v_projected")
        full_ready = sem("full_ready")
        v_ready = sem("v_ready")
        part1_ready = sem("part1_ready")
        rest_ready = sem("rest_ready")
        part2_ready = sem("part2_ready")
        part3_ready = sem("part3_ready")
        stack_stored = [sem(f"stack_stored{b}") for b in range(4)]
        v_stored = [sem(f"v_stored{b}") for b in range(4)]
        block = ctx.enter_context(nc.Block())
        NCONST = len(given)

        LAST = NPAIR + LPAIR

        def run(eng, stages):
            pipelined(eng, stages, unroll=4, loop_from=4, loop_to=8, ahead=5)

        def kind(u):
            return 1 if isinstance(u.n, int) and u.n >= NPAIR else 0

        @block.sync
        def _(sp):
            for name, src in given.items():
                sp.dma_start(c[name][:], src).then_inc(const_loaded, 16)

            def load(u):
                wait(sp, xh_ready, u.n - 3)
                sp.dma_start(xt[:, u.mod(4)], rows(x_t, 4 * u.n, 4).rearrange("t p d -> p t d")).then_inc(x_loaded[u.mod(4)], 16)

            def store(u):
                b = u.mod(4)
                sp.wait_ge(v_ready, u.n + 1)
                sp.dma_start(rows(v_t, 4 * u.n, 4).rearrange("t p d -> p t d"), v_sb[:, b]).then_inc(v_stored[b], 16)
                sp.wait_ge(part3_ready, u.n + 1)
                for s, stack in enumerate((q_stack, k_stack)):
                    dst = rows(stack, u.n, 1).rearrange("o r t n -> (o r) t n")
                    for k, (t0, n) in enumerate(((0, 3), (3, 2), (5, 1))):
                        if s == 0:
                            src = part[:, b, 0, k:k + 1, :].to_broadcast([P, n, PAIR])
                        else:
                            src = part[:, b, 1, 0:n, :]
                        sp.dma_start(dst[:, t0:t0 + n, :], src).then_inc(stack_stored[b], 16)
            def place_mask(u):
                if isinstance(u.n, int) and u.n == 0:
                    sp.wait_ge(stacks_cleared, 3)
                    sp.wait_ge(mask_cast, 2)
                    for h in range(2):
                        for dst, src in ((qs, block_qb), (ks, block_kb)):
                            sp.dma_start(dst[MASKROW:MASKROW + NBLK, h],
                                         src[:].unsqueeze(1).to_broadcast([NBLK, NH, S])).then_inc(mask_placed, 16)
            sp.dma_start(block_q[:], blockq_in).then_inc(mask_loaded, 16)
            sp.dma_start(block_k[:], blockk_in).then_inc(mask_loaded, 16)
            run(sp, [(5, NPAIR, load), (-1, LAST, store), (-10, 1, place_mask)])
            for b in range(4):
                uses = len(range(b, LAST, 4))
                sp.wait_ge(stack_stored[b], 16 * 6 * uses)
                sp.wait_ge(v_stored[b], 16 * uses)
            sp.wait_ge(mask_placed, 64)

        @block.vector
        def _(dve):
            nc.vector.memset(c["powm"][:], -0.5).then_inc(pow_set, 1)
            nc.vector.memset(c["ones"][:], 1.0)
            nc.vector.memset(c["base"][:], 0.0)
            nc.vector.memset(c["empty"][:, 0:D + 1], 0.0)
            nc.vector.memset(c["empty"][:, D + 1:ROW], NOWHERE)
            nc.vector.memset(qs[:].bitcast(U32), 0).then_inc(stacks_cleared, 1)
            dve.wait_ge(const_loaded, 16 * NCONST)
            nc.vector.tensor_copy(c["ident_bf"][:], c["ident"][:])
            dve.wait_ge(mask_loaded, 32)
            nc.vector.tensor_copy(block_qb[:], block_q[:]).then_inc(mask_cast, 1)
            nc.vector.tensor_copy(block_kb[:], block_k[:]).then_inc(mask_cast, 1)

            def statistics(u):
                b = u.mod(4)
                dve.wait_ge(x_loaded[b], 16 * (u.div(4) + 1))
                for t in range(4):
                    last = nc.vector.bn_stats(stats[:, t], xt[:, b, t])
                last.then_inc(stats_done, 1)
                hold(dve, stats_done, u.n + 1)
                for t in range(4):
                    last = nc.vector.bn_aggr(mv[:, b, t], stats[:, t])
                last.then_inc(stats_ready, 1)

            def normalize(u):
                dve.wait_ge(rstd_ready, u.n + 1)
                hold(dve, xT_ready, u.n - 1)
                for t in range(4):
                    last = nc.vector.tensor_scalar(xh[:, u.mod(2), t], xt[:, u.mod(4), t], mv[:, u.mod(4), t, 0:1],
                                                   rstd[:, u.mod(2), t:t + 1], ALU.subtract, ALU.mult)
                last.then_inc(xh_ready, 1)

            def local_tokens(u):
                dve.wait_ge(xg_ready, u.n + 1)
                src = ps_x[:, u.mod(2)].rearrange("f (b s) -> f b s", b=2)[:, :, 0:LW]
                dst = xl[:, bass.ds(2 * LW * u.n, 2 * LW)].rearrange("f (b s) -> f b s", b=2)
                nc.vector.tensor_scalar(dst, src, c["ln"][:, 2:3], c["ln"][:, 3:4], ALU.mult,
                                        ALU.add).then_inc(xl_ready, 1)

            def take_projections(u):
                k, h = kind(u), u.mod(2)
                dve.wait_ge(qk_projected, u.n + 1)
                wait(dve, part1_ready, u.n - 1)
                nc.vector.tensor_scalar(full[:, h, 0], ps_q[:, h], c["bqk"][:, k, 0:1], SCALE, ALU.add, ALU.mult)
                nc.vector.tensor_scalar(full[:, h, 1], ps_k[:, h], c["bqk"][:, k, 1:2], None,
                                        ALU.add).then_inc(full_ready, 1)
                dve.wait_ge(v_projected, u.n + 1)
                wait(dve, v_stored[u.mod(4)], 16 * u.div(4))
                nc.vector.tensor_tensor(v_sb[:, u.mod(4)], ps_v[:, h].rearrange("p (t d) -> p t d", t=4),
                                        c["bv"][:, k].unsqueeze(1).to_broadcast([P, 4, D]),
                                        ALU.add).then_inc(v_ready, 1)

            def take_rest(u):
                h = u.mod(2)
                dve.wait_ge(part1_ready, u.n + 1)
                wait(dve, part3_ready, u.n - 1)
                nc.vector.tensor_tensor(rest[:, h], full[:, h], part[:, u.mod(4), :, 0],
                                        ALU.subtract).then_inc(rest_ready, 1)
            run(dve, [(0, LAST, take_projections), (1, NPAIR, local_tokens), (3, NPAIR, normalize),
                      (4, NPAIR, statistics), (0, LAST, take_rest)])

        @block.gpsimd
        def _(pool):
            pool.wait_ge(pow_set, 1)

            def deviation(u):
                hold(pool, stats_ready, u.n + 1)
                hold(pool, xh_ready, u.n - 1)
                norm_chain.start(u.n)
                norm_chain.link(pool, nc.gpsimd.tensor_scalar(veps[:, u.mod(2)], mv[:, u.mod(4), :, 1], EPS, None, ALU.add))
                nc.gpsimd.tensor_tensor(rstd[:, u.mod(2)], veps[:, u.mod(2)], c["powm"][:, 0:4],
                                        ALU.pow).then_inc(rstd_ready, 1)
                norm_chain.end()

            def third_part(u):
                hold(pool, part2_ready, u.n + 1)
                p = part[:, u.mod(4)]
                nc.gpsimd.tensor_tensor(p[:, :, 2], rest[:, u.mod(2)], p[:, :, 1], ALU.subtract).then_inc(part3_ready, 1)
            def clear(u):
                if not (isinstance(u.n, int) and u.n == 0):
                    return
                nc.gpsimd.memset(ks[:].bitcast(U32), 0).then_inc(stacks_cleared, 1)
                nc.gpsimd.memset(vp[:], 0.0).then_inc(v_cleared, 1)
                pool.wait_ge(stacks_cleared, 2)
                pool.wait_ge(v_cleared, 1)
                for g in range(2):
                    dst = vp[:].rearrange("p c k (u g j) w -> p (c k u) g j w", g=2, j=4)
                    nc.gpsimd.memset(dst[:, :, g, :, 16 * g + DH:16 * g + DH + 1], 1.0).then_inc(v_cleared, 1)
                pool.wait_ge(v_cleared, 3)
                nc.gpsimd.memset(ks[MAXROW:KEXP], -1.0).then_inc(stacks_cleared, 1)
                pool.wait_ge(stacks_cleared, 3)
            run(pool, [(-1, LAST, third_part), (4, NPAIR, deviation), (0, 1, clear)])

        @block.scalar
        def _(act):
            act.wait_ge(const_loaded, 16 * NCONST)

            def scale_shift(u):
                h = u.mod(2)
                act.wait_ge(xT_ready, u.n + 1)
                wait(act, v_projected, u.n - 1)
                nc.scalar.activation(xg[:, h], ps_x[:, h], ACT.Identity, scale=c["ln"][:, 0:1],
                                     bias=c["ln"][:, 1:2]).then_inc(xg_ready, 1)

            def first_part(u):
                act.wait_ge(full_ready, u.n + 1)
                wait(act, stack_stored[u.mod(4)], 16 * 6 * u.div(4))
                nc.scalar.copy(part[:, u.mod(4), :, 0], full[:, u.mod(2)]).then_inc(part1_ready, 1)

            def second_part(u):
                act.wait_ge(rest_ready, u.n + 1)
                nc.scalar.copy(part[:, u.mod(4), :, 1], rest[:, u.mod(2)]).then_inc(part2_ready, 1)
            run(act, [(0, LAST, first_part), (2, NPAIR, scale_shift), (0, LAST, second_part)])

        @block.tensor
        def _(pe):
            pe.wait_ge(const_loaded, 16 * NCONST)

            def turn(u):
                pe.wait_ge(xh_ready, u.n + 1)
                wait(pe, xl_ready, u.n - 1)
                for t in range(4):
                    last = nc.tensor.transpose(ps_x[:, u.mod(2), t * P:(t + 1) * P], xh[:, u.mod(2), t], c["ident"][:])
                last.then_inc(xT_ready, 1)

            def project(u):
                k, h = kind(u), u.mod(2)
                w = c["wqkv"][:, k]
                if k == 0:
                    pe.wait_ge(xg_ready, u.n + 1)
                    src = xg[:, h]
                else:
                    pe.wait_ge(xl_ready, NPAIR)
                    src = xl[:, (u.n - NPAIR) * PAIR:(u.n - NPAIR + 1) * PAIR]
                wait(pe, full_ready, u.n - 1)
                nc.tensor.matmul(ps_q[:, h], w[:, 0:D], src, start=True, stop=True)
                nc.tensor.matmul(ps_k[:, h], w[:, D:2 * D], src, start=True, stop=True).then_inc(qk_projected, 1)
                wait(pe, v_ready, u.n - 1)
                for t in range(4):
                    last = nc.tensor.matmul(ps_v[:, h, t * D:(t + 1) * D], src[:, t * P:(t + 1) * P],
                                            w[:, 2 * D:3 * D], start=True, stop=True)
                last.then_inc(v_projected, 1)
            run(pe, [(2, NPAIR, turn), (1, LAST, project)])


def attend(nc, c, qs, ks, vp, x, q_stack, k_stack, v_rows, x_local, routed, out):
    LU = B * LW // S
    U = LU + B
    ctx = ExitStack()
    with ctx:
        def sb(name, shape, dt=F32):
            return ctx.enter_context(nc.sbuf_tensor(f"a_{name}", shape, dt))

        def sem(name):
            return ctx.enter_context(nc.semaphore(f"a_{name}"))

        prob = sb("prob", [P, 8, 2 * 2 * S])
        vc = sb("vc", [P, 2, 2, D])
        mx = sb("mx", [P, 2, 2, NH])
        mrest = sb("mrest", [P, 2, 2, 8])
        mpart = sb("mpart", [P, 2, 2, 3, 8], BF16)
        mT = sb("mT", [24, 2, S], BF16)
        oT = sb("oT", [P, 2 * S])
        rden = sb("rden", [P, 4, 8])
        oN = sb("oN", [P, 2, D])
        oNT = sb("oNT", [P, S])
        xr = sb("xr", [P, 2, 2, D])
        y = sb("y", [P, 2, 2, D])
        stats = sb("stats", [P, 2, 6])
        mv = sb("mv", [P, 2, 2])
        veps = sb("veps", [P, 2])
        rstd = sb("rstd", [P, 2])
        row = sb("row", [P, 2, 2, ROW])
        x1T = sb("x1T", [P, S])
        stats2 = sb("stats2", [P, 2, 6])
        mv2 = sb("mv2", [P, 2, 2])
        veps2 = sb("veps2", [P, 2])
        rstd2 = sb("rstd2", [P, 2])
        o1 = sb("o1", [P, 2, D])
        lmax = sb("lmax", [P, 2])
        shifted = sb("shifted", [P, 2, E])
        gexp = sb("gexp", [P, 2, E])
        gsum = sb("gsum", [P, 2])
        pri = sb("pri", [P, 2, E])
        pmax = sb("pmax", [P, 2])
        mask = sb("mask", [P, 2, E])
        count = sb("count", [P, 2, 2, E])
        loc = sb("loc", [P, 2, E])
        locslot = sb("locslot", [P, 2, 2, E])
        picked = sb("picked", [P, 2, 2])
        over = sb("over", [P, 2])
        slot = sb("slot", [P, 2], U32)
        ps_b = ctx.enter_context(nc.psum_tensor("a_ps_b", [P, 4, 2 * S], F32))
        ps_a = ctx.enter_context(nc.psum_tensor("a_ps_a", [P, 2, 2 * S], F32))
        ps_o = ctx.enter_context(nc.psum_tensor("a_ps_o", [P, 2 * S], F32))
        ps_m = ctx.enter_context(nc.psum_tensor("a_ps_m", [P, 2 * S], F32))
        ps_m_bf = ps_m[:].bitcast(BF16)

        stack_loaded = [[sem(f"stack_loaded{h}{f}") for f in range(2)] for h in range(2)]
        v_loaded = [sem("v_loaded0"), sem("v_loaded1")]
        xr_loaded = [sem("xr_loaded0"), sem("xr_loaded1")]
        routed_cleared = sem("routed_cleared")
        max_scores = sem("max_scores")
        max_done = sem("max_done")
        max_split = sem("max_split")
        max_turned = sem("max_turned")
        mT_ready = sem("mT_ready")
        max_rows = [sem("max_rows0"), sem("max_rows1")]
        v_spread = sem("v_spread")
        scores = sem("scores")
        exp_done = sem("exp_done")
        pv_done = sem("pv_done")
        oT_ready = sem("oT_ready")
        o_turned = sem("o_turned")
        o_normed = sem("o_normed")
        oN_turned = sem("oN_turned")
        oNT_ready = sem("oNT_ready")
        projected = sem("projected")
        xr_ready = sem("xr_ready")
        y_ready = sem("y_ready")
        y_stored = [sem("y_stored0"), sem("y_stored1")]
        split_chain = Chain(sem("split_chain"), 3)
        norm_chain = Chain(sem("norm_chain"), 1)
        stat_chain = Chain(sem("stat_chain"), 1)
        stats_ready = sem("stats_ready")
        dev_chain = Chain(sem("dev_chain"), 1)
        rstd_ready = sem("rstd_ready")
        x1_ready = sem("x1_ready")
        row_numbered = sem("row_numbered")
        tok_moved = sem("tok_moved")
        stat2_chain = Chain(sem("stat2_chain"), 1)
        stats2_ready = sem("stats2_ready")
        dev2_chain = Chain(sem("dev2_chain"), 1)
        rstd2_ready = sem("rstd2_ready")
        o1_ready = sem("o1_ready")
        o1_stored = sem("o1_stored")
        x1_turned = sem("x1_turned")
        x1T_ready = sem("x1T_ready")
        logits_ready = sem("logits_ready")
        logits_read = sem("logits_read")
        gexp_ready = sem("gexp_ready")
        mask_ready = sem("mask_ready")
        gate_ready = sem("gate_ready")
        counted = sem("counted")
        counts_copied = sem("counts_copied")
        mask_chain = Chain(sem("mask_chain"), 3)
        gate_chain = Chain(sem("gate_chain"), 1)
        place_chain = Chain(sem("place_chain"), 4)
        places_ready = sem("places_ready")
        pick_chain = Chain(sem("pick_chain"), 2)
        slot_ready = sem("slot_ready")
        scattered = [sem("scattered0"), sem("scattered1")]
        block = ctx.enter_context(nc.Block())

        def there(u):
            return not isinstance(u.n, int) or 0 <= u.n < U

        def is_local(u):
            return isinstance(u.n, int) and u.n < LU

        def routes(u):
            return there(u) and not is_local(u)

        def run(eng, unit):
            pipelined(eng, [(0, U + 3, unit)], unroll=2, loop_from=8, loop_to=U - 2, ahead=0)

        def batch(u):
            return Step(u.i, u.j - LU, 2)

        @block.sync
        def _(sp):
            def load_stack(u, half):
                h = u.mod(2)
                wait(sp, scores, 8 * (u.n - 2) + 4 * half + 4)
                heads = slice(8 * half, 8 * half + 8)
                pair = Step(u.i, u.j - LU, 2).div(2) if not is_local(u) else NPAIR + u.n // 2
                for dst, stack in ((qs, q_stack), (ks, k_stack)):
                    src = rows(stack, pair, 1)[0, 64 * half:64 * half + 64, :, h * S:(h + 1) * S]
                    sp.dma_start(dst[0:STACK, h, heads, :],
                                 src.rearrange("(g d) t n -> (d t) g n", d=DH)).then_inc(stack_loaded[h][half], 16)
                    if isinstance(u.n, int) and u.n in (LU, LU + 1):
                        sp.dma_start(dst[MASKROW:MASKROW + NBLK, h, heads, :],
                                     dst[MASKROW + NBLK:MASKROW + 2 * NBLK, h, heads, :]).then_inc(stack_loaded[h][half], 16)

            def load_v(u):
                h = u.mod(2)
                wait(sp, v_spread, u.n - 1)
                at = batch(u).n if not is_local(u) else B + u.n
                sp.dma_start(vc[:, h], rows(v_rows, at, 1).rearrange("o (k p) d -> p (o k) d", p=P)).then_inc(v_loaded[h], 16)

            def load_xr(u):
                h = u.mod(2)
                wait(sp, y_ready, u.n - 1)
                if is_local(u):
                    for t in range(2):
                        sp.dma_start(xr[:, h, t], x[8 * u.n + 4 * t:8 * u.n + 4 * t + 4, 0:LW, :]).then_inc(xr_loaded[h], 16)
                    return
                if isinstance(u.n, int) and u.n == LU:
                    sp.wait_ge(y_stored[0], 32)
                if isinstance(u.n, int) and u.n == LU + 3:
                    sp.wait_ge(y_stored[0], 64)
                    sp.wait_ge(y_stored[1], 64)
                at = batch(u).n
                sp.dma_start(xr[0:LW, h, 0], rows(x_local, at, 1).rearrange("o s d -> (o s) d")).then_inc(xr_loaded[h], 16)
                sp.dma_start(xr[LW:P, h, 0], rows(x, at, 1)[0, LW:P, :]).then_inc(xr_loaded[h], 16)
                sp.dma_start(xr[:, h, 1], rows(x, at, 1)[0, P:S, :]).then_inc(xr_loaded[h], 16)

            def place_max(u, half):
                sp.wait_ge(mT_ready, 2 * u.n + half + 1)
                sp.dma_start(qs[MAXROW:KEXP, u.mod(2), 8 * half:8 * half + 8, :], mT[:, half, :]).then_inc(max_rows[half], 16)

            def store_y(u):
                sp.wait_ge(y_ready, u.n + 1)
                for t in range(2):
                    sp.dma_start(x_local[8 * u.n + 4 * t:8 * u.n + 4 * t + 4],
                                 y[:, u.mod(2), t]).then_inc(y_stored[u.mod(2)], 16)

            def store_o1(u):
                g = batch(u)
                sp.wait_ge(o1_ready, g.n + 1)
                sp.dma_start(rows(out, g.n, 1).rearrange("o (t p) d -> p (o t) d", p=P), o1[:]).then_inc(o1_stored, 16)

            def unit(u):
                after1, after2, before2, before3 = u.plus(1), u.plus(2), u.plus(-2), u.plus(-3)
                if isinstance(u.n, int) and u.n == 0:
                    load_stack(u, 0)
                    load_stack(u, 1)
                    load_v(u)
                    load_stack(after1, 0)
                    place_max(u, 0)
                if there(after1):
                    load_stack(after1, 1)
                    load_v(after1)
                if there(u):
                    load_xr(u)
                if routes(before3):
                    store_o1(before3)
                if is_local(before2) and there(before2):
                    store_y(before2)
                if there(u):
                    place_max(u, 1)
                if there(after2):
                    load_stack(after2, 0)
                if there(after1):
                    place_max(after1, 0)
            run(sp, unit)
            sp.wait_ge(o1_stored, 16 * B)

        @block.tensor
        def _(pe):
            def max_pass(u, hp):
                h = u.mod(2)
                if hp % 4 == 0:
                    extra = 0 if isinstance(u.n, int) and u.n < LU else 32
                    pe.wait_ge(stack_loaded[h][hp // 4], 32 * (u.div(2) + 1) + extra)
                for qt in range(2):
                    wait(pe, max_done, 16 * u.n + 2 * hp + qt - 1)
                    for e in range(2):
                        last = nc.tensor.matmul(ps_a[:, qt, e * S:(e + 1) * S],
                                                qs[0:KMAX, h, 2 * hp + e, qt * P:(qt + 1) * P],
                                                ks[0:KMAX, h, 2 * hp + e, :], start=True, stop=True)
                    last.then_inc(max_scores, 1)

            def exp_pass(u, hp):
                if hp % 4 == 0:
                    pe.wait_ge(max_rows[hp // 4], 16 * (u.n + 1))
                wait(pe, exp_done, 8 * u.n + hp - 1)
                for e in range(2):
                    for kt in range(2):
                        last = nc.tensor.matmul(ps_b[:, 2 * (hp % 2) + e, kt * S:(kt + 1) * S],
                                                ks[0:KEXP, u.mod(2), 2 * hp + e, kt * P:(kt + 1) * P],
                                                qs[0:KEXP, u.mod(2), 2 * hp + e, :], start=True, stop=True)
                last.then_inc(scores, 1)

            def p_v(u, q, kt):
                if q == 0 and kt == 0:
                    wait(pe, oT_ready, u.n)
                    pe.wait_ge(v_spread, u.n + 1)
                if kt == 0:
                    pe.wait_ge(exp_done, 8 * u.n + 2 * q + 2)
                for j in range(4):
                    at = (j % 2) * 2 * S + kt * S
                    last = nc.tensor.matmul(ps_o[32 * j:32 * j + 32, (q // 2) * S:(q // 2 + 1) * S],
                                            vp[:, u.mod(2), kt, 4 * q + j, :],
                                            prob[:, 2 * q + j // 2, at:at + S],
                                            start=(q % 2 == 0 and kt == 0), stop=(q % 2 == 1 and kt == 1))
                if kt == 1:
                    last.then_inc(pv_done, 1)

            def turn_max(u, half):
                pe.wait_ge(max_split, 2 * u.n + half + 1)
                for qt in range(2):
                    last = nc.tensor.transpose(ps_m_bf[0:24, qt * P:(qt + 1) * P],
                                               mpart[:, half, qt].rearrange("p a h -> p (a h)"), c["ident_bf"][:])
                last.then_inc(max_turned, 1)

            def turn_o(u):
                pe.wait_ge(oT_ready, u.n + 1)
                for qt in range(2):
                    for g in range(2):
                        last = nc.tensor.transpose(ps_m[:, (2 * qt + g) * P:(2 * qt + g + 1) * P],
                                                   oT[:, g * S + qt * P:g * S + (qt + 1) * P], c["ident"][:])
                last.then_inc(o_turned, 1)

            def turn_oN(u):
                pe.wait_ge(o_normed, u.n + 1)
                for qt in range(2):
                    last = nc.tensor.transpose(ps_m[:, qt * P:(qt + 1) * P], oN[:, qt], c["ident"][:])
                last.then_inc(oN_turned, 1)

            def project(u):
                pe.wait_ge(oNT_ready, u.n + 1)
                for qt in range(2):
                    last = nc.tensor.matmul(ps_m[:, qt * D:(qt + 1) * D], oNT[:, qt * P:(qt + 1) * P],
                                            c["wo"][:, 1 if is_local(u) else 0], start=True, stop=True)
                last.then_inc(projected, 1)

            def turn_x1(u):
                g = batch(u)
                pe.wait_ge(x1_ready, g.n + 1)
                for qt in range(2):
                    last = nc.tensor.transpose(ps_m[:, qt * P:(qt + 1) * P], row[:, u.mod(2), qt, 0:D], c["ident"][:])
                last.then_inc(x1_turned, 1)

            def logits(u):
                pe.wait_ge(x1T_ready, batch(u).n + 1)
                for qt in range(2):
                    last = nc.tensor.matmul(ps_m[:, qt * E:(qt + 1) * E], x1T[:, qt * P:(qt + 1) * P],
                                            c["wg"][:], start=True, stop=True)
                last.then_inc(logits_ready, 1)

            def count_tokens(u):
                pe.wait_ge(mask_ready, batch(u).n + 1)
                m = mask[:].rearrange("p t e -> p (t e)")
                nc.tensor.matmul(ps_m[:, 0:2 * E], c["tri"][:], m, start=True, stop=True)
                nc.tensor.matmul(ps_m[:, 2 * E:4 * E], c["ones"][:], m, start=True, stop=True).then_inc(counted, 1)

            def unit(u):
                after1, before1, before2, before3 = u.plus(1), u.plus(-1), u.plus(-2), u.plus(-3)
                if isinstance(u.n, int) and u.n == 0:
                    for hp in range(8):
                        max_pass(u, hp)
                        if hp == 6:
                            turn_max(u, 0)
                for hp in range(8):
                    if there(u):
                        exp_pass(u, hp)
                    if hp <= 2 and there(before1):
                        q, kt = divmod(hp + 5, 2)
                        p_v(before1, q, kt)
                    if hp >= 4 and there(u):
                        p_v(u, *divmod(hp - 3, 2))
                    if there(after1):
                        max_pass(after1, hp)
                    if hp == 0 and routes(before3):
                        wait(pe, y_ready, u.n - 1 if there(before2) else U)
                        count_tokens(before3)
                    if hp == 1 and there(u):
                        wait(pe, y_ready, u.n - 1)
                        if routes(before3):
                            pe.wait_ge(counts_copied, batch(before3).n + 1)
                        turn_max(u, 1)
                    if hp == 2 and routes(before2):
                        if there(u):
                            pe.wait_ge(mT_ready, 2 * u.n + 2)
                        elif routes(before3):
                            pe.wait_ge(counts_copied, batch(before3).n + 1)
                        turn_x1(before2)
                    if hp == 3 and there(before1):
                        if there(u):
                            pe.wait_ge(mT_ready, 2 * u.n + 2)
                        if routes(before2):
                            pe.wait_ge(x1T_ready, batch(before2).n + 1)
                        turn_o(before1)
                    if hp == 4 and routes(before2):
                        if there(before1):
                            pe.wait_ge(o_normed, u.n)
                        logits(before2)
                    if hp == 5 and there(before1):
                        if routes(before2):
                            pe.wait_ge(logits_read, batch(before2).n + 1)
                        turn_oN(before1)
                    if hp == 6 and there(after1):
                        if there(before1):
                            pe.wait_ge(oNT_ready, u.n)
                        else:
                            pe.wait_ge(mT_ready, 2 * u.n + 2)
                        turn_max(after1, 0)
                    if hp == 7 and there(before1):
                        if there(after1):
                            pe.wait_ge(mT_ready, 2 * u.n + 3)
                        project(before1)
                    if hp == 3 and there(u):
                        p_v(u, 0, 0)
            run(pe, unit)

        @block.scalar
        def _(act):
            def exponential(u, hp):
                act.wait_ge(scores, 8 * u.n + hp + 1)
                wait(act, pv_done, 4 * u.n + hp // 2 - 3)
                nc.scalar.activation(prob[:, hp, :], ps_b[:, 2 * (hp % 2):2 * (hp % 2) + 2, :].rearrange("p a n -> p (a n)"),
                                     ACT.Exp).then_inc(exp_done, 1)

            def copy_max(u, half):
                act.wait_ge(max_turned, 2 * u.n + half + 1)
                wait(act, max_rows[half], 16 * u.n)
                nc.scalar.copy(mT[:, half, :], ps_m_bf[0:24, 0:S]).then_inc(mT_ready, 1)

            def copy_o(u):
                act.wait_ge(pv_done, 4 * u.n + 4)
                wait(act, o_turned, u.n)
                nc.scalar.copy(oT[:], ps_o[:]).then_inc(oT_ready, 1)

            def copy_oNT(u):
                act.wait_ge(oN_turned, u.n + 1)
                wait(act, projected, u.n)
                nc.scalar.copy(oNT[:], ps_m[:, 0:S]).then_inc(oNT_ready, 1)

            def copy_x1T(u):
                g = batch(u)
                act.wait_ge(x1_turned, g.n + 1)
                wait(act, logits_ready, g.n)
                nc.scalar.copy(x1T[:], ps_m[:, 0:S]).then_inc(x1T_ready, 1)

            def gate_exp(u):
                g = batch(u)
                act.wait_ge(logits_read, g.n + 1)
                wait(act, gate_ready, g.n)
                nc.scalar.activation(gexp[:], shifted[:], ACT.Exp).then_inc(gexp_ready, 1)

            def copy_counts(u):
                g = batch(u)
                act.wait_ge(counted, g.n + 1)
                wait(act, places_ready, g.n)
                nc.scalar.copy(count[:].rearrange("p a t e -> p (a t e)"), ps_m[:, 0:4 * E]).then_inc(counts_copied, 1)

            def unit(u):
                after1, before1, before2, before3 = u.plus(1), u.plus(-1), u.plus(-2), u.plus(-3)
                if isinstance(u.n, int) and u.n == 0:
                    copy_max(u, 0)
                for hp in range(8):
                    if there(u):
                        exponential(u, hp)
                    if hp == 0 and routes(before3):
                        copy_counts(before3)
                    if hp == 1 and there(u):
                        copy_max(u, 1)
                    if hp == 2 and there(before1):
                        copy_o(before1)
                    if hp == 2 and routes(before2):
                        copy_x1T(before2)
                    if hp == 5 and routes(before2):
                        gate_exp(before2)
                    if hp == 5 and there(before1):
                        copy_oNT(before1)
                    if hp == 6 and there(after1):
                        copy_max(after1, 0)
            run(act, unit)

        @block.vector
        def _(dve):
            def take_max(u, hp):
                for qt in range(2):
                    dve.wait_ge(max_scores, 16 * u.n + 2 * hp + qt + 1)
                    if qt == 0 and hp % 4 == 0:
                        wait(dve, max_split, 2 * u.n - 3 + hp // 4)
                    nc.vector.reduce_max(mx[:, u.mod(2), qt, 2 * hp:2 * hp + 2],
                                         ps_a[:, qt].rearrange("p (e k) -> p e k", e=2), axis=AX).then_inc(max_done, 1)

            def norm_o(u):
                dve.wait_ge(o_turned, u.n + 1)
                v = ps_m[:].rearrange("p (a g w) -> p a g w", a=4, w=16)
                norm_chain.start(u.n)
                norm_chain.link(dve, nc.vector.reciprocal(rden[:], v[:, :, :, DH]))
                norm_chain.end()
                wait(dve, oN_turned, u.n)
                nc.vector.tensor_tensor(oN[:].rearrange("p t (g d) -> p (t g) d", d=DH).rearrange("p (a g) d -> p a g d", a=4),
                                        v[:, :, :, 0:DH],
                                        rden[:].unsqueeze(3).to_broadcast([P, 4, 8, DH]), ALU.mult).then_inc(o_normed, 1)

            def add_residual(u):
                h = u.mod(2)
                dve.wait_ge(projected, u.n + 1)
                if isinstance(u.n, int) and 2 <= u.n < LU + 2:
                    dve.wait_ge(y_stored[h], 32 * (u.n // 2))
                dve.wait_ge(xr_ready, u.n + 1)
                nc.vector.tensor_tensor(y[:, h], ps_m[:, 0:2 * D].rearrange("p (t d) -> p t d", t=2), xr[:, h],
                                        ALU.add).then_inc(y_ready, 1)

            def statistics(u):
                g = batch(u)
                dve.wait_ge(y_ready, u.n + 1)
                stat_chain.start(g.n)
                for t in range(2):
                    last = nc.vector.bn_stats(stats[:, t], y[:, u.mod(2), t])
                stat_chain.link(dve, last)
                stat_chain.end()
                for t in range(2):
                    last = nc.vector.bn_aggr(mv[:, t], stats[:, t])
                last.then_inc(stats_ready, 1)

            def norm_rows(u):
                g, h = batch(u), u.mod(2)
                wait(dve, scattered[h], 32 * g.div(2))
                dve.wait_ge(rstd_ready, g.n + 1)
                for t in range(2):
                    last = nc.vector.tensor_scalar(row[:, h, t, 0:D], y[:, h, t], mv[:, t, 0:1], rstd[:, t:t + 1],
                                                   ALU.subtract, ALU.mult)
                last.then_inc(x1_ready, 1)

            def second_statistics(u):
                g = batch(u)
                stat2_chain.start(g.n)
                dve.wait_ge(x1_ready, g.n + 1)
                for t in range(2):
                    last = nc.vector.bn_stats(stats2[:, t], row[:, u.mod(2), t, 0:D])
                stat2_chain.link(dve, last)
                stat2_chain.end()
                for t in range(2):
                    last = nc.vector.bn_aggr(mv2[:, t], stats2[:, t])
                last.then_inc(stats2_ready, 1)

            def norm_again(u):
                g = batch(u)
                wait(dve, o1_stored, 16 * g.n)
                dve.wait_ge(rstd2_ready, g.n + 1)
                for t in range(2):
                    last = nc.vector.tensor_scalar(o1[:, t], row[:, u.mod(2), t, 0:D], mv2[:, t, 0:1], rstd2[:, t:t + 1],
                                                   ALU.subtract, ALU.mult)
                last.then_inc(o1_ready, 1)

            def route(u):
                g = batch(u)
                dve.wait_ge(logits_ready, g.n + 1)
                lg = ps_m[:, 0:2 * E].rearrange("p (t e) -> p t e", t=2)
                mask_chain.start(g.n)
                mask_chain.link(dve, nc.vector.reduce_max(lmax[:], lg, axis=AX))
                nc.vector.tensor_tensor(shifted[:], lg, lmax[:].unsqueeze(2).to_broadcast([P, 2, E]),
                                        ALU.subtract).then_inc(logits_read, 1)
                dve.wait_ge(logits_read, g.n + 1)
                mask_chain.link(dve, nc.vector.scalar_tensor_tensor(out=pri[:], in0=shifted[:], scalar=0.0,
                                                                    in1=c["prio"][:], op0=ALU.is_ge, op1=ALU.mult))
                mask_chain.link(dve, nc.vector.reduce_max(pmax[:], pri[:], axis=AX))
                mask_chain.end()
                wait(dve, places_ready, g.n)
                nc.vector.tensor_tensor(mask[:], pri[:], pmax[:].unsqueeze(2).to_broadcast([P, 2, E]),
                                        ALU.is_equal).then_inc(mask_ready, 1)

            def gate(u):
                g = batch(u)
                dve.wait_ge(gexp_ready, g.n + 1)
                gate_chain.start(g.n)
                gate_chain.link(dve, nc.vector.reduce_sum(gsum[:], gexp[:], axis=AX))
                gate_chain.end()
                nc.vector.reciprocal(row[:, u.mod(2), :, D], gsum[:]).then_inc(gate_ready, 1)

            def pick(u):
                g = batch(u)
                dve.wait_ge(places_ready, g.n + 1)
                pick_chain.start(g.n)
                pick_chain.link(dve, nc.vector.reduce_sum(picked[:], locslot[:], axis=AX))
                pick_chain.link(dve, nc.vector.tensor_scalar(over[:], picked[:, 0], CAP + 0.5, NOWHERE, ALU.is_gt, ALU.mult))
                pick_chain.end()
                before = g.plus(-1)
                wait(dve, scattered[before.mod(2)], 32 * (before.div(2) + 1))
                nc.vector.tensor_tensor(slot[:], picked[:, 1], over[:], ALU.add).then_inc(slot_ready, 1)

            def unit(u):
                after1, before1, before2, before3 = u.plus(1), u.plus(-1), u.plus(-2), u.plus(-3)
                if isinstance(u.n, int) and u.n == 0:
                    for hp in range(8):
                        take_max(u, hp)
                for hp in range(8):
                    if hp == 0 and there(before2):
                        add_residual(before2)
                    if routes(before2):
                        if hp == 0:
                            statistics(before2)
                        if hp == 1:
                            norm_rows(before2)
                            second_statistics(before2)
                        if hp == 3:
                            norm_again(before2)
                    if hp == 3 and routes(before3):
                        pick(before3)
                    if hp == 4 and there(before1):
                        norm_o(before1)
                    if hp == 5 and routes(before2):
                        route(before2)
                    if hp == 6 and routes(before2):
                        gate(before2)
                    if there(after1):
                        take_max(after1, hp)
            run(dve, unit)

        @block.gpsimd
        def _(pool):
            def split_max(u, half):
                hold(pool, max_done, 16 * u.n + 8 * half + 8)
                hold(pool, max_turned, 2 * u.n + half - 1)
                src = mx[:, u.mod(2), :, 8 * half:8 * half + 8]
                r, part = mrest[:, half], mpart[:, half]
                split_chain.start(2 * u.n + half)
                split_chain.link(pool, nc.gpsimd.tensor_copy(part[:, :, 0], src))
                split_chain.link(pool, nc.gpsimd.tensor_tensor(r, src, part[:, :, 0], ALU.subtract))
                split_chain.link(pool, nc.gpsimd.tensor_copy(part[:, :, 1], r))
                split_chain.end()
                nc.gpsimd.tensor_tensor(part[:, :, 2], r, part[:, :, 1], ALU.subtract).then_inc(max_split, 1)

            def spread_v(u):
                h = u.mod(2)
                hold(pool, v_loaded[h], 16 * (u.div(2) + 1))
                hold(pool, pv_done, 4 * (u.n - 1))
                for g in range(2):
                    dst = vp[:, h].rearrange("p k (u g j) w -> p k u g j w", g=2, j=4)[:, :, :, g, :, 16 * g:16 * g + DH]
                    src = vc[:, h].rearrange("p k (u g j d) -> p k u g j d", g=2, j=4, d=DH)[:, :, :, g]
                    for kt in range(2):
                        last = nc.gpsimd.tensor_copy(dst[:, kt], src[:, kt])
                last.then_inc(v_spread, 1)

            def bias_residual(u):
                h = u.mod(2)
                if is_local(u):
                    hold(pool, xr_loaded[h], 32 * (u.div(2) + 1))
                else:
                    hold(pool, xr_loaded[h], 32 * LU // 2 + 48 * (batch(u).div(2) + 1))
                nc.gpsimd.tensor_tensor(xr[:, h], xr[:, h], c["bo"][:, 1 if is_local(u) else 0].unsqueeze(1).to_broadcast([P, 2, D]),
                                        ALU.add).then_inc(xr_ready, 1)

            def deviation(u):
                g = batch(u)
                hold(pool, stats_ready, g.n + 1)
                dev_chain.start(g.n)
                dev_chain.link(pool, nc.gpsimd.tensor_scalar(veps[:], mv[:, :, 1], EPS, None, ALU.add))
                dev_chain.end()
                nc.gpsimd.tensor_tensor(rstd[:], veps[:], c["powm"][:, 0:2], ALU.pow).then_inc(rstd_ready, 1)

            def number_rows(u):
                g, h = batch(u), u.mod(2)
                hold(pool, scattered[h], 32 * g.div(2))
                hold(pool, tok_moved, g.n)
                nc.gpsimd.tensor_copy(row[:, h, :, D + 1], c["tokid"][:]).then_inc(row_numbered, 1)
                hold(pool, row_numbered, g.n + 1)
                nc.gpsimd.tensor_scalar(c["tokid"][:], c["tokid"][:], float(S), None, ALU.add).then_inc(tok_moved, 1)

            def second_deviation(u):
                g = batch(u)
                hold(pool, stats2_ready, g.n + 1)
                dev2_chain.start(g.n)
                dev2_chain.link(pool, nc.gpsimd.tensor_scalar(veps2[:], mv2[:, :, 1], EPS, None, ALU.add))
                dev2_chain.end()
                nc.gpsimd.tensor_tensor(rstd2[:], veps2[:], c["powm"][:, 0:2], ALU.pow).then_inc(rstd2_ready, 1)

            def queue_places(u):
                g = batch(u)
                hold(pool, counts_copied, g.n + 1)
                b = c["base"]
                place_chain.start(g.n)
                place_chain.link(pool, nc.gpsimd.tensor_tensor(b[:, 1], b[:, 0], count[:, 1, 0], ALU.add))
                place_chain.link(pool, nc.gpsimd.tensor_tensor(loc[:], count[:, 0], b[:], ALU.add))
                nc.gpsimd.tensor_tensor(locslot[:, 0], loc[:], mask[:], ALU.mult)
                place_chain.link(pool, nc.gpsimd.tensor_tensor(b[:, 0], b[:, 1], count[:, 1, 1], ALU.add))
                place_chain.link(pool, nc.gpsimd.tensor_tensor(loc[:], loc[:], c["slot0"][:], ALU.add))
                place_chain.end()
                nc.gpsimd.tensor_tensor(locslot[:, 1], loc[:], mask[:], ALU.mult).then_inc(places_ready, 1)

            def scatter(u):
                g, h = batch(u), u.mod(2)
                if isinstance(g.n, int) and g.n == 0:
                    pool.wait_ge(routed_cleared, 16)
                hold(pool, slot_ready, g.n + 1)
                hold(pool, gate_ready, g.n + 1)
                for t in range(2):
                    pool.indirect_dma_start(out=routed, out_offset=bass.IndirectOffsetOnAxis(ap=slot[:, t:t + 1], axis=0),
                                            in_=row[:, h, t, :], in_offset=None, bounds_check=T - 1,
                                            oob_is_err=False).then_inc(scattered[h], 16)

            def unit(u):
                after1, before2, before3 = u.plus(1), u.plus(-2), u.plus(-3)
                if isinstance(u.n, int) and u.n == 0:
                    pool.dma_start(routed.rearrange("(t p) r -> p t r", p=P),
                                   c["empty"][:].unsqueeze(1).to_broadcast([P, T // P, ROW])).then_inc(routed_cleared, 16)
                    split_max(u, 0)
                    spread_v(u)
                if there(u):
                    split_max(u, 1)
                if routes(before2):
                    deviation(before2)
                    number_rows(before2)
                if routes(before3):
                    queue_places(before3)
                if routes(before2):
                    second_deviation(before2)
                if there(after1):
                    spread_v(after1)
                if there(u):
                    bias_residual(u)
                if routes(before3):
                    scatter(before3)
                if there(after1):
                    split_max(after1, 0)
            run(pool, unit)
            for h in range(2):
                hold(pool, scattered[h], 32 * (B // 2))


def experts(nc, c, w1, b1, w2, b2, routed, out):
    routed_t = routed.rearrange("(n p) r -> n p r", p=P)
    out_rows = out.rearrange("b s d -> (b s) d")
    ctx = ExitStack()
    with ctx:
        def sb(name, shape, dt=F32):
            return ctx.enter_context(nc.sbuf_tensor(name, shape, dt))

        def sem(name):
            return ctx.enter_context(nc.semaphore(name))

        w1_sb = sb("w1_sb", [P, 2, F])
        w2_sb = sb("w2_sb", [P, 2, FT, D])
        b1_sb = sb("b1_sb", [P, 2, FT])
        b2_sb = sb("b2_sb", [P, 2, D])
        rows_sb = sb("rows_sb", [P, 4, CT, ROW])
        xT = sb("xT", [P, 2, CH])
        hT = sb("hT", [P, 2, FT, CH])
        t1 = sb("t1", [P, 2, CT, D])
        z = sb("z", [P, 2, CT, D])
        stats = sb("e_stats", [P, CT, 6])
        mv = sb("e_mv", [P, 2, CT, 2])
        veps = sb("e_veps", [P, 2, CT])
        rstd = sb("e_rstd", [P, 2, CT])
        res = sb("res", [P, 2, CT, D])
        dest = sb("dest", [P, 2, CT], U32)
        ps_x = ctx.enter_context(nc.psum_tensor("e_ps_x", [P, CH], F32))
        ps_h = ctx.enter_context(nc.psum_tensor("e_ps_h", [P, FT, CH], F32))
        ps_y = ctx.enter_context(nc.psum_tensor("e_ps_y", [P, 2, CH], F32))

        w_loaded = [sem("w_loaded0"), sem("w_loaded1")]
        rows_loaded = [sem(f"rows_loaded{h}") for h in range(4)]
        rows_turned = sem("rows_turned")
        xT_ready = sem("e_xT_ready")
        hidden = sem("hidden")
        hT_ready = sem("hT_ready")
        y_ready = sem("e_y_ready")
        y_read = sem("e_y_read")
        post_chain = Chain(sem("post_chain"), 2)
        z_stats = sem("z_stats")
        ln_chain = Chain(sem("e_ln_chain"), 1)
        rstd_ready = sem("e_rstd_ready")
        res_ready = sem("res_ready")
        scattered = [sem("e_scattered0"), sem("e_scattered1")]
        block = ctx.enter_context(nc.Block())

        def steps(eng, before, step, after):
            before()

            def body(i, first, last):
                for h in range(4):
                    step(4 * i + h, i, h, last)
            stepped(eng, NCH // 4, body)
            after()

        @block.sync
        def _(sp):
            def load_w(e, ie, he):
                wait(sp, y_read, 2 * e - 2)
                sp.dma_start(w1_sb[:, he], rows(w1, e, 1).rearrange("o k f -> (o k) f")).then_inc(w_loaded[he], 16)
                sp.dma_start(w2_sb[:, he], rows(w2, e, 1).rearrange("o (g p) d -> p (o g) d", p=P)).then_inc(w_loaded[he], 16)
                sp.dma_start(b1_sb[:, he], rows(b1, e, 1).rearrange("o p g -> (o p) g")).then_inc(w_loaded[he], 16)
                sp.dma_start(b2_sb[:, he], rows(b2, e, 1).to_broadcast([P, D])).then_inc(w_loaded[he], 16)

            def load_rows(k, h):
                wait(sp, z_stats, k - 3)
                sp.dma_start(rows_sb[:, h], rows(routed_t, CT * k, CT).rearrange("t p r -> p t r")).then_inc(rows_loaded[h], 16)

            def before():
                load_rows(0, 0)
                load_w(0, 0, 0)
                load_rows(1, 1)
                load_rows(2, 2)

            def step(k, i, h, last):
                if h % 2 == 0 and not (last and h == 2):
                    load_w(2 * i + h // 2 + 1, i + (h // 2 + 1) // 2, (h // 2 + 1) % 2)
                if not (last and h > 0):
                    load_rows(k + 3, (h + 3) % 4)

            def after():
                pass
            steps(sp, before, step, after)

        @block.tensor
        def _(pe):
            def turn(k, ih, h):
                pe.wait_ge(rows_loaded[h], 16 * (ih + 1))
                wait(pe, xT_ready, k)
                for t in range(CT):
                    last = nc.tensor.transpose(ps_x[:, t * P:(t + 1) * P], rows_sb[:, h, t, 0:D], c["ident"][:])
                last.then_inc(rows_turned, 1)

            def up(k, ie, he):
                pe.wait_ge(xT_ready, k + 1)
                pe.wait_ge(w_loaded[he], 64 * (ie + 1))
                for f in range(FT):
                    wait(pe, hT_ready, FT * (k - 1) + f + 1)
                    nc.tensor.matmul(ps_h[:, f], w1_sb[:, he, f * P:(f + 1) * P], xT[:, h_of(k)],
                                     start=True, stop=True).then_inc(hidden, 1)

            def down(k, he, hk):
                pe.wait_ge(hT_ready, FT * (k + 1))
                wait(pe, y_read, k - 1)
                for t in range(CT):
                    for f in range(FT):
                        last = nc.tensor.matmul(ps_y[:, hk, t * D:(t + 1) * D], hT[:, hk, f, t * P:(t + 1) * P],
                                                w2_sb[:, he, f], start=(f == 0), stop=(f == FT - 1))
                last.then_inc(y_ready, 1)

            parity = [0]

            def h_of(k):
                return parity[0]

            def before():
                turn(0, 0, 0)
                turn(1, 0, 1)
                parity[0] = 0
                up(0, 0, 0)

            def step(k, i, h, last):
                if not (last and h == 3):
                    parity[0] = (h + 1) % 2
                    up(k + 1, i + (h + 1) // 4, ((h + 1) // 2) % 2)
                if not (last and h >= 2):
                    turn(k + 2, i + (h + 2) // 4, (h + 2) % 4)
                down(k, (h // 2) % 2, h % 2)

            def after():
                pass
            steps(pe, before, step, after)

        @block.scalar
        def _(act):
            def copy_x(k, hk):
                act.wait_ge(rows_turned, k + 1)
                wait(act, hidden, FT * (k - 1))
                nc.scalar.copy(xT[:, hk], ps_x[:]).then_inc(xT_ready, 1)

            def relu(k, he, hk):
                wait(act, y_ready, k - 1)
                for f in range(FT):
                    act.wait_ge(hidden, FT * k + f + 1)
                    nc.scalar.activation(hT[:, hk, f], ps_h[:, f], ACT.Relu, bias=b1_sb[:, he, f:f + 1]).then_inc(hT_ready, 1)

            def before():
                copy_x(0, 0)
                copy_x(1, 1)
                relu(0, 0, 0)

            def step(k, i, h, last):
                if not (last and h == 3):
                    relu(k + 1, ((h + 1) // 2) % 2, (h + 1) % 2)
                if not (last and h >= 2):
                    copy_x(k + 2, h % 2)

            def after():
                pass
            steps(act, before, step, after)

        @block.vector
        def _(dve):
            def before():
                pass

            def step(k, i, h, last):
                he, hk = (h // 2) % 2, h % 2
                post_chain.start(k)
                dve.wait_ge(y_ready, k + 1)
                nc.vector.tensor_tensor(t1[:, hk], ps_y[:, hk].rearrange("p (t d) -> p t d", t=CT),
                                        b2_sb[:, he].unsqueeze(1).to_broadcast([P, CT, D]), ALU.add).then_inc(y_read, 1)
                dve.wait_ge(y_read, k + 1)
                for t in range(CT):
                    ins = nc.vector.scalar_tensor_tensor(out=z[:, hk, t], in0=t1[:, hk, t],
                                                         scalar=rows_sb[:, h, t, D:D + 1],
                                                         in1=rows_sb[:, h, t, 0:D], op0=ALU.mult, op1=ALU.add)
                post_chain.link(dve, ins)
                for t in range(CT):
                    ins = nc.vector.bn_stats(stats[:, t], z[:, hk, t])
                post_chain.link(dve, ins)
                post_chain.end()
                wait(dve, scattered[hk], 16 * CT * (2 * i + h // 2))
                nc.vector.tensor_copy(dest[:, hk], rows_sb[:, h, :, D + 1])
                for t in range(CT):
                    ins = nc.vector.bn_aggr(mv[:, hk, t], stats[:, t])
                ins.then_inc(z_stats, 1)

            def normalize(k, hk):
                dve.wait_ge(rstd_ready, k + 1)
                for t in range(CT):
                    ins = nc.vector.tensor_scalar(res[:, hk, t], z[:, hk, t], mv[:, hk, t, 0:1], rstd[:, hk, t:t + 1],
                                                  ALU.subtract, ALU.mult)
                ins.then_inc(res_ready, 1)

            def step_then_last(k, i, h, last):
                step(k, i, h, last)
                if not (isinstance(k, int) and k == 0):
                    normalize(k - 1, (h + 1) % 2)

            def after():
                normalize(NCH - 1, 1)
            steps(dve, before, step_then_last, after)

        @block.gpsimd
        def _(pool):
            def before():
                pass

            def step(k, i, h, last):
                hk = h % 2
                hold(pool, z_stats, k + 1)
                ln_chain.start(k)
                ln_chain.link(pool, nc.gpsimd.tensor_scalar(veps[:, hk], mv[:, hk, :, 1], EPS, None, ALU.add))
                ln_chain.end()
                nc.gpsimd.tensor_tensor(rstd[:, hk], veps[:, hk], c["powm"][:, 0:CT], ALU.pow).then_inc(rstd_ready, 1)
                if not (isinstance(k, int) and k == 0):
                    scatter(k - 1, (h + 1) % 2)

            def scatter(k, hk):
                hold(pool, res_ready, k + 1)
                for t in range(CT):
                    pool.indirect_dma_start(out=out_rows, out_offset=bass.IndirectOffsetOnAxis(ap=dest[:, hk, t:t + 1], axis=0),
                                            in_=res[:, hk, t], in_offset=None, bounds_check=T - 1,
                                            oob_is_err=False).then_inc(scattered[hk], 16)

            def after():
                scatter(NCH - 1, 1)
                for h in range(2):
                    hold(pool, scattered[h], 16 * CT * NCH // 2)
            steps(pool, before, step, after)


def kernel(**inputs):
    import numpy as np
    import concourse.bacc as bacc
    from concourse.bass_utils import run_bass_kernel_spmd

    a = {k.removeprefix("L0_attn_").removeprefix("L0_ffn_"): np.asarray(v) for k, v in inputs.items()}
    f32 = np.float32

    def both(g, l, axis=1):
        return np.ascontiguousarray(np.stack([g, l], axis=axis))

    def head_order(w):
        return w.reshape(2, 2, 4, DH, D).transpose(0, 2, 1, 3, 4).reshape(D, D)

    def spread(v):
        return np.ascontiguousarray(np.broadcast_to(v, (P,) + v.shape))

    blk = np.arange(S) // LW
    same = blk[None, :] == np.arange(NBLK)[:, None]
    arrays = {
        "x": a["x"],
        "wqkv": both(a["wg_in"].T, a["wl_in"].T),
        "bqk": both(a["bg_in"][:2 * D].reshape(2, D).T, a["bl_in"][:2 * D].reshape(2, D).T),
        "bv_row": spread(np.stack([a["bg_in"][2 * D:], a["bl_in"][2 * D:]])),
        "ln_cols": np.stack([a["ln_g_g"], a["ln_g_b"], a["ln_l_g"], a["ln_l_b"]], axis=1),
        "wo": both(head_order(a["wg_out"].T), head_order(a["wl_out"].T)),
        "bo_row": spread(np.stack([a["bg_out"], a["bl_out"]])),
        "wg": a["Wg"],
        "w1": a["W1"],
        "b1": a["b1"].reshape(E, FT, P).transpose(0, 2, 1),
        "w2": a["W2"],
        "b2": a["b2"],
        "eye_in": np.eye(P, dtype=f32),
        "tri_in": np.triu(np.ones((P, P), f32)),
        "blockq_in": same.astype(f32),
        "blockk_in": np.where(same, f32(0), f32(-2.0 ** 100)),
        "tokid_in": (np.arange(P)[:, None] + P * np.arange(2)[None, :]).astype(f32),
        "slot_in": spread(np.broadcast_to(CAP * np.arange(E) - 1, (2, E)).astype(f32)),
        "prio_in": spread(np.broadcast_to(E - np.arange(E), (2, E)).astype(f32)),
    }
    arrays = {k: np.ascontiguousarray(v) for k, v in arrays.items()}
    nc = bacc.Bacc("TRN2", target_bir_lowering=False, num_devices=1)
    aps = {k: nc.dram_tensor(k, v.shape, mybir.dt.from_np(v.dtype), kind="ExternalInput").ap() for k, v in arrays.items()}
    out = nc.dram_tensor("out", (B, S, D), F32, kind="ExternalOutput").ap()
    build(nc, out=out, **aps)
    result = run_bass_kernel_spmd(nc, [arrays], core_ids=[0])
    return result.results[0]["out"]
```

```python
from contextlib import ExitStack

import concourse.bass as bass
from concourse import mybir

F32 = mybir.dt.float32
BF16 = mybir.dt.bfloat16
U32 = mybir.dt.uint32
ALU = mybir.AluOpType
ACT = mybir.ActivationFunctionType
AX = mybir.AxisListType.X

P = 128
B, S, D = 32, 256, 128
T = B * S
NH, DH = 16, 8
SCALE = DH ** -0.5
LW = 32
EPS = 1e-5
PAIR = 2 * S
NPAIR = T // PAIR
LPAIR = B * LW // PAIR
TERMS = 6
STACK = TERMS * DH
MASKROW = STACK
NBLK = S // LW
MAXROW = 96
KMAX = MAXROW
KEXP = MAXROW + 3
E, F = 8, 512
FT = F // P
CAP = T // E
ROW = D + 2
NB = 6
TWO_MINUS_ONES = -(1 + 0xBF80 / 2 ** 23)
NOWHERE = float(2 * T)
CH = 512
NCH = T // CH
CT = CH // P


def wait(eng, sem, value):
    if isinstance(value, int) and value <= 0:
        return
    eng.wait_ge(sem, value)


def hold(eng, sem, value):
    if isinstance(value, int) and value <= 0:
        return
    eng.wait_ge(sem, value)
    if not isinstance(value, int):
        eng.nop(nofuse=True)


class Chain:

    def __init__(self, sem, steps):
        self.sem, self.steps, self.base, self.k = sem, steps, 0, 0

    def start(self, n):
        self.base, self.k = n * self.steps, 0

    def link(self, eng, ins):
        ins.then_inc(self.sem, 1)
        self.k += 1
        hold(eng, self.sem, self.base + self.k)

    def end(self):
        assert self.k == self.steps, (self.k, self.steps)


def stepped(eng, steps, body):
    body(0, True, steps == 1)
    if steps > 2:
        with eng.Fori(1, steps - 1) as i:
            body(i, False, False)
    if steps > 1:
        body(steps - 1, False, True)


class Step:

    def __init__(self, i, j, unroll):
        self.i, self.j, self.unroll = i, j, unroll
        self.n = unroll * i + j

    def mod(self, k):
        return self.j % k

    def plus(self, k):
        return Step(self.i, self.j + k, self.unroll)

    def div(self, k):
        return (self.unroll // k) * self.i + self.j // k if not isinstance(self.i, int) else self.n // k


def pipelined(eng, stages, unroll, loop_from, loop_to, ahead):
    def step(i, j):
        for offset, count, stage in stages:
            u = Step(i, j + offset, unroll)
            if 0 <= u.n < count if isinstance(i, int) else count > 1:
                stage(u)
    for s in range(-ahead, loop_from):
        step(0, s)
    with eng.Fori(loop_from // unroll, loop_to // unroll) as i:
        for j in range(unroll):
            step(i, j)
    for s in range(loop_to, max(count - offset for offset, count, _ in stages)):
        step(0, s)


def rows(ap, start, count):
    return ap[bass.ds(start, count)]


def fetch_stack(sp, h, u, half):
    b = u.mod(2)
    for dst, stack in ((h["qs"], h["q_stack"]), (h["ks"], h["k_stack"])):
        src = rows(stack, u.div(2), 1)[0, 64 * half:64 * half + 64, :, b * S:(b + 1) * S]
        sp.dma_start(dst[0:STACK, b, 8 * half:8 * half + 8, :],
                     src.rearrange("(g d) t n -> (d t) g n", d=DH)).then_inc(h["stack_loaded"][b][half], 16)


def fetch_v(sp, h, u):
    sp.dma_start(h["vc"][:, u.mod(2)],
                 rows(h["v_rows"], u.n, 1).rearrange("o (k p) d -> p (o k) d", p=P)).then_inc(h["v_loaded"][u.mod(2)], 16)


def build(nc, x, wqkv, bqk, bv_row, ln_cols, wo, bo_row, wg, w1, b1, w2, b2,
          eye_in, tri_in, blockq_in, blockk_in, tokid_in, slot_in, prio_in, out):
    ctx = ExitStack()
    with ctx:
        def sb(name, shape, dt=F32):
            return ctx.enter_context(nc.sbuf_tensor(name, shape, dt))

        ident = sb("ident", [P, P])
        ident_bf = sb("ident_bf", [P, P], BF16)
        tri = sb("tri", [P, P])
        ones = sb("ones", [P, P])
        wqkv_sb = sb("wqkv_sb", [P, 2, 3 * D])
        bqk_sb = sb("bqk_sb", [P, 2, 2])
        bv_sb = sb("bv_sb", [P, 2, D])
        ln_sb = sb("ln_sb", [P, 4])
        wo_sb = sb("wo_sb", [P, 2, D])
        bo_sb = sb("bo_sb", [P, 2, D])
        wg_sb = sb("wg_sb", [P, E])
        powm = sb("powm", [P, 8])
        tokid = sb("tokid", [P, 2])
        slot0 = sb("slot0", [P, 2, E])
        prio = sb("prio", [P, 2, E])
        base = sb("base", [P, 2, E])
        empty = sb("empty", [P, ROW])

        q_stack = nc.dram_tensor("q_stack", [NPAIR + LPAIR, P, TERMS, PAIR], BF16, kind="Internal").ap()
        k_stack = nc.dram_tensor("k_stack", [NPAIR + LPAIR, P, TERMS, PAIR], BF16, kind="Internal").ap()
        v_rows = nc.dram_tensor("v_rows", [(NPAIR + LPAIR) * 2, S, D], F32, kind="Internal").ap()
        x_local = nc.dram_tensor("x_local", [B, LW, D], F32, kind="Internal").ap()
        routed = nc.dram_tensor("routed", [T, ROW], F32, kind="Internal").ap()

        c = dict(ident=ident, ident_bf=ident_bf, tri=tri, ones=ones, wqkv=wqkv_sb, bqk=bqk_sb, bv=bv_sb,
                 ln=ln_sb, wo=wo_sb, bo=bo_sb, wg=wg_sb, powm=powm, tokid=tokid, slot0=slot0, prio=prio,
                 base=base, empty=empty)
        with ExitStack() as shared:
            h = dict(
                qs=shared.enter_context(nc.sbuf_tensor("qs", [P, 2, NH, S], BF16)),
                ks=shared.enter_context(nc.sbuf_tensor("ks", [P, 2, NH, S], BF16)),
                vp=shared.enter_context(nc.sbuf_tensor("vp", [P, 2, 2, NH, 32], F32)),
                vc=shared.enter_context(nc.sbuf_tensor("vc", [P, 2, 2, D], F32)),
                part=shared.enter_context(nc.sbuf_tensor("part", [P, NB, 2, 3, PAIR], BF16)),
                v_sb=shared.enter_context(nc.sbuf_tensor("v_sb", [P, NB, 4, D], F32)),
                stack_stored=[shared.enter_context(nc.semaphore(f"stack_stored{b}")) for b in range(NB)],
                v_stored=[shared.enter_context(nc.semaphore(f"v_stored{b}")) for b in range(NB)],
                stack_loaded=[[shared.enter_context(nc.semaphore(f"stack_loaded{b}{f}")) for f in range(2)] for b in range(2)],
                v_loaded=[shared.enter_context(nc.semaphore(f"v_loaded{b}")) for b in range(2)],
                q_stack=q_stack, k_stack=k_stack, v_rows=v_rows)
            front(nc, c, h, x,
                  dict(ident=eye_in, tri=tri_in, wqkv=wqkv, bqk=bqk, bv=bv_row, ln=ln_cols, wo=wo, bo=bo_row,
                       wg=wg, tokid=tokid_in, slot0=slot_in, prio=prio_in), blockq_in, blockk_in)
            attend(nc, c, h, x, x_local, routed, out)
        experts(nc, c, w1, b1, w2, b2, routed, out)


def front(nc, c, handed, x, given, blockq_in, blockk_in):
    x_t = x.rearrange("b (h p) d -> (b h) p d", p=P)
    qs, ks, vp, part, v_sb = (handed[k] for k in ("qs", "ks", "vp", "part", "v_sb"))
    q_stack, k_stack, v_rows = (handed[k] for k in ("q_stack", "k_stack", "v_rows"))
    stack_stored, v_stored = handed["stack_stored"], handed["v_stored"]
    v_t = v_rows.rearrange("u (h p) d -> (u h) p d", p=P)
    ctx = ExitStack()
    with ctx:
        def sb(name, shape, dt=F32):
            return ctx.enter_context(nc.sbuf_tensor(name, shape, dt))

        def sem(name):
            return ctx.enter_context(nc.semaphore(name))

        xt = sb("xt", [P, NB, 4, D])
        stats = sb("stats", [P, 2, 4, 6])
        mv = sb("mv", [P, NB, 4, 2])
        veps = sb("veps", [P, 2, 4])
        rstd = sb("rstd", [P, 2, 4])
        xh = sb("xh", [P, 2, 4, D])
        xg = sb("xg", [P, 2, PAIR])
        full = sb("full", [P, 2, 2, PAIR])
        rest = sb("rest", [P, 2, 2, PAIR])
        bq_scaled = sb("bq_scaled", [P, 2])
        block_q = sb("block_q", [NBLK, S])
        block_k = sb("block_k", [NBLK, S])
        block_qb = sb("block_qb", [NBLK, S], BF16)
        block_kb = sb("block_kb", [NBLK, S], BF16)
        ps_x = ctx.enter_context(nc.psum_tensor("ps_x", [P, 2, PAIR], F32))
        ps_q = ctx.enter_context(nc.psum_tensor("ps_q", [P, 2, PAIR], F32))
        ps_k = ctx.enter_context(nc.psum_tensor("ps_k", [P, 2, PAIR], F32))
        ps_v = ctx.enter_context(nc.psum_tensor("ps_v", [P, 2, PAIR], F32))

        const_loaded = sem("const_loaded")
        stacks_cleared = sem("stacks_cleared")
        v_cleared = sem("v_cleared")
        mask_loaded = sem("mask_loaded")
        mask_cast = sem("mask_cast")
        mask_placed = sem("mask_placed")
        x_loaded = [sem(f"x_loaded{b}") for b in range(NB)]
        bias_scaled = sem("bias_scaled")
        stats_done = sem("stats_done")
        stats_ready = sem("stats_ready")
        norm_chain = Chain(sem("front_norm_chain"), 1)
        pow_set = sem("pow_set")
        rstd_ready = sem("rstd_ready")
        xh_ready = sem("xh_ready")
        xT_ready = sem("xT_ready")
        xg_ready = sem("xg_ready")
        qk_projected = sem("qk_projected")
        v_projected = sem("v_projected")
        full_ready = sem("full_ready")
        v_ready = sem("v_ready")
        part1_ready = sem("part1_ready")
        rest_ready = sem("rest_ready")
        part2_ready = sem("part2_ready")
        part3_ready = sem("part3_ready")
        block = ctx.enter_context(nc.Block())
        NCONST = len(given)

        LAST = NPAIR + LPAIR

        def run(eng, stages):
            pipelined(eng, stages, unroll=NB, loop_from=NB, loop_to=2 * NB, ahead=NB)

        def kind(u):
            return 1 if isinstance(u.n, int) and u.n < LPAIR else 0

        @block.sync
        def _(sp):
            def load_constants(u):
                for name, src in given.items():
                    sp.dma_start(c[name][:], src).then_inc(const_loaded, 16)
                sp.dma_start(block_q[:], blockq_in).then_inc(mask_loaded, 16)
                sp.dma_start(block_k[:], blockk_in).then_inc(mask_loaded, 16)

            def load(u):
                wait(sp, xh_ready, u.n - NB + 1)
                b = u.mod(NB)
                if kind(u):
                    for t in range(4):
                        n = 4 * (4 * u.n + t)
                        sp.dma_start(xt[:, b, t], x[n:n + 4, 0:LW, :]).then_inc(x_loaded[b], 16)
                else:
                    sp.dma_start(xt[:, b], rows(x_t, 4 * u.n - 4 * LPAIR, 4).rearrange("t p d -> p t d")).then_inc(x_loaded[b], 16)

            def store(u):
                b = u.mod(NB)
                sp.wait_ge(v_ready, u.n + 1)
                sp.dma_start(rows(v_t, 4 * u.n, 4).rearrange("t p d -> p t d"), v_sb[:, b]).then_inc(v_stored[b], 16)
                sp.wait_ge(part3_ready, u.n + 1)
                for s, stack in enumerate((q_stack, k_stack)):
                    dst = rows(stack, u.n, 1).rearrange("o r t n -> (o r) t n")
                    for k, (t0, n) in enumerate(((0, 3), (3, 2), (5, 1))):
                        if s == 0:
                            src = part[:, b, 0, k:k + 1, :].to_broadcast([P, n, PAIR])
                        else:
                            src = part[:, b, 1, 0:n, :]
                        sp.dma_start(dst[:, t0:t0 + n, :], src).then_inc(stack_stored[b], 16)

            def place_mask(u):
                sp.wait_ge(stacks_cleared, 3)
                sp.wait_ge(mask_cast, 2)
                for h in range(2):
                    for dst, src in ((qs, block_qb), (ks, block_kb)):
                        sp.dma_start(dst[MASKROW:MASKROW + NBLK, h],
                                     src[:].unsqueeze(1).to_broadcast([NBLK, NH, S])).then_inc(mask_placed, 16)

            def first_units(u):
                sp.wait_ge(stack_stored[0], 16 * 6)
                sp.wait_ge(v_stored[0], 16)
                for n in range(2):
                    first = Step(0, n, 2)
                    fetch_stack(sp, handed, first, 0)
                    fetch_stack(sp, handed, first, 1)
                    fetch_v(sp, handed, first)

            run(sp, [(NB - 1, LAST, load), (NB - 2, 1, load_constants), (-1, LAST, store), (1 - NB, 1, place_mask), (-2 * NB - 1, 1, first_units)])
            sp.wait_ge(mask_placed, 64)

        @block.vector
        def _(dve):
            nc.vector.memset(c["powm"][:], -0.5).then_inc(pow_set, 1)
            nc.vector.memset(c["ones"][:], 1.0)
            nc.vector.memset(c["base"][:], 0.0)
            nc.vector.memset(c["empty"][:, 0:D + 1], 0.0)
            nc.vector.memset(c["empty"][:, D + 1:ROW], NOWHERE)
            nc.vector.memset(qs[:].bitcast(U32), 0).then_inc(stacks_cleared, 1)

            def cast_constants(u):
                dve.wait_ge(const_loaded, 16 * NCONST)
                nc.vector.tensor_scalar(bq_scaled[:], c["bqk"][:, :, 0], SCALE, None, ALU.mult).then_inc(bias_scaled, 1)
                nc.vector.tensor_copy(c["ident_bf"][:], c["ident"][:])
                dve.wait_ge(mask_loaded, 32)
                nc.vector.tensor_copy(block_qb[:], block_q[:]).then_inc(mask_cast, 1)
                nc.vector.tensor_copy(block_kb[:], block_k[:]).then_inc(mask_cast, 1)

            def statistics(u):
                b = u.mod(NB)
                dve.wait_ge(x_loaded[b], 16 * (u.div(NB) + (4 if b < LPAIR else 1)))
                for t in range(4):
                    last = nc.vector.bn_stats(stats[:, u.mod(2), t], xt[:, b, t])
                last.then_inc(stats_done, 1)
                hold(dve, stats_done, u.n + 1)
                for t in range(4):
                    last = nc.vector.bn_aggr(mv[:, b, t], stats[:, u.mod(2), t])
                last.then_inc(stats_ready, 1)

            def normalize(u):
                dve.wait_ge(rstd_ready, u.n + 1)
                hold(dve, xT_ready, u.n - 1)
                for t in range(4):
                    last = nc.vector.tensor_scalar(xh[:, u.mod(2), t], xt[:, u.mod(NB), t], mv[:, u.mod(NB), t, 0:1],
                                                   rstd[:, u.mod(2), t:t + 1], ALU.subtract, ALU.mult)
                last.then_inc(xh_ready, 1)

            def take_v(u):
                k, h = kind(u), u.mod(2)
                dve.wait_ge(v_projected, u.n + 1)
                wait(dve, v_stored[u.mod(NB)], 16 * u.div(NB))
                nc.vector.tensor_tensor(v_sb[:, u.mod(NB)], ps_v[:, h].rearrange("p (t d) -> p t d", t=4),
                                        c["bv"][:, k].unsqueeze(1).to_broadcast([P, 4, D]),
                                        ALU.add).then_inc(v_ready, 1)

            def take_rest(u):
                h = u.mod(2)
                dve.wait_ge(part1_ready, u.n + 1)
                wait(dve, part3_ready, u.n - 1)
                nc.vector.tensor_tensor(rest[:, h], full[:, h], part[:, u.mod(NB), :, 0],
                                        ALU.subtract).then_inc(rest_ready, 1)
            run(dve, [(0, LAST, take_v), (4, LAST, statistics), (2, 1, cast_constants), (3, LAST, normalize), (0, LAST, take_rest)])

        @block.gpsimd
        def _(pool):
            nc.gpsimd.memset(ks[:].bitcast(U32), 0).then_inc(stacks_cleared, 1)
            nc.gpsimd.memset(vp[:], 0.0).then_inc(v_cleared, 1)
            pool.wait_ge(stacks_cleared, 2)
            pool.wait_ge(v_cleared, 1)
            for g in range(2):
                dst = vp[:].rearrange("p c k (u g j) w -> p (c k u) g j w", g=2, j=4)
                nc.gpsimd.memset(dst[:, :, g, :, 16 * g + DH:16 * g + DH + 1], 1.0).then_inc(v_cleared, 1)
            pool.wait_ge(v_cleared, 3)
            nc.gpsimd.memset(ks[MAXROW:KEXP].bitcast(F32), TWO_MINUS_ONES).then_inc(stacks_cleared, 1)
            pool.wait_ge(stacks_cleared, 3)
            pool.wait_ge(pow_set, 1)

            def deviation(u):
                hold(pool, stats_ready, u.n + 1)
                hold(pool, xh_ready, u.n - 1)
                norm_chain.start(u.n)
                norm_chain.link(pool, nc.gpsimd.tensor_scalar(veps[:, u.mod(2)], mv[:, u.mod(NB), :, 1], EPS, None, ALU.add))
                nc.gpsimd.tensor_tensor(rstd[:, u.mod(2)], veps[:, u.mod(2)], c["powm"][:, 0:4],
                                        ALU.pow).then_inc(rstd_ready, 1)
                norm_chain.end()

            def third_part(u):
                hold(pool, part2_ready, u.n + 1)
                p = part[:, u.mod(NB)]
                nc.gpsimd.tensor_tensor(p[:, :, 2], rest[:, u.mod(2)], p[:, :, 1], ALU.subtract).then_inc(part3_ready, 1)
            run(pool, [(-1, LAST, third_part), (4, LAST, deviation)])

        @block.scalar
        def _(act):
            act.wait_ge(const_loaded, 16 * NCONST)
            act.wait_ge(bias_scaled, 1)

            def scale_shift(u):
                h = u.mod(2)
                act.wait_ge(xT_ready, u.n + 1)
                wait(act, v_projected, u.n - 1)
                k = 2 * kind(u)
                nc.scalar.activation(xg[:, h], ps_x[:, h], ACT.Identity, scale=c["ln"][:, k:k + 1],
                                     bias=c["ln"][:, k + 1:k + 2]).then_inc(xg_ready, 1)

            def take_projections(u):
                k, h = kind(u), u.mod(2)
                act.wait_ge(qk_projected, u.n + 1)
                wait(act, rest_ready, u.n - 1)
                nc.scalar.activation(full[:, h, 0], ps_q[:, h], ACT.Identity, scale=SCALE, bias=bq_scaled[:, k:k + 1])
                nc.scalar.activation(full[:, h, 1], ps_k[:, h], ACT.Identity, bias=c["bqk"][:, k, 1:2]).then_inc(full_ready, 1)

            def first_part(u):
                act.wait_ge(full_ready, u.n + 1)
                wait(act, stack_stored[u.mod(NB)], 16 * 6 * u.div(NB))
                nc.scalar.copy(part[:, u.mod(NB), :, 0], full[:, u.mod(2)]).then_inc(part1_ready, 1)

            def second_part(u):
                act.wait_ge(rest_ready, u.n + 1)
                nc.scalar.copy(part[:, u.mod(NB), :, 1], rest[:, u.mod(2)]).then_inc(part2_ready, 1)
            run(act, [(1, LAST, take_projections), (1, LAST, first_part), (2, LAST, scale_shift), (0, LAST, second_part)])

        @block.tensor
        def _(pe):
            pe.wait_ge(const_loaded, 16 * NCONST)

            def turn(u):
                pe.wait_ge(xh_ready, u.n + 1)
                wait(pe, xg_ready, u.n - 1)
                for t in range(4):
                    last = nc.tensor.transpose(ps_x[:, u.mod(2), t * P:(t + 1) * P], xh[:, u.mod(2), t], c["ident"][:])
                last.then_inc(xT_ready, 1)

            def project(u):
                k, h = kind(u), u.mod(2)
                w = c["wqkv"][:, k]
                pe.wait_ge(xg_ready, u.n + 1)
                src = xg[:, h]
                wait(pe, full_ready, u.n - 1)
                nc.tensor.matmul(ps_q[:, h], w[:, 0:D], src, start=True, stop=True)
                nc.tensor.matmul(ps_k[:, h], w[:, D:2 * D], src, start=True, stop=True).then_inc(qk_projected, 1)
                wait(pe, v_ready, u.n - 1)
                for t in range(4):
                    last = nc.tensor.matmul(ps_v[:, h, t * D:(t + 1) * D], src[:, t * P:(t + 1) * P],
                                            w[:, 2 * D:3 * D], start=True, stop=True)
                last.then_inc(v_projected, 1)
            run(pe, [(2, LAST, turn), (1, LAST, project)])


def attend(nc, c, handed, x, x_local, routed, out):
    qs, ks, vp, vc = (handed[k] for k in ("qs", "ks", "vp", "vc"))
    stack_stored, v_stored, stack_loaded, v_loaded = (
        handed[k] for k in ("stack_stored", "v_stored", "stack_loaded", "v_loaded"))
    LU = B * LW // S
    U = LU + B
    LOOP = LU + 4
    ctx = ExitStack()
    with ctx:
        def sb(name, shape, dt=F32):
            return ctx.enter_context(nc.sbuf_tensor(f"a_{name}", shape, dt))

        def sem(name):
            return ctx.enter_context(nc.semaphore(f"a_{name}"))

        prob = sb("prob", [P, 8, 2 * 2 * S])
        mx = sb("mx", [P, 2, 2, NH])
        mrest = sb("mrest", [P, 2, 2, 8])
        mpart = sb("mpart", [P, 2, 2, 3, 8], BF16)
        mT = sb("mT", [24, 2, S], BF16)
        oT = sb("oT", [P, 2 * S])
        rden = sb("rden", [P, 4, 8])
        oN = sb("oN", [P, 2, D])
        oNT = sb("oNT", [P, S])
        xr = sb("xr", [P, 2, 2, D])
        y = sb("y", [P, 2, 2, D])
        stats = sb("stats", [P, 2, 6])
        mv = sb("mv", [P, 2, 2])
        veps = sb("veps", [P, 2, 2])
        rstd = sb("rstd", [P, 2, 2])
        scale2 = sb("scale2", [P, 2])
        row = sb("row", [P, 2, 2, ROW])
        x1T = sb("x1T", [P, S])
        o1 = sb("o1", [P, 2, D])
        lmax = sb("lmax", [P, 2])
        shifted = sb("shifted", [P, 2, E])
        gexp = sb("gexp", [P, 2, E])
        gsum = sb("gsum", [P, 2])
        pri = sb("pri", [P, 2, E])
        pmax = sb("pmax", [P, 2])
        mask = sb("mask", [P, 2, E])
        count = sb("count", [P, 2, 2, E])
        loc = sb("loc", [P, 2, E])
        locslot = sb("locslot", [P, 2, 2, E])
        picked = sb("picked", [P, 2, 2])
        over = sb("over", [P, 2])
        slot = sb("slot", [P, 2], U32)
        ps_b = ctx.enter_context(nc.psum_tensor("a_ps_b", [P, 4, 2 * S], F32))
        ps_a = ctx.enter_context(nc.psum_tensor("a_ps_a", [P, 2, 2 * S], F32))
        ps_o = ctx.enter_context(nc.psum_tensor("a_ps_o", [P, 2 * S], F32))
        ps_m = ctx.enter_context(nc.psum_tensor("a_ps_m", [P, 2 * S], F32))
        ps_m_bf = ps_m[:].bitcast(BF16)

        xr_loaded = [sem("xr_loaded0"), sem("xr_loaded1")]
        routed_cleared = sem("routed_cleared")
        max_scores = sem("max_scores")
        max_done = sem("max_done")
        max_split = sem("max_split")
        max_turned = sem("max_turned")
        mT_ready = sem("mT_ready")
        max_rows = [sem("max_rows0"), sem("max_rows1")]
        v_spread = sem("v_spread")
        scores = sem("scores")
        exp_done = sem("exp_done")
        pv_done = sem("pv_done")
        oT_ready = sem("oT_ready")
        o_turned = sem("o_turned")
        o_normed = sem("o_normed")
        oN_turned = sem("oN_turned")
        oNT_ready = sem("oNT_ready")
        projected = sem("projected")
        xr_ready = sem("xr_ready")
        y_ready = sem("y_ready")
        y_stored = [sem("y_stored0"), sem("y_stored1")]
        split_chain = Chain(sem("split_chain"), 3)
        rden_ready = sem("rden_ready")
        stats_taken = sem("stats_taken")
        stats_ready = sem("stats_ready")
        dev_chain = Chain(sem("dev_chain"), 2)
        rstd_ready = sem("rstd_ready")
        rstd2_ready = sem("rstd2_ready")
        x1_ready = sem("x1_ready")
        row_numbered = sem("row_numbered")
        tok_moved = sem("tok_moved")
        o1_ready = sem("o1_ready")
        o1_stored = sem("o1_stored")
        x1_turned = sem("x1_turned")
        x1T_ready = sem("x1T_ready")
        logits_ready = sem("logits_ready")
        logits_read = sem("logits_read")
        gexp_ready = sem("gexp_ready")
        mask_ready = sem("mask_ready")
        gate_ready = sem("gate_ready")
        counted = sem("counted")
        counts_copied = sem("counts_copied")
        lmax_ready = sem("lmax_ready")
        pri_ready = sem("pri_ready")
        pmax_ready = sem("pmax_ready")
        gsum_ready = sem("gsum_ready")
        place_chain = Chain(sem("place_chain"), 4)
        places_ready = sem("places_ready")
        picked_ready = sem("picked_ready")
        over_ready = sem("over_ready")
        slot_ready = sem("slot_ready")
        scattered = [sem("scattered0"), sem("scattered1")]
        block = ctx.enter_context(nc.Block())

        def there(u):
            return not isinstance(u.n, int) or 0 <= u.n < U

        def is_local(u):
            return isinstance(u.n, int) and u.n < LU

        def routes(u):
            return there(u) and not is_local(u)

        def run(eng, unit):
            pipelined(eng, [(0, U + 3, unit)], unroll=2, loop_from=LOOP, loop_to=U - 2, ahead=0)

        def batch(u):
            return Step(u.i, u.j - LU, 2)

        @block.sync
        def _(sp):
            def load_stack(u, half):
                h = u.mod(2)
                wait(sp, scores, 8 * (u.n - 2) + 4 * half + 4)
                if isinstance(u.n, int) and u.n < LOOP:
                    sp.wait_ge(stack_stored[u.n // 2 % NB], 16 * 6 * (u.n // 2 // NB + 1))
                if isinstance(u.n, int) and u.n in (LU, LU + 1):
                    for dst in (qs, ks):
                        heads = dst[:, h, 8 * half:8 * half + 8, :]
                        sp.dma_start(heads[MASKROW:MASKROW + NBLK],
                                     heads[MASKROW + NBLK:MASKROW + 2 * NBLK]).then_inc(stack_loaded[h][half], 16)
                fetch_stack(sp, handed, u, half)

            def load_v(u):
                wait(sp, v_spread, u.n - 1)
                if isinstance(u.n, int) and u.n < LOOP:
                    sp.wait_ge(v_stored[u.n // 2 % NB], 16 * (u.n // 2 // NB + 1))
                fetch_v(sp, handed, u)

            def load_xr(u):
                h = u.mod(2)
                wait(sp, y_ready, u.n - 1)
                if is_local(u):
                    for t in range(2):
                        sp.dma_start(xr[:, h, t], x[8 * u.n + 4 * t:8 * u.n + 4 * t + 4, 0:LW, :]).then_inc(xr_loaded[h], 16)
                    return
                if isinstance(u.n, int) and u.n == LU:
                    sp.wait_ge(y_stored[0], 32)
                if isinstance(u.n, int) and u.n == LU + 3:
                    sp.wait_ge(y_stored[0], 64)
                    sp.wait_ge(y_stored[1], 64)
                at = batch(u).n
                sp.dma_start(xr[0:LW, h, 0], rows(x_local, at, 1).rearrange("o s d -> (o s) d")).then_inc(xr_loaded[h], 16)
                sp.dma_start(xr[LW:P, h, 0], rows(x, at, 1)[0, LW:P, :]).then_inc(xr_loaded[h], 16)
                sp.dma_start(xr[:, h, 1], rows(x, at, 1)[0, P:S, :]).then_inc(xr_loaded[h], 16)

            def place_max(u, half):
                sp.wait_ge(mT_ready, 2 * u.n + half + 1)
                sp.dma_start(qs[MAXROW:KEXP, u.mod(2), 8 * half:8 * half + 8, :], mT[:, half, :]).then_inc(max_rows[half], 16)

            def store_y(u):
                sp.wait_ge(y_ready, u.n + 1)
                for t in range(2):
                    sp.dma_start(x_local[8 * u.n + 4 * t:8 * u.n + 4 * t + 4],
                                 y[:, u.mod(2), t]).then_inc(y_stored[u.mod(2)], 16)

            def clear_routed(u):
                for k in range(2):
                    first = (2 * (u.n - LU + 1) + k) * (T // 8)
                    sp.dma_start(routed[first:first + T // 8].rearrange("(t p) r -> p t r", p=P),
                                 c["empty"][:].unsqueeze(1).to_broadcast([P, T // P // 8, ROW])).then_inc(routed_cleared, 16)

            def store_o1(u):
                g = batch(u)
                sp.wait_ge(o1_ready, g.n + 1)
                sp.dma_start(rows(out, g.n, 1).rearrange("o (t p) d -> p (o t) d", p=P), o1[:]).then_inc(o1_stored, 16)

            def unit(u):
                after1, after2, before2, before3 = u.plus(1), u.plus(2), u.plus(-2), u.plus(-3)
                if isinstance(u.n, int) and u.n == 0:
                    place_max(u, 0)
                if there(after1) and not (isinstance(u.n, int) and u.n == 0):
                    load_stack(after1, 1)
                    load_v(after1)
                if there(u):
                    load_xr(u)
                if routes(before3):
                    store_o1(before3)
                if is_local(before2) and there(before2):
                    store_y(before2)
                if there(u):
                    place_max(u, 1)
                if there(after2):
                    load_stack(after2, 0)
                if there(after1):
                    place_max(after1, 0)
                if isinstance(u.n, int) and LU - 1 <= u.n < LU + 3:
                    clear_routed(u)
                if isinstance(u.n, int) and u.n == LOOP - 1:
                    for b in range(NB):
                        uses = len(range(b, NPAIR + LPAIR, NB))
                        sp.wait_ge(stack_stored[b], 16 * 6 * uses)
                        sp.wait_ge(v_stored[b], 16 * uses)
            run(sp, unit)
            sp.wait_ge(o1_stored, 16 * B)

        @block.tensor
        def _(pe):
            def max_pass(u, hp, qt):
                h = u.mod(2)
                if hp % 4 == 0 and qt == 0:
                    extra = 0 if isinstance(u.n, int) and u.n < LU else 32
                    pe.wait_ge(stack_loaded[h][hp // 4], 32 * (u.div(2) + 1) + extra)
                wait(pe, max_done, 16 * u.n + 2 * hp + qt - 1)
                keys = slice(qt * P, (qt + 1) * P) if is_local(u) else slice(0, S)
                for e in range(2):
                    last = nc.tensor.matmul(ps_a[:, qt, e * S:e * S + keys.stop - keys.start],
                                            qs[0:KMAX, h, 2 * hp + e, qt * P:(qt + 1) * P],
                                            ks[0:KMAX, h, 2 * hp + e, keys], start=True, stop=True)
                last.then_inc(max_scores, 1)

            def exp_pass(u, hp):
                if hp % 4 == 0:
                    pe.wait_ge(max_rows[hp // 4], 16 * (u.n + 1))
                wait(pe, exp_done, 8 * u.n + hp - 1)
                n = P if is_local(u) else S
                for e in range(2):
                    for kt in range(2):
                        queries = slice(kt * P, (kt + 1) * P) if is_local(u) else slice(0, S)
                        last = nc.tensor.matmul(ps_b[:, 2 * (hp % 2) + e, kt * n:(kt + 1) * n],
                                                ks[0:KEXP, u.mod(2), 2 * hp + e, kt * P:(kt + 1) * P],
                                                qs[0:KEXP, u.mod(2), 2 * hp + e, queries], start=True, stop=True)
                last.then_inc(scores, 1)

            def p_v(u, q, kt):
                if q == 0 and kt == 0:
                    wait(pe, oT_ready, u.n)
                    pe.wait_ge(v_spread, u.n + 1)
                if kt == 0:
                    pe.wait_ge(exp_done, 8 * u.n + 2 * q + 2)
                n = P if is_local(u) else S
                col = (q // 2) * S + (kt * P if is_local(u) else 0)
                for j in range(4):
                    at = (j % 2) * 2 * n + kt * n
                    last = nc.tensor.matmul(ps_o[32 * j:32 * j + 32, col:col + n],
                                            vp[:, u.mod(2), kt, 4 * q + j, :],
                                            prob[:, 2 * q + j // 2, at:at + n],
                                            start=(q % 2 == 0 and kt == 0), stop=(q % 2 == 1 and kt == 1))
                if kt == 1:
                    last.then_inc(pv_done, 1)

            def turn_max(u, half):
                pe.wait_ge(max_split, 2 * u.n + half + 1)
                for qt in range(2):
                    last = nc.tensor.transpose(ps_m_bf[0:24, qt * P:(qt + 1) * P],
                                               mpart[:, half, qt].rearrange("p a h -> p (a h)"), c["ident_bf"][:])
                last.then_inc(max_turned, 1)

            def turn_o(u):
                pe.wait_ge(oT_ready, u.n + 1)
                for qt in range(2):
                    for g in range(2):
                        last = nc.tensor.transpose(ps_m[:, (2 * qt + g) * P:(2 * qt + g + 1) * P],
                                                   oT[:, g * S + qt * P:g * S + (qt + 1) * P], c["ident"][:])
                last.then_inc(o_turned, 1)

            def turn_oN(u):
                for qt in range(2):
                    last = nc.tensor.transpose(ps_m[:, qt * P:(qt + 1) * P], oN[:, qt], c["ident"][:])
                last.then_inc(oN_turned, 1)

            def project(u):
                pe.wait_ge(oNT_ready, u.n + 1)
                for qt in range(2):
                    last = nc.tensor.matmul(ps_m[:, qt * D:(qt + 1) * D], oNT[:, qt * P:(qt + 1) * P],
                                            c["wo"][:, 1 if is_local(u) else 0], start=True, stop=True)
                last.then_inc(projected, 1)

            def turn_x1(u):
                g = batch(u)
                pe.wait_ge(x1_ready, 2 * g.n + 2)
                for qt in range(2):
                    last = nc.tensor.transpose(ps_m[:, S + qt * P:S + (qt + 1) * P], row[:, u.mod(2), qt, 0:D], c["ident"][:])
                last.then_inc(x1_turned, 1)

            def logits(u):
                pe.wait_ge(x1T_ready, batch(u).n + 1)
                for qt in range(2):
                    last = nc.tensor.matmul(ps_m[:, S + qt * E:S + (qt + 1) * E], x1T[:, qt * P:(qt + 1) * P],
                                            c["wg"][:], start=True, stop=True)
                last.then_inc(logits_ready, 1)

            def count_tokens(u):
                pe.wait_ge(mask_ready, batch(u).n + 1)
                m = mask[:].rearrange("p t e -> p (t e)")
                nc.tensor.matmul(ps_m[:, 0:2 * E], c["tri"][:], m, start=True, stop=True)
                nc.tensor.matmul(ps_m[:, 2 * E:4 * E], c["ones"][:], m, start=True, stop=True).then_inc(counted, 1)

            def unit(u):
                after1, before1, before2, before3 = u.plus(1), u.plus(-1), u.plus(-2), u.plus(-3)
                if isinstance(u.n, int) and u.n == 0:
                    for hp in range(8):
                        max_pass(u, hp, 0)
                        max_pass(u, hp, 1)
                        if hp == 6:
                            turn_max(u, 0)
                for hp in range(8):
                    if there(u):
                        exp_pass(u, hp)
                    if there(after1):
                        max_pass(after1, hp, 0)
                    if hp <= 2 and there(before1):
                        q, kt = divmod(hp + 5, 2)
                        p_v(before1, q, kt)
                    if hp >= 4 and there(u):
                        p_v(u, *divmod(hp - 3, 2))
                    if there(after1):
                        max_pass(after1, hp, 1)
                    if hp == 1 and there(u):
                        wait(pe, y_ready, u.n - 1)
                        if routes(before3):
                            pe.wait_ge(logits_read, batch(before3).n + 1)
                        turn_max(u, 1)
                    if hp == 2 and routes(before3):
                        if there(u):
                            pe.wait_ge(mT_ready, 2 * u.n + 2)
                        else:
                            pe.wait_ge(y_ready, min(u.n - 1, U))
                        count_tokens(before3)
                    if hp == 3 and there(before1):
                        if routes(before3):
                            pe.wait_ge(counts_copied, batch(before3).n + 1)
                        else:
                            pe.wait_ge(mT_ready, 2 * u.n + 2)
                        turn_o(before1)
                    if hp == 5 and there(after1):
                        if there(before1):
                            pe.wait_ge(o_normed, u.n)
                        else:
                            pe.wait_ge(mT_ready, 2 * u.n + 2)
                        turn_max(after1, 0)
                    if hp == 6:
                        if there(after1):
                            pe.wait_ge(mT_ready, 2 * u.n + 3)
                        elif routes(before3) and not there(before1):
                            pe.wait_ge(counts_copied, batch(before3).n + 1)
                        if there(before1):
                            pe.wait_ge(o_normed, u.n)
                        if routes(before2):
                            turn_x1(before2)
                        if there(before1):
                            turn_oN(before1)
                    if hp == 7:
                        if there(before1):
                            pe.wait_ge(oNT_ready, u.n)
                        if routes(before2):
                            logits(before2)
                        if there(before1):
                            project(before1)
                    if hp == 3 and there(u):
                        p_v(u, 0, 0)
            run(pe, unit)

        @block.scalar
        def _(act):
            def exponential(u, hp):
                act.wait_ge(scores, 8 * u.n + hp + 1)
                wait(act, pv_done, 4 * u.n + hp // 2 - 3)
                n = 2 * (P if is_local(u) else S)
                nc.scalar.activation(prob[:, hp, 0:2 * n].rearrange("p (a n) -> p a n", a=2),
                                     ps_b[:, 2 * (hp % 2):2 * (hp % 2) + 2, 0:n], ACT.Exp).then_inc(exp_done, 1)

            def copy_max(u, half):
                act.wait_ge(max_turned, 2 * u.n + half + 1)
                wait(act, max_rows[half], 16 * u.n)
                nc.scalar.copy(mT[:, half, :], ps_m_bf[0:24, 0:S]).then_inc(mT_ready, 1)

            def copy_o(u):
                act.wait_ge(pv_done, 4 * u.n + 4)
                wait(act, o_turned, u.n)
                nc.scalar.copy(oT[:], ps_o[:]).then_inc(oT_ready, 1)

            def copy_oNT(u):
                act.wait_ge(oN_turned, u.n + 1)
                wait(act, projected, u.n)
                nc.scalar.copy(oNT[:], ps_m[:, 0:S]).then_inc(oNT_ready, 1)

            def copy_x1T(u):
                g = batch(u)
                act.wait_ge(x1_turned, g.n + 1)
                wait(act, logits_ready, g.n)
                nc.scalar.copy(x1T[:], ps_m[:, S:2 * S]).then_inc(x1T_ready, 1)

            def norm_again(u):
                g = batch(u)
                act.wait_ge(x1_ready, 2 * g.n + 2)
                act.wait_ge(rstd2_ready, g.n + 1)
                wait(act, o1_stored, 16 * g.n)
                for t in range(2):
                    last = nc.scalar.activation(o1[:, t], row[:, u.mod(2), t, 0:D], ACT.Copy, scale=scale2[:, t:t + 1])
                last.then_inc(o1_ready, 1)

            def number_rows(u):
                g, h = batch(u), u.mod(2)
                wait(act, scattered[h], 32 * g.div(2))
                wait(act, tok_moved, g.n)
                nc.scalar.copy(row[:, h, :, D + 1], c["tokid"][:]).then_inc(row_numbered, 1)
                act.wait_ge(row_numbered, g.n + 1)
                nc.scalar.activation(c["tokid"][:], c["tokid"][:], ACT.Copy, bias=float(S)).then_inc(tok_moved, 1)

            def gate_exp(u):
                g = batch(u)
                act.wait_ge(logits_read, g.n + 1)
                wait(act, gate_ready, g.n)
                nc.scalar.activation(gexp[:], shifted[:], ACT.Exp).then_inc(gexp_ready, 1)

            def copy_counts(u):
                g = batch(u)
                act.wait_ge(counted, g.n + 1)
                wait(act, places_ready, g.n)
                nc.scalar.copy(count[:].rearrange("p a t e -> p (a t e)"), ps_m[:, 0:4 * E]).then_inc(counts_copied, 1)

            def unit(u):
                after1, before1, before2, before3 = u.plus(1), u.plus(-1), u.plus(-2), u.plus(-3)
                if isinstance(u.n, int) and u.n == 0:
                    copy_max(u, 0)
                for hp in range(8):
                    if there(u):
                        exponential(u, hp)
                    if hp == 1 and there(u):
                        copy_max(u, 1)
                    if hp == 2 and there(before1):
                        copy_o(before1)
                    if hp == 2 and routes(before3):
                        gate_exp(before3)
                        copy_counts(before3)
                    if hp == 5 and there(after1):
                        copy_max(after1, 0)
                    if hp == 6 and there(before1):
                        copy_oNT(before1)
                    if hp == 6 and routes(before2):
                        copy_x1T(before2)
                    if hp == 7 and routes(before2):
                        norm_again(before2)
                    if hp == 3 and routes(before2):
                        number_rows(before2)
            run(act, unit)

        @block.vector
        def _(dve):
            def take_max(u, hp, qt):
                dve.wait_ge(max_scores, 16 * u.n + 2 * hp + qt + 1)
                if qt == 0 and hp % 4 == 0:
                    wait(dve, max_split, 2 * u.n - 3 + hp // 4)
                k = P if is_local(u) else S
                nc.vector.reduce_max(mx[:, u.mod(2), qt, 2 * hp:2 * hp + 2],
                                     ps_a[:, qt].rearrange("p (e k) -> p e k", e=2)[:, :, 0:k], axis=AX).then_inc(max_done, 1)

            def add_residual(u):
                h, g = u.mod(2), batch(u)
                dve.wait_ge(projected, u.n + 1)
                if isinstance(u.n, int) and 2 <= u.n < LU + 2:
                    dve.wait_ge(y_stored[h], 32 * (u.n // 2))
                dve.wait_ge(xr_ready, u.n + 1)
                nc.vector.tensor_tensor(y[:, h], ps_m[:, 0:2 * D].rearrange("p (t d) -> p t d", t=2), xr[:, h],
                                        ALU.add).then_inc(y_ready, 1)

            def statistics(u):
                dve.wait_ge(y_ready, u.n + 1)
                for t in range(2):
                    last = nc.vector.bn_stats(stats[:, t], y[:, u.mod(2), t])
                last.then_inc(stats_taken, 1)

            def mean_variance(u):
                g = batch(u)
                hold(dve, stats_taken, g.n + 1)
                hold(dve, rstd2_ready, g.n)
                for t in range(2):
                    last = nc.vector.bn_aggr(mv[:, t], stats[:, t])
                last.then_inc(stats_ready, 1)

            def norm_row_tile(u, t):
                g, h = batch(u), u.mod(2)
                wait(dve, scattered[h], 32 * g.div(2))
                dve.wait_ge(rstd_ready, g.n + 1)
                nc.vector.tensor_scalar(row[:, h, t, 0:D], y[:, h, t], mv[:, t, 0:1], rstd[:, 0, t:t + 1],
                                        ALU.subtract, ALU.mult).then_inc(x1_ready, 1)

            def norm_rows0(u):
                norm_row_tile(u, 0)

            def norm_rows1(u):
                norm_row_tile(u, 1)

            turned = ps_m[:].rearrange("p (a g w) -> p a g w", a=4, w=16)

            def invert_denominators(u):
                dve.wait_ge(o_turned, u.n + 1)
                nc.vector.reciprocal(rden[:], turned[:, :, :, DH]).then_inc(rden_ready, 1)

            def norm_o(u):
                dve.wait_ge(rden_ready, u.n + 1)
                wait(dve, oN_turned, u.n)
                nc.vector.tensor_tensor(oN[:].rearrange("p t (g d) -> p (t g) d", d=DH).rearrange("p (a g) d -> p a g d", a=4),
                                        turned[:, :, :, 0:DH],
                                        rden[:].unsqueeze(3).to_broadcast([P, 4, 8, DH]), ALU.mult).then_inc(o_normed, 1)

            lg = ps_m[:, S:S + 2 * E].rearrange("p (t e) -> p t e", t=2)

            def logit_max(u):
                dve.wait_ge(logits_ready, batch(u).n + 1)
                nc.vector.reduce_max(lmax[:], lg, axis=AX).then_inc(lmax_ready, 1)

            def shift_logits(u):
                g = batch(u)
                dve.wait_ge(lmax_ready, g.n + 1)
                nc.vector.tensor_tensor(shifted[:], lg, lmax[:].unsqueeze(2).to_broadcast([P, 2, E]),
                                        ALU.subtract).then_inc(logits_read, 1)

            def priorities(u):
                dve.wait_ge(logits_read, batch(u).n + 1)
                nc.vector.scalar_tensor_tensor(out=pri[:], in0=shifted[:], scalar=0.0, in1=c["prio"][:],
                                               op0=ALU.is_ge, op1=ALU.mult).then_inc(pri_ready, 1)

            def top_priority(u):
                dve.wait_ge(pri_ready, batch(u).n + 1)
                nc.vector.reduce_max(pmax[:], pri[:], axis=AX).then_inc(pmax_ready, 1)

            def expert_mask(u):
                g = batch(u)
                dve.wait_ge(pmax_ready, g.n + 1)
                wait(dve, places_ready, g.n)
                nc.vector.tensor_tensor(mask[:], pri[:], pmax[:].unsqueeze(2).to_broadcast([P, 2, E]),
                                        ALU.is_equal).then_inc(mask_ready, 1)

            def gate_sum(u):
                dve.wait_ge(gexp_ready, batch(u).n + 1)
                nc.vector.reduce_sum(gsum[:], gexp[:], axis=AX).then_inc(gsum_ready, 1)

            def gate(u):
                dve.wait_ge(gsum_ready, batch(u).n + 1)
                nc.vector.reciprocal(row[:, u.mod(2), :, D], gsum[:]).then_inc(gate_ready, 1)

            def pick_place(u):
                dve.wait_ge(places_ready, batch(u).n + 1)
                nc.vector.reduce_sum(picked[:], locslot[:], axis=AX).then_inc(picked_ready, 1)

            def beyond_capacity(u):
                dve.wait_ge(picked_ready, batch(u).n + 1)
                nc.vector.tensor_scalar(over[:], picked[:, 0], CAP + 0.5, NOWHERE, ALU.is_gt,
                                        ALU.mult).then_inc(over_ready, 1)

            def pick_slot(u):
                g = batch(u)
                dve.wait_ge(over_ready, g.n + 1)
                before = g.plus(-1)
                wait(dve, scattered[before.mod(2)], 32 * (before.div(2) + 1))
                nc.vector.tensor_tensor(slot[:], picked[:, 1], over[:], ALU.add).then_inc(slot_ready, 1)

            FILL = {
                (0, 0): [(2, add_residual), (3, logit_max)],
                (0, 1): [(3, shift_logits), (2, statistics)],
                (1, 0): [(3, priorities), (2, mean_variance)],
                (1, 1): [(3, top_priority)],
                (2, 0): [(3, expert_mask)],
                (3, 0): [(3, gate_sum)],
                (3, 1): [(3, gate)],
                (4, 0): [(1, invert_denominators)],
                (4, 1): [(1, norm_o)],
                (5, 0): [(2, norm_rows0)],
                (5, 1): [(2, norm_rows1)],
                (6, 0): [(3, pick_place)],
                (6, 1): [(3, beyond_capacity)],
                (7, 0): [(3, pick_slot)],
            }
            FOR_ALL = (add_residual, invert_denominators, norm_o)

            def unit(u):
                after1 = u.plus(1)
                if isinstance(u.n, int) and u.n == 0:
                    for hp in range(8):
                        for qt in range(2):
                            take_max(u, hp, qt)
                for hp in range(8):
                    for qt in range(2):
                        for back, stage in FILL.get((hp, qt), ()):
                            v = u.plus(-back)
                            if there(v) if stage in FOR_ALL else routes(v):
                                stage(v)
                        if there(after1):
                            take_max(after1, hp, qt)
            run(dve, unit)

        @block.gpsimd
        def _(pool):
            def split_max(u, half):
                hold(pool, max_done, 16 * u.n + 8 * half + 8)
                hold(pool, max_turned, 2 * u.n + half - 1)
                src = mx[:, u.mod(2), :, 8 * half:8 * half + 8]
                r, part = mrest[:, half], mpart[:, half]
                split_chain.start(2 * u.n + half)
                split_chain.link(pool, nc.gpsimd.tensor_copy(part[:, :, 0], src))
                split_chain.link(pool, nc.gpsimd.tensor_tensor(r, src, part[:, :, 0], ALU.subtract))
                split_chain.link(pool, nc.gpsimd.tensor_copy(part[:, :, 1], r))
                split_chain.end()
                nc.gpsimd.tensor_tensor(part[:, :, 2], r, part[:, :, 1], ALU.subtract).then_inc(max_split, 1)

            def spread_v(u):
                h = u.mod(2)
                hold(pool, v_loaded[h], 16 * (u.div(2) + 1))
                hold(pool, pv_done, 4 * (u.n - 1))
                for g in range(2):
                    dst = vp[:, h].rearrange("p k (u g j) w -> p k u g j w", g=2, j=4)[:, :, :, g, :, 16 * g:16 * g + DH]
                    src = vc[:, h].rearrange("p k (u g j d) -> p k u g j d", g=2, j=4, d=DH)[:, :, :, g]
                    for kt in range(2):
                        last = nc.gpsimd.tensor_copy(dst[:, kt], src[:, kt])
                last.then_inc(v_spread, 1)

            def bias_residual(u):
                h = u.mod(2)
                if is_local(u):
                    hold(pool, xr_loaded[h], 32 * (u.div(2) + 1))
                else:
                    hold(pool, xr_loaded[h], 32 * LU // 2 + 48 * (batch(u).div(2) + 1))
                nc.gpsimd.tensor_tensor(xr[:, h], xr[:, h], c["bo"][:, 1 if is_local(u) else 0].unsqueeze(1).to_broadcast([P, 2, D]),
                                        ALU.add).then_inc(xr_ready, 1)

            def deviation(u):
                g = batch(u)
                hold(pool, stats_ready, g.n + 1)
                hold(pool, o1_ready, g.n)
                dev_chain.start(g.n)
                nc.gpsimd.tensor_scalar(veps[:, 0], mv[:, :, 1], EPS, None, ALU.add)
                dev_chain.link(pool, nc.gpsimd.tensor_scalar(veps[:, 1], mv[:, :, 1], 1.0 + EPS, EPS * EPS, ALU.mult, ALU.add))
                nc.gpsimd.tensor_tensor(rstd[:].rearrange("p a t -> p (a t)"), veps[:].rearrange("p a t -> p (a t)"),
                                        c["powm"][:, 0:4], ALU.pow).then_inc(rstd_ready, 1)
                hold(pool, rstd_ready, g.n + 1)
                dev_chain.link(pool, nc.gpsimd.tensor_tensor(scale2[:], rstd[:, 0], rstd[:, 1], ALU.mult))
                nc.gpsimd.tensor_tensor(scale2[:], scale2[:], veps[:, 0], ALU.mult).then_inc(rstd2_ready, 1)
                dev_chain.end()

            def queue_places(u):
                g = batch(u)
                hold(pool, counts_copied, g.n + 1)
                b = c["base"]
                place_chain.start(g.n)
                place_chain.link(pool, nc.gpsimd.tensor_tensor(b[:, 1], b[:, 0], count[:, 1, 0], ALU.add))
                place_chain.link(pool, nc.gpsimd.tensor_tensor(loc[:], count[:, 0], b[:], ALU.add))
                nc.gpsimd.tensor_tensor(locslot[:, 0], loc[:], mask[:], ALU.mult)
                place_chain.link(pool, nc.gpsimd.tensor_tensor(b[:, 0], b[:, 1], count[:, 1, 1], ALU.add))
                place_chain.link(pool, nc.gpsimd.tensor_tensor(loc[:], loc[:], c["slot0"][:], ALU.add))
                place_chain.end()
                nc.gpsimd.tensor_tensor(locslot[:, 1], loc[:], mask[:], ALU.mult).then_inc(places_ready, 1)

            def scatter(u):
                g, h = batch(u), u.mod(2)
                if isinstance(g.n, int) and g.n == 0:
                    pool.wait_ge(routed_cleared, 16 * 8)
                hold(pool, slot_ready, g.n + 1)
                hold(pool, gate_ready, g.n + 1)
                hold(pool, row_numbered, g.n + 1)
                for t in range(2):
                    pool.indirect_dma_start(out=routed, out_offset=bass.IndirectOffsetOnAxis(ap=slot[:, t:t + 1], axis=0),
                                            in_=row[:, h, t, :], in_offset=None, bounds_check=T - 1,
                                            oob_is_err=False).then_inc(scattered[h], 16)

            def unit(u):
                after1, before2, before3 = u.plus(1), u.plus(-2), u.plus(-3)
                if isinstance(u.n, int) and u.n == 0:
                    split_max(u, 0)
                    spread_v(u)
                if there(u):
                    split_max(u, 1)
                if routes(before2):
                    deviation(before2)
                if there(u):
                    bias_residual(u)
                if there(after1):
                    split_max(after1, 0)
                if routes(before3):
                    queue_places(before3)
                if there(after1):
                    spread_v(after1)
                if routes(before3):
                    scatter(before3)
            run(pool, unit)
            for h in range(2):
                hold(pool, scattered[h], 32 * (B // 2))


def experts(nc, c, w1, b1, w2, b2, routed, out):
    routed_t = routed.rearrange("(n p) r -> n p r", p=P)
    out_rows = out.rearrange("b s d -> (b s) d")
    ctx = ExitStack()
    with ctx:
        def sb(name, shape, dt=F32):
            return ctx.enter_context(nc.sbuf_tensor(name, shape, dt))

        def sem(name):
            return ctx.enter_context(nc.semaphore(name))

        w1_sb = sb("w1_sb", [P, 2, F])
        w2_sb = sb("w2_sb", [P, 2, FT, D])
        b1_sb = sb("b1_sb", [P, 2, FT])
        b2_sb = sb("b2_sb", [P, 2, D])
        rows_sb = sb("rows_sb", [P, 4, CT, ROW])
        xT = sb("xT", [P, 2, CH])
        hT = sb("hT", [P, 2, FT, CH])
        t1 = sb("t1", [P, 2, CT, D])
        z = sb("z", [P, 2, CT, D])
        stats = sb("e_stats", [P, CT, 6])
        mv = sb("e_mv", [P, 2, CT, 2])
        veps = sb("e_veps", [P, 2, CT])
        rstd = sb("e_rstd", [P, 2, CT])
        res = sb("res", [P, 4, CT, D])
        dest = sb("dest", [P, 4, CT], U32)
        ps_x = ctx.enter_context(nc.psum_tensor("e_ps_x", [P, CH], F32))
        ps_h = ctx.enter_context(nc.psum_tensor("e_ps_h", [P, FT, CH], F32))
        ps_y = ctx.enter_context(nc.psum_tensor("e_ps_y", [P, 2, CH], F32))

        w_loaded = [sem("w_loaded0"), sem("w_loaded1")]
        rows_loaded = [sem(f"rows_loaded{h}") for h in range(4)]
        rows_turned = sem("rows_turned")
        xT_ready = sem("e_xT_ready")
        hidden = sem("hidden")
        hT_ready = sem("hT_ready")
        y_ready = sem("e_y_ready")
        y_read = sem("e_y_read")
        post_chain = Chain(sem("post_chain"), 2)
        z_stats = sem("z_stats")
        ln_chain = Chain(sem("e_ln_chain"), 1)
        rstd_ready = sem("e_rstd_ready")
        res_ready = sem("res_ready")
        scattered = [sem(f"e_scattered{h}") for h in range(4)]
        block = ctx.enter_context(nc.Block())

        def steps(eng, before, step, after):
            before()

            def body(i, first, last):
                for h in range(4):
                    step(4 * i + h, i, h, last)
            stepped(eng, NCH // 4, body)
            after()

        @block.sync
        def _(sp):
            def load_w(e, ie, he):
                wait(sp, y_read, 2 * e - 2)
                sp.dma_start(w1_sb[:, he], rows(w1, e, 1).rearrange("o k f -> (o k) f")).then_inc(w_loaded[he], 16)
                sp.dma_start(w2_sb[:, he], rows(w2, e, 1).rearrange("o (g p) d -> p (o g) d", p=P)).then_inc(w_loaded[he], 16)
                sp.dma_start(b1_sb[:, he], rows(b1, e, 1).rearrange("o p g -> (o p) g")).then_inc(w_loaded[he], 16)
                sp.dma_start(b2_sb[:, he], rows(b2, e, 1).to_broadcast([P, D])).then_inc(w_loaded[he], 16)

            def load_rows(k, h):
                wait(sp, z_stats, k - 3)
                sp.dma_start(rows_sb[:, h], rows(routed_t, CT * k, CT).rearrange("t p r -> p t r")).then_inc(rows_loaded[h], 16)

            def before():
                load_rows(0, 0)
                load_w(0, 0, 0)
                load_rows(1, 1)
                load_rows(2, 2)

            def step(k, i, h, last):
                if h % 2 == 0 and not (last and h == 2):
                    load_w(2 * i + h // 2 + 1, i + (h // 2 + 1) // 2, (h // 2 + 1) % 2)
                if not (last and h > 0):
                    load_rows(k + 3, (h + 3) % 4)

            def after():
                pass
            steps(sp, before, step, after)

        @block.tensor
        def _(pe):
            def turn(k, ih, h):
                pe.wait_ge(rows_loaded[h], 16 * (ih + 1))
                wait(pe, xT_ready, k)
                for t in range(CT):
                    last = nc.tensor.transpose(ps_x[:, t * P:(t + 1) * P], rows_sb[:, h, t, 0:D], c["ident"][:])
                last.then_inc(rows_turned, 1)

            def up(k, ie, he):
                pe.wait_ge(xT_ready, k + 1)
                pe.wait_ge(w_loaded[he], 64 * (ie + 1))
                for f in range(FT):
                    wait(pe, hT_ready, FT * (k - 1) + f + 1)
                    nc.tensor.matmul(ps_h[:, f], w1_sb[:, he, f * P:(f + 1) * P], xT[:, h_of(k)],
                                     start=True, stop=True).then_inc(hidden, 1)

            def down(k, he, hk):
                pe.wait_ge(hT_ready, FT * (k + 1))
                wait(pe, y_read, k - 1)
                for t in range(CT):
                    for f in range(FT):
                        last = nc.tensor.matmul(ps_y[:, hk, t * D:(t + 1) * D], hT[:, hk, f, t * P:(t + 1) * P],
                                                w2_sb[:, he, f], start=(f == 0), stop=(f == FT - 1))
                last.then_inc(y_ready, 1)

            parity = [0]

            def h_of(k):
                return parity[0]

            def before():
                turn(0, 0, 0)
                turn(1, 0, 1)
                parity[0] = 0
                up(0, 0, 0)

            def step(k, i, h, last):
                if not (last and h == 3):
                    parity[0] = (h + 1) % 2
                    up(k + 1, i + (h + 1) // 4, ((h + 1) // 2) % 2)
                if not (last and h >= 2):
                    turn(k + 2, i + (h + 2) // 4, (h + 2) % 4)
                down(k, (h // 2) % 2, h % 2)

            def after():
                pass
            steps(pe, before, step, after)

        @block.scalar
        def _(act):
            def copy_x(k, hk):
                act.wait_ge(rows_turned, k + 1)
                wait(act, hidden, FT * (k - 1))
                nc.scalar.copy(xT[:, hk], ps_x[:]).then_inc(xT_ready, 1)

            def relu(k, he, hk):
                wait(act, y_ready, k - 1)
                for f in range(FT):
                    act.wait_ge(hidden, FT * k + f + 1)
                    nc.scalar.activation(hT[:, hk, f], ps_h[:, f], ACT.Relu, bias=b1_sb[:, he, f:f + 1]).then_inc(hT_ready, 1)

            def before():
                copy_x(0, 0)
                copy_x(1, 1)
                relu(0, 0, 0)

            def step(k, i, h, last):
                if not (last and h == 3):
                    relu(k + 1, ((h + 1) // 2) % 2, (h + 1) % 2)
                if not (last and h >= 2):
                    copy_x(k + 2, h % 2)

            def after():
                pass
            steps(act, before, step, after)

        @block.vector
        def _(dve):
            def before():
                pass

            def step(k, i, h, last):
                he, hk = (h // 2) % 2, h % 2
                post_chain.start(k)
                dve.wait_ge(y_ready, k + 1)
                nc.vector.tensor_tensor(t1[:, hk], ps_y[:, hk].rearrange("p (t d) -> p t d", t=CT),
                                        b2_sb[:, he].unsqueeze(1).to_broadcast([P, CT, D]), ALU.add).then_inc(y_read, 1)
                dve.wait_ge(y_read, k + 1)
                for t in range(CT):
                    ins = nc.vector.scalar_tensor_tensor(out=z[:, hk, t], in0=t1[:, hk, t],
                                                         scalar=rows_sb[:, h, t, D:D + 1],
                                                         in1=rows_sb[:, h, t, 0:D], op0=ALU.mult, op1=ALU.add)
                post_chain.link(dve, ins)
                for t in range(CT):
                    ins = nc.vector.bn_stats(stats[:, t], z[:, hk, t])
                post_chain.link(dve, ins)
                post_chain.end()
                wait(dve, scattered[h], 16 * CT * i)
                nc.vector.tensor_copy(dest[:, h], rows_sb[:, h, :, D + 1])
                for t in range(CT):
                    ins = nc.vector.bn_aggr(mv[:, hk, t], stats[:, t])
                ins.then_inc(z_stats, 1)

            def normalize(k, h):
                hk = h % 2
                dve.wait_ge(rstd_ready, k + 1)
                for t in range(CT):
                    ins = nc.vector.tensor_scalar(res[:, h, t], z[:, hk, t], mv[:, hk, t, 0:1], rstd[:, hk, t:t + 1],
                                                  ALU.subtract, ALU.mult)
                ins.then_inc(res_ready, 1)

            def step_then_last(k, i, h, last):
                step(k, i, h, last)
                if not (isinstance(k, int) and k == 0):
                    normalize(k - 1, (h + 3) % 4)

            def after():
                normalize(NCH - 1, 3)
            steps(dve, before, step_then_last, after)

        @block.gpsimd
        def _(pool):
            def before():
                pass

            def step(k, i, h, last):
                hk = h % 2
                hold(pool, z_stats, k + 1)
                ln_chain.start(k)
                ln_chain.link(pool, nc.gpsimd.tensor_scalar(veps[:, hk], mv[:, hk, :, 1], EPS, None, ALU.add))
                ln_chain.end()
                nc.gpsimd.tensor_tensor(rstd[:, hk], veps[:, hk], c["powm"][:, 0:CT], ALU.pow).then_inc(rstd_ready, 1)
                if not (isinstance(k, int) and k == 0):
                    scatter(k - 1, (h + 3) % 4)

            def scatter(k, h):
                hold(pool, res_ready, k + 1)
                for t in range(CT):
                    pool.indirect_dma_start(out=out_rows, out_offset=bass.IndirectOffsetOnAxis(ap=dest[:, h, t:t + 1], axis=0),
                                            in_=res[:, h, t], in_offset=None, bounds_check=T - 1,
                                            oob_is_err=False).then_inc(scattered[h], 16)

            def after():
                scatter(NCH - 1, 3)
                for h in range(4):
                    hold(pool, scattered[h], 16 * CT * NCH // 4)
            steps(pool, before, step, after)


def kernel(**inputs):
    import numpy as np
    import concourse.bacc as bacc
    from concourse.bass_utils import run_bass_kernel_spmd

    a = {k.removeprefix("L0_attn_").removeprefix("L0_ffn_"): np.asarray(v) for k, v in inputs.items()}
    f32 = np.float32

    def both(g, l, axis=1):
        return np.ascontiguousarray(np.stack([g, l], axis=axis))

    def head_order(w):
        return w.reshape(2, 2, 4, DH, D).transpose(0, 2, 1, 3, 4).reshape(D, D)

    def spread(v):
        return np.ascontiguousarray(np.broadcast_to(v, (P,) + v.shape))

    blk = np.arange(S) // LW
    same = blk[None, :] == np.arange(NBLK)[:, None]
    arrays = {
        "x": a["x"],
        "wqkv": both(a["wg_in"].T, a["wl_in"].T),
        "bqk": both(a["bg_in"][:2 * D].reshape(2, D).T, a["bl_in"][:2 * D].reshape(2, D).T),
        "bv_row": spread(np.stack([a["bg_in"][2 * D:], a["bl_in"][2 * D:]])),
        "ln_cols": np.stack([a["ln_g_g"], a["ln_g_b"], a["ln_l_g"], a["ln_l_b"]], axis=1),
        "wo": both(head_order(a["wg_out"].T), head_order(a["wl_out"].T)),
        "bo_row": spread(np.stack([a["bg_out"], a["bl_out"]])),
        "wg": a["Wg"],
        "w1": a["W1"],
        "b1": a["b1"].reshape(E, FT, P).transpose(0, 2, 1),
        "w2": a["W2"],
        "b2": a["b2"],
        "eye_in": np.eye(P, dtype=f32),
        "tri_in": np.triu(np.ones((P, P), f32)),
        "blockq_in": same.astype(f32),
        "blockk_in": np.where(same, f32(0), f32(-2.0 ** 100)),
        "tokid_in": (np.arange(P)[:, None] + P * np.arange(2)[None, :]).astype(f32),
        "slot_in": spread(np.broadcast_to(CAP * np.arange(E) - 1, (2, E)).astype(f32)),
        "prio_in": spread(np.broadcast_to(E - np.arange(E), (2, E)).astype(f32)),
    }
    arrays = {k: np.ascontiguousarray(v) for k, v in arrays.items()}
    nc = bacc.Bacc("TRN2", target_bir_lowering=False, num_devices=1)
    aps = {k: nc.dram_tensor(k, v.shape, mybir.dt.from_np(v.dtype), kind="ExternalInput").ap() for k, v in arrays.items()}
    out = nc.dram_tensor("out", (B, S, D), F32, kind="ExternalOutput").ap()
    build(nc, out=out, **aps)
    result = run_bass_kernel_spmd(nc, [arrays], core_ids=[0])
    return result.results[0]["out"]
```
